# Optimizing a Trainium2 kernel written in Bass

```python
import numpy as np
import jax
import jax.numpy as jnp

def _softmax(x, axis=-1):
    return jax.nn.softmax(x, axis=axis)

def _gelu(x):
    return jax.nn.gelu(x, approximate=True)

def _silu(x):
    return jax.nn.silu(x)

def _sigmoid(x):
    return jax.nn.sigmoid(x)

def _layernorm(x, axis=-1, eps=1e-05):
    m = jnp.mean(x, axis=axis, keepdims=True)
    v = jnp.var(x, axis=axis, keepdims=True)
    return (x - m) / jnp.sqrt(v + eps)

def _scatter_add(tgt, idx, src, axis=0):
    return tgt.at[idx].add(src)

def _segment_sum(src, seg, n):
    return jax.ops.segment_sum(src, seg, n)
kernel_name = 'mk_perceiver_d1_seqx_r4_945497'

def setup_inputs(seed: int=0):
    np.random.seed(seed)
    _w = jnp.asarray

    def _rec_inputs():
        import jax
        import jax.numpy as jnp
        _rk = jax.random.key(seed)
        x = 7.22e-05 + 1 * jax.random.normal(jax.random.fold_in(_rk, 1), (2, 256, 256), jnp.float32)
        _lenS = 256 - jax.random.randint(jax.random.fold_in(_rk, 7), (2,), 0, max(1, 256 // 4) + 1, jnp.int32)
        _lenS2 = 4096 - jax.random.randint(jax.random.fold_in(_rk, 8), (2,), 0, max(1, 4096 // 4) + 1, jnp.int32)
        _ctx_1024P = jax.random.normal(jax.random.fold_in(_rk, 11), (2, 16, 256), jnp.float32)
        _ctx_1024c = jax.random.dirichlet(jax.random.fold_in(_rk, 511), 0.3 * jnp.ones((16,), jnp.float32), (2, 4096))
        _ctx_1024t = jnp.einsum('bsk,bkd->bsd', _ctx_1024c, _ctx_1024P)
        _ctx_1024t = _ctx_1024t * jax.lax.rsqrt(jnp.mean(jnp.square(_ctx_1024t)) + 1e-12) * 0.953939
        ctx_1024 = 4.13588e-05 + 0.999923 * (_ctx_1024t + 0.3 * jax.random.normal(jax.random.fold_in(_rk, 611), (2, 4096, 256), jnp.float32))
        _validS = jnp.arange(256)[None, :] < _lenS[:, None]
        _validS2 = jnp.arange(4096)[None, :] < _lenS2[:, None]
        _causal = jnp.tril(jnp.ones((256, 256), dtype=bool))
        mask_1x1xSxS2_bk1 = jnp.broadcast_to(_validS2[0:1, None, None, :], (1, 1, 256, 4096))
        return (x, ctx_1024, mask_1x1xSxS2_bk1)
    x, ctx_1024, mask_1x1xSxS2_bk1 = _rec_inputs()

    def _L0_xattn_setup():
        import jax, jax.numpy as jnp
        import numpy as np
        D_MODEL = 256
        N_HEADS = 16
        D_K = D_MODEL // N_HEADS
        BATCH = 4
        SEQ = 512

        def _split_heads(x):
            b, s, _ = x.shape
            return x.reshape(b, s, N_HEADS, D_K).transpose(0, 2, 1, 3)
        key = jax.random.key(seed)
        ks = jax.random.split(key, 12)
        s = 1.0 / np.sqrt(D_MODEL)
        inp = {'query': jax.random.normal(ks[0], (BATCH, SEQ, D_MODEL), jnp.float32), 'key': jax.random.normal(ks[1], (BATCH, SEQ, D_MODEL), jnp.float32), 'value': jax.random.normal(ks[2], (BATCH, SEQ, D_MODEL), jnp.float32), 'mask': jnp.triu(jnp.ones((SEQ, SEQ), bool), k=1)[None, None, :, :], 'w_q': jax.random.normal(ks[3], (D_MODEL, D_MODEL), jnp.float32) * s, 'b_q': jax.random.normal(ks[4], (D_MODEL,), jnp.float32) * s, 'w_k': jax.random.normal(ks[5], (D_MODEL, D_MODEL), jnp.float32) * s, 'b_k': jax.random.normal(ks[6], (D_MODEL,), jnp.float32) * s, 'w_v': jax.random.normal(ks[7], (D_MODEL, D_MODEL), jnp.float32) * s, 'b_v': jax.random.normal(ks[8], (D_MODEL,), jnp.float32) * s, 'w_o': jax.random.normal(ks[9], (D_MODEL, D_MODEL), jnp.float32) * s, 'b_o': jax.random.normal(ks[10], (D_MODEL,), jnp.float32) * s}
        return inp
    _L0_xattn_all = _L0_xattn_setup()
    _L0_xattn_in = {k: v for k, v in _L0_xattn_all.items() if k in ('w_q', 'b_q', 'w_k', 'b_k', 'w_v', 'b_v', 'w_o', 'b_o')}
    del _L0_xattn_all

    def _L0_attn_setup():
        import jax, jax.numpy as jnp
        import numpy as np
        D_MODEL = 256
        NUM_HEADS = 4
        EXPAND_K = 1.0
        EXPAND_V = 2.0
        KEY_DIM = int(D_MODEL * EXPAND_K)
        VALUE_DIM = int(D_MODEL * EXPAND_V)
        HEAD_K = KEY_DIM // NUM_HEADS
        HEAD_V = VALUE_DIM // NUM_HEADS
        CHUNK = 64
        EPS = 1e-05
        ROPE_BASE = 10000.0

        def _apply_rotary(q, k):
            d = q.shape[-1]
            half = d // 2
            inv_freq = 1.0 / ROPE_BASE ** (jnp.arange(0, d, 2, dtype=jnp.float32) / d)
            t = jnp.arange(q.shape[1], dtype=jnp.float32)
            freqs = t[:, None] * inv_freq[None, :]
            cos = jnp.cos(freqs)[None, :, None, :]
            sin = jnp.sin(freqs)[None, :, None, :]

            def rot(x):
                x1, x2 = (x[..., :half], x[..., half:])
                return jnp.concatenate([x1 * cos - x2 * sin, x2 * cos + x1 * sin], axis=-1)
            return (rot(q), rot(k))

        def _chunk_retention(q, k, v, gamma):
            B, T, H, dk = q.shape
            dv = v.shape[-1]
            C = CHUNK
            N = T // C
            qc = q.reshape(B, N, C, H, dk).transpose(1, 0, 3, 2, 4)
            kc = k.reshape(B, N, C, H, dk).transpose(1, 0, 3, 2, 4)
            vc = v.reshape(B, N, C, H, dv).transpose(1, 0, 3, 2, 4)
            i = jnp.arange(C, dtype=jnp.float32)
            cross_dec = gamma[:, None] ** (i + 1.0)
            k_dec = gamma[:, None] ** (C - 1.0 - i)
            diff = i[:, None] - i[None, :]
            mask = jnp.where(diff >= 0, gamma[:, None, None] ** diff, 0.0)
            gC = gamma ** C

            def step(S, inp):
                qb, kb, vb = inp
                attn = jnp.einsum('bhid,bhjd->bhij', qb, kb) * mask
                o_intra = jnp.einsum('bhij,bhjv->bhiv', attn, vb)
                o_inter = jnp.einsum('bhid,bhdv->bhiv', qb * cross_dec[:, :, None], S)
                S_new = gC[:, None, None] * S + jnp.einsum('bhjd,bhjv->bhdv', kb * k_dec[:, :, None], vb)
                return (S_new, o_intra + o_inter)
            S0 = jnp.zeros((B, H, dk, dv), dtype=q.dtype)
            _, o = jax.lax.scan(step, S0, (qc, kc, vc))
            return o.transpose(1, 0, 3, 2, 4).reshape(B, T, H, dv)
        key = jax.random.key(seed)
        ks = jax.random.split(key, 7)
        B, T = (4, 512)
        s = 0.02
        return {'x': jax.random.normal(ks[0], (B, T, D_MODEL), dtype=jnp.float32), 'Wq': jax.random.normal(ks[1], (KEY_DIM, D_MODEL), dtype=jnp.float32) * s, 'Wk': jax.random.normal(ks[2], (KEY_DIM, D_MODEL), dtype=jnp.float32) * s, 'Wv': jax.random.normal(ks[3], (VALUE_DIM, D_MODEL), dtype=jnp.float32) * s, 'Wg': jax.random.normal(ks[4], (VALUE_DIM, D_MODEL), dtype=jnp.float32) * s, 'Wo': jax.random.normal(ks[5], (D_MODEL, VALUE_DIM), dtype=jnp.float32) * s, 'gnorm_w': jnp.ones((HEAD_V,), dtype=jnp.float32)}
    _L0_attn_all = _L0_attn_setup()
    _L0_attn_in = {k: v for k, v in _L0_attn_all.items() if k in ('Wq', 'Wk', 'Wv', 'Wg', 'Wo', 'gnorm_w')}
    del _L0_attn_all

    def _L0_ffn_setup():
        import jax, jax.numpy as jnp
        import numpy as np
        THRESHOLD = 0.1
        key = jax.random.key(seed)
        k1, k2, k3 = jax.random.split(key, 3)
        B, S, D, E = (4, 1024, 256, 8)
        inputs = jax.random.normal(k1, (B, S, D), dtype=jnp.float32)
        gate_w = jax.random.normal(k2, (D, E), dtype=jnp.float32) * 0.02
        gate_b = jnp.zeros((E,), dtype=jnp.float32)
        expert_w = jax.random.normal(k3, (E, D, D), dtype=jnp.float32) * 0.02
        expert_b = jnp.zeros((E, D), dtype=jnp.float32)
        return {'inputs': inputs, 'gate_w': gate_w, 'gate_b': gate_b, 'expert_w': expert_w, 'expert_b': expert_b}
    _L0_ffn_all = _L0_ffn_setup()
    _L0_ffn_in = {k: v for k, v in _L0_ffn_all.items() if k in ('gate_w', 'gate_b', 'expert_w', 'expert_b')}
    del _L0_ffn_all
    return {'x': x, 'ctx_1024': ctx_1024, 'mask_1x1xSxS2_bk1': mask_1x1xSxS2_bk1, 'L0_xattn_w_q': _L0_xattn_in['w_q'], 'L0_xattn_b_q': _L0_xattn_in['b_q'], 'L0_xattn_w_k': _L0_xattn_in['w_k'], 'L0_xattn_b_k': _L0_xattn_in['b_k'], 'L0_xattn_w_v': _L0_xattn_in['w_v'], 'L0_xattn_b_v': _L0_xattn_in['b_v'], 'L0_xattn_w_o': _L0_xattn_in['w_o'], 'L0_xattn_b_o': _L0_xattn_in['b_o'], 'L0_attn_Wq': _L0_attn_in['Wq'], 'L0_attn_Wk': _L0_attn_in['Wk'], 'L0_attn_Wv': _L0_attn_in['Wv'], 'L0_attn_Wg': _L0_attn_in['Wg'], 'L0_attn_Wo': _L0_attn_in['Wo'], 'L0_attn_gnorm_w': _L0_attn_in['gnorm_w'], 'L0_ffn_gate_w': _L0_ffn_in['gate_w'], 'L0_ffn_gate_b': _L0_ffn_in['gate_b'], 'L0_ffn_expert_w': _L0_ffn_in['expert_w'], 'L0_ffn_expert_b': _L0_ffn_in['expert_b']}

def reference(x, ctx_1024, mask_1x1xSxS2_bk1, L0_xattn_w_q, L0_xattn_b_q, L0_xattn_w_k, L0_xattn_b_k, L0_xattn_w_v, L0_xattn_b_v, L0_xattn_w_o, L0_xattn_b_o, L0_attn_Wq, L0_attn_Wk, L0_attn_Wv, L0_attn_Wg, L0_attn_Wo, L0_attn_gnorm_w, L0_ffn_gate_w, L0_ffn_gate_b, L0_ffn_expert_w, L0_ffn_expert_b):
    import jax
    import jax.numpy as jnp

    def _L0_xattn_ref(query, key, value, mask, w_q, b_q, w_k, b_k, w_v, b_v, w_o, b_o):
        import jax, jax.numpy as jnp
        import numpy as np
        D_MODEL = 256
        N_HEADS = 16
        D_K = D_MODEL // N_HEADS
        BATCH = 4
        SEQ = 512

        def _split_heads(x):
            b, s, _ = x.shape
            return x.reshape(b, s, N_HEADS, D_K).transpose(0, 2, 1, 3)
        q = _split_heads(query @ w_q.T + b_q)
        k = _split_heads(key @ w_k.T + b_k)
        v = _split_heads(value @ w_v.T + b_v)
        scale = 1.0 / jnp.sqrt(jnp.asarray(D_K, q.dtype))
        scores = jnp.einsum('bhqd,bhkd->bhqk', q, k) * scale
        scores = jnp.where(mask, jnp.asarray(-jnp.inf, scores.dtype), scores)
        weights = jax.nn.softmax(scores, axis=-1)
        attn = jnp.einsum('bhqk,bhkd->bhqd', weights, v)
        b = attn.shape[0]
        attn = attn.transpose(0, 2, 1, 3).reshape(b, -1, D_MODEL)
        return attn @ w_o.T + b_o

    def _L0_attn_ref(x, Wq, Wk, Wv, Wg, Wo, gnorm_w):
        import jax, jax.numpy as jnp
        import numpy as np
        D_MODEL = 256
        NUM_HEADS = 4
        EXPAND_K = 1.0
        EXPAND_V = 2.0
        KEY_DIM = int(D_MODEL * EXPAND_K)
        VALUE_DIM = int(D_MODEL * EXPAND_V)
        HEAD_K = KEY_DIM // NUM_HEADS
        HEAD_V = VALUE_DIM // NUM_HEADS
        CHUNK = 64
        EPS = 1e-05
        ROPE_BASE = 10000.0

        def _apply_rotary(q, k):
            d = q.shape[-1]
            half = d // 2
            inv_freq = 1.0 / ROPE_BASE ** (jnp.arange(0, d, 2, dtype=jnp.float32) / d)
            t = jnp.arange(q.shape[1], dtype=jnp.float32)
            freqs = t[:, None] * inv_freq[None, :]
            cos = jnp.cos(freqs)[None, :, None, :]
            sin = jnp.sin(freqs)[None, :, None, :]

            def rot(x):
                x1, x2 = (x[..., :half], x[..., half:])
                return jnp.concatenate([x1 * cos - x2 * sin, x2 * cos + x1 * sin], axis=-1)
            return (rot(q), rot(k))

        def _chunk_retention(q, k, v, gamma):
            B, T, H, dk = q.shape
            dv = v.shape[-1]
            C = CHUNK
            N = T // C
            qc = q.reshape(B, N, C, H, dk).transpose(1, 0, 3, 2, 4)
            kc = k.reshape(B, N, C, H, dk).transpose(1, 0, 3, 2, 4)
            vc = v.reshape(B, N, C, H, dv).transpose(1, 0, 3, 2, 4)
            i = jnp.arange(C, dtype=jnp.float32)
            cross_dec = gamma[:, None] ** (i + 1.0)
            k_dec = gamma[:, None] ** (C - 1.0 - i)
            diff = i[:, None] - i[None, :]
            mask = jnp.where(diff >= 0, gamma[:, None, None] ** diff, 0.0)
            gC = gamma ** C

            def step(S, inp):
                qb, kb, vb = inp
                attn = jnp.einsum('bhid,bhjd->bhij', qb, kb) * mask
                o_intra = jnp.einsum('bhij,bhjv->bhiv', attn, vb)
                o_inter = jnp.einsum('bhid,bhdv->bhiv', qb * cross_dec[:, :, None], S)
                S_new = gC[:, None, None] * S + jnp.einsum('bhjd,bhjv->bhdv', kb * k_dec[:, :, None], vb)
                return (S_new, o_intra + o_inter)
            S0 = jnp.zeros((B, H, dk, dv), dtype=q.dtype)
            _, o = jax.lax.scan(step, S0, (qc, kc, vc))
            return o.transpose(1, 0, 3, 2, 4).reshape(B, T, H, dv)
        B, T, _ = x.shape
        H = NUM_HEADS
        q = (x @ Wq.T).reshape(B, T, H, HEAD_K)
        k = (x @ Wk.T).reshape(B, T, H, HEAD_K)
        v = (x @ Wv.T).reshape(B, T, H, HEAD_V)
        g = (x @ Wg.T).reshape(B, T, H, HEAD_V)
        q, k = _apply_rotary(q, k)
        q = q * HEAD_K ** (-0.5)
        gamma = 1.0 - jnp.exp2(-5.0 - jnp.arange(H, dtype=jnp.float32))
        o = _chunk_retention(q, k, v, gamma)
        var = jnp.mean(o * o, axis=-1, keepdims=True)
        o = o * jax.lax.rsqrt(var + EPS) * gnorm_w
        o = o * (g * jax.nn.sigmoid(g))
        return o.reshape(B, T, H * HEAD_V) @ Wo.T

    def _L0_ffn_ref(inputs, gate_w, gate_b, expert_w, expert_b):
        import jax, jax.numpy as jnp
        import numpy as np
        THRESHOLD = 0.1
        d = inputs.shape[-1]
        x = inputs.reshape(-1, d)
        gate_logits = jax.nn.softmax(x @ gate_w + gate_b, axis=-1)
        selected = (gate_logits >= THRESHOLD).astype(x.dtype)
        weights = gate_logits * selected
        wsum = jnp.sum(weights, axis=-1, keepdims=True)
        weights = weights / jnp.where(wsum == 0, jnp.ones_like(wsum), wsum)
        E = expert_w.shape[0]
        out = jnp.zeros((x.shape[0], expert_w.shape[-1]), dtype=x.dtype)
        for e in range(E):
            out = out + weights[:, e:e + 1] * (x @ expert_w[e] + expert_b[e])
        return out.reshape(*inputs.shape[:-1], out.shape[-1])
    x = x + _L0_xattn_ref(_layernorm(x, axis=-1), ctx_1024, ctx_1024, mask_1x1xSxS2_bk1, L0_xattn_w_q, L0_xattn_b_q, L0_xattn_w_k, L0_xattn_b_k, L0_xattn_w_v, L0_xattn_b_v, L0_xattn_w_o, L0_xattn_b_o)
    x = x + _L0_attn_ref(_layernorm(x, axis=-1), L0_attn_Wq, L0_attn_Wk, L0_attn_Wv, L0_attn_Wg, L0_attn_Wo, L0_attn_gnorm_w)
    x = x + _L0_ffn_ref(_layernorm(x, axis=-1), L0_ffn_gate_w, L0_ffn_gate_b, L0_ffn_expert_w, L0_ffn_expert_b)
    return x

_drawn_inputs = setup_inputs


def setup_inputs(seed=0):
    import zlib

    import numpy as np

    out = dict(_drawn_inputs(seed))
    spreads = {'L0_attn_gnorm_w': (1.0, 0.6), 'L0_ffn_gate_b': (0.0, 0.1), 'L0_ffn_expert_b': (0.0, 0.1)}
    factors = {'L0_xattn_b_q': 4.309, 'L0_xattn_b_k': 8.0}
    for name, (base, spread) in spreads.items():
        noise = np.random.default_rng([zlib.crc32(name.encode()), seed]).standard_normal(out[name].shape)
        drawn = base * np.exp(spread * noise) if base else spread * noise
        out[name] = jnp.asarray(drawn.astype(out[name].dtype))
    for name, factor in factors.items():
        out[name] = (out[name] * factor).astype(out[name].dtype)
    return out
```

```python
from contextlib import ExitStack

import numpy as np
import concourse.bass as bass
from concourse import mybir

F32 = mybir.dt.float32
BF16 = mybir.dt.bfloat16
I32 = mybir.dt.int32
U8 = mybir.dt.uint8
U16 = mybir.dt.uint16
ALU = mybir.AluOpType
ACT = mybir.ActivationFunctionType
AXX = mybir.AxisListType.X

P = 128
NB = 2
NQ = 256
D = 256
NKEY = 4096
NH, DK = 16, 16
QT = NQ // P
TT = NB * QT
KIN = D // P
CH = 512
NCH = NKEY // CH
KT = CH // P
G = 4
NG = NH // G
STAGES = NB * NG
PADV = 32
K_PART = (0, 0, 0, 1, 1, 2)
Q_PART = (0, 1, 2, 0, 1, 0)
NPROD = len(K_PART)
MROW = NPROD * DK
KROWS = MROW + 3
HIDDEN = -1e30
MAX_FLOOR = -1e20

RH, RDK, RDV = 4, 64, 128
NV = RH * RDV
NE = 8
EPS = 1e-5
RSQRT_MAGIC = float(0x5F3759DF)
NEWTON = 3

STEPS = STAGES + 3
A_PER = STAGES * NG * QT
U_PER = STAGES * KT
X_USES = [(t, k) for t in range(STEPS) for k in (1, 2)
          if (k == 1 and 1 <= t <= STAGES) or (k == 2 and 3 <= t)]
X_PER = len(X_USES)
X_INDEX = {use: n for n, use in enumerate(X_USES)}
SPLIT_OPS = 3
MAX_OPS = 6
COMBINE_OPS = 2
DVE_PER = NB * SPLIT_OPS + STAGES * (MAX_OPS + COMBINE_OPS)
CREDIT = 3


def build(nc, a):
    with ExitStack() as ctx:
        def sb(name, shape, dt=F32):
            return ctx.enter_context(nc.sbuf_tensor(name, shape, dt))

        def sem(name):
            return ctx.enter_context(nc.semaphore(name))

        ident = sb("ident", [P, P])
        identb = sb("identb", [P, P], BF16)
        ones = sb("ones", [P, 1])
        x_in = sb("x_in", [P, TT, D])
        xbo = sb("xbo", [P, TT, D])
        xn = sb("xn", [P, TT, D])
        xnT = sb("xnT", [P, KIN, TT * P])
        wq = sb("wq", [P, KIN, D])
        wk = sb("wk", [P, KIN, D])
        wv = sb("wv", [P, KIN, D])
        wo = sb("wo", [P, KIN, D])
        bq = sb("bq", [P, KIN])
        bq4 = sb("bq4", [P, KIN])
        bk = sb("bk", [P, KIN])
        bv_row = sb("bv_row", [P, D])
        bo_row = sb("bo_row", [P, D])
        w_ret = sb("w_ret", [P, KIN, 2 * D + 2 * NV])
        w_reto = sb("w_reto", [P, NV // P, D])
        gn_row = sb("gn_row", [P, RDV])
        rope = sb("rope", [P, 2, QT, RDK // 2])
        decay = sb("decay", [P, RH, 3 * P])
        w_gate = sb("w_gate", [P, KIN, NE])
        gb_row = sb("gb_row", [P, NE])
        w_exp = sb("w_exp", [P, KIN, NE, D])
        b_exp = sb("b_exp", [NE, D])
        index = sb("index", [1, NCH])

        mask_all = sb("mask_all", [P, QT, NKEY], U8)
        mask_room = mask_all[:, :, :].rearrange("p t k -> p (t k)").bitcast(F32)
        x1 = mask_room[:, 0:TT * D].rearrange("p (t c) -> p t c", t=TT)
        x2 = mask_room[:, TT * D:2 * TT * D].rearrange("p (t c) -> p t c", t=TT)
        hid_min = sb("hid_min", [P, QT, NCH])
        seen = sb("seen", [P, QT, NCH])
        tiny = sb("tiny", [1, 8, 2 * NCH])
        rank_eq = sb("rank_eq", [1, NCH, NCH])
        chunk_list = sb("chunk_list", [1, NCH + 1], I32)
        n_active = sb("n_active", [1, 1], I32)

        ctxT = sb("ctxT", [P, NB, KIN, CH])
        mask_q = sb("mask_q", [P, QT, CH], U8)
        mask_k = sb("mask_k", [P, KT, NQ], U8)
        hide_q = sb("hide_q", [P, QT, CH], BF16)
        hide_k = sb("hide_k", [P, KT, NQ], BF16)
        k32 = sb("k32", [P, NB, KIN, CH])
        k_rest = sb("k_rest", [P, KIN, CH])
        kpart = sb("kpart", [P, NB, 3, KIN, CH], BF16)
        kstack = sb("kstack", [P, NB, NH, CH], BF16)
        qpart = sb("qpart", [P, 3, KIN, TT * P], BF16)
        qstack = sb("qstack", [P, NB, NH, NQ], BF16)
        vals = sb("vals", [P, NB, KT, NH, PADV])
        prob = sb("prob", [P, 3, G * NQ])
        junk = sb("junk", [P, 2, CH], BF16)
        outT = sb("outT", [P, 2, NQ])
        cmax = sb("cmax", [P, 2, QT * G])
        mnew = sb("mnew", [P, QT * G])
        mrun = sb("mrun", [P, STAGES, QT * G])
        mdiff = sb("mdiff", [P, 2, QT * G])
        alpha = sb("alpha", [P, 4, QT * G])
        mrest = sb("mrest", [P, QT, G])
        mpart = sb("mpart", [P, 2, QT, 3, G], BF16)
        mrows = sb("mrows", [3 * G, 2, NQ], BF16)
        acc = sb("acc", [P, STAGES, QT * G, DK + 1])
        rsum = sb("rsum", [P, STAGES, QT * G])
        stats = sb("stats", [P, TT, 6])
        moments = sb("moments", [P, TT, 2])
        glog = sb("glog", [P, TT, NE])
        gexp = sb("gexp", [P, TT, NE])
        nwts = sb("nwts", [P, TT, NE])
        gmax = sb("gmax", [P, TT])
        gsum = sb("gsum", [P, TT])
        gw1 = sb("gw1", [P, 4])
        wT = sb("wT", [NE, 2, P])
        nw = sb("nw", [P, 4, 4])
        prob_flat = prob[:, :, :].rearrange("p a b -> p (a b)")
        q32 = prob_flat[:, 0:KIN * TT * P].rearrange("p (f t) -> p f t", f=KIN)
        q_rest = prob_flat[:, KIN * TT * P:2 * KIN * TT * P].rearrange("p (f t) -> p f t", f=KIN)

        late0 = kstack[:, 0, :, :].rearrange("p h k -> p (h k)").bitcast(F32)
        late1 = kstack[:, 1, :, :].rearrange("p h k -> p (h k)").bitcast(F32)
        late2 = k32[:, :, :, :].rearrange("p b f k -> p (b f k)")
        late3 = kpart[:, :, :, :, :].rearrange("p b c f k -> p (b c f k)").bitcast(F32)
        late4 = vals[:, :, :, :, :].rearrange("p b k h e -> p (b k h e)")
        v_tok = late0[:, 0:TT * NV].rearrange("p (t c) -> p t c", t=TT)
        g_tok = late0[:, TT * NV:2 * TT * NV].rearrange("p (t c) -> p t c", t=TT)
        qkT = late1[:, 0:4 * TT * P].rearrange("p (f t) -> p f t", f=4)
        yT = late1[:, 2048:4096].rearrange("p (f t) -> p f t", f=4)
        e_tok = late2[:, 0:2 * NV].rearrange("p (t c) -> p t c", t=2)
        ropes = late3[:, 0:2048].rearrange("p (t c) -> p t c", t=4)
        at_tok = late4[:, 0:TT * D].rearrange("p (t c) -> p t c", t=TT)
        gsq = late4[:, 1024:2048].rearrange("p (t c) -> p t c", t=2)
        y_tok = late4[:, 2048:4096].rearrange("p (t c) -> p t c", t=TT)
        attn = late2[:, 1024:1024 + 2 * 384].rearrange("p (r c) -> p r c", r=2)
        qk_rot = late3[:, 2048:3072].rearrange("p (t c) -> p t c", t=2)
        atT = xnT

        bank = ctx.enter_context(nc.psum_tensor("bank", [P, 8, 512], F32))
        A0, S0, OB, XB = 0, 2, 6, 7
        xbank_b = bank[:, XB, :].bitcast(BF16)

        names = """x_loaded mask_loaded w_loaded late_loaded const_ready ident_ready dve_pre xn_ready
            xnT_ready xnT_evac q_ready q_evac q_cut q_written q_stacked seen_ready seen_summed
            list_ready chunk_loaded kv_ready k_evac v_evac k_cut k_written hide_ready max_ready
            max_read max_cut dve_loop diff_ready alpha_ready x_ready x_read mrows_ready mrows_written mrows_loaded
            score_ready prob_ready prob_used out_read outT_ready
            at_ready atT_ready atT_evac o_ready x1_ready
            n2_ready n2T_ready n2T_evac proj_ready vg_evac e_ready rope_ready qkT_ready qkT_evac
            gate_half gate_rcp gate_done att_ready att_done ret_ready sq_ready y_ready yT_ready yT_evac
            ro_ready x2_ready n3_ready n3T_ready n3T_evac logit_ready neg_max exp_ready w_ready
            wT_ready wT_evac bias_ready pair_ready pair_read out_done dve_post out_written settled""".split()
        s = {n: sem(n) for n in names}
        k_stacked = [sem(f"k_stacked{b}") for b in range(NB)]

        kscr, qscr, mscr = a["kscr"], a["qscr"], a["mscr"]
        block = ctx.enter_context(nc.Block())

        def settle(eng):
            eng.sem_inc(s["settled"], 1)

        @block.sync
        def _(sp):
            for t in range(TT):
                sp.dma_start(x_in[:, t, :], a["x"][t * P:(t + 1) * P, :]).then_inc(s["x_loaded"], 16)
            sp.dma_start(mask_all[:, :, :], a["mask"].rearrange("(t p) k -> p t k", p=P)).then_inc(s["mask_loaded"], 16)
            sp.dma_start(index[:, :], a["index"]).then_inc(s["mask_loaded"], 16)
            sp.dma_start(ident[:, :], a["ident"]).then_inc(s["ident_ready"], 16)
            for w, n in ((wq, "wq"), (wk, "wk"), (wv, "wv"), (wo, "wo")):
                sp.dma_start(w[:, :, :], a[n].rearrange("(c p) n -> p c n", p=P)).then_inc(s["w_loaded"], 16)
            for w, n in ((bq, "bq"), (bk, "bk")):
                sp.dma_start(w[:, :], a[n]).then_inc(s["w_loaded"], 16)
            for w, n in ((bv_row, "bv"), (bo_row, "bo")):
                sp.dma_start(w[:, :], a[n].rearrange("(a n) -> a n", a=1).to_broadcast([P, D])).then_inc(s["w_loaded"], 16)

            sp.wait_ge(s["q_cut"], 1)
            for c in range(3):
                sp.dma_start(qscr[c].rearrange("(f r) t -> r f t", r=P), qpart[:, c, :, :]).then_inc(s["q_written"], 16)
            sp.wait_ge(s["q_written"], 3 * 16)
            for i, c in enumerate(Q_PART):
                for b in range(NB):
                    sp.dma_start(qstack[DK * i:DK * (i + 1), b, :, :],
                                 qscr[c, :, b * NQ:(b + 1) * NQ].rearrange("(h d) q -> d h q", d=DK)
                                 ).then_inc(s["q_stacked"], 16)

            def load_chunk(c):
                for b in range(NB):
                    sp.dma_start(ctxT[:, b, :, :], a["ctxT"][b, :, bass.ds(c * CH, CH)].rearrange("(f p) k -> p f k", p=P)
                                 ).then_inc(s["chunk_loaded"], 16)
                sp.dma_start(mask_q[:, :, :], a["mask"][:, bass.ds(c * CH, CH)].rearrange("(t p) k -> p t k", p=P)
                             ).then_inc(s["chunk_loaded"], 16)
                sp.dma_start(mask_k[:, :, :], a["maskT"][bass.ds(c * CH, CH), :].rearrange("(t p) q -> p t q", p=P)
                             ).then_inc(s["chunk_loaded"], 16)

            sp.wait_ge(s["list_ready"], 2)
            n = sp.value_load(n_active[0:1, 0:1], min_val=1, max_val=NCH)
            load_chunk(sp.value_load(chunk_list[0:1, 0:1], min_val=0, max_val=NCH - 1))
            late = [(w_ret, "w_ret", "(c p) n -> p c n"), (w_reto, "w_reto", "(c p) n -> p c n"),
                    (w_gate, "w_gate", "(c p) n -> p c n")]
            for w, nm, how in late:
                sp.dma_start(w[:, :, :], a[nm].rearrange(how, p=P)).then_inc(s["late_loaded"], 16)
            for c in range(KIN):
                sp.dma_start(w_exp[:, c, :, :], a["w_exp"][:, c * P:(c + 1) * P, :].rearrange("e p n -> p e n")).then_inc(s["late_loaded"], 16)
            sp.dma_start(b_exp[:, :], a["b_exp"]).then_inc(s["late_loaded"], 16)
            sp.dma_start(rope[:, :, :, :], a["rope"]).then_inc(s["late_loaded"], 16)
            sp.dma_start(decay[:, :, :], a["decay"]).then_inc(s["late_loaded"], 16)
            sp.dma_start(gn_row[:, :], a["gn"].rearrange("(a n) -> a n", a=1).to_broadcast([P, RDV])).then_inc(s["late_loaded"], 16)
            sp.dma_start(gb_row[:, :], a["gb"].rearrange("(a n) -> a n", a=1).to_broadcast([P, NE])).then_inc(s["late_loaded"], 16)

            with sp.Fori(0, NCH) as it:
                with sp.If(it < n):
                    for b in range(NB):
                        sp.wait_ge(s["k_cut"], it * NB + b + 1)
                        for c in range(3):
                            sp.dma_start(kscr[b, c].rearrange("(f r) k -> r f k", r=P), kpart[:, b, c, :, :]
                                         ).then_inc(s["k_written"], 16)
                        sp.wait_ge(s["k_written"], (it * NB + b + 1) * 48)
                        for i, c in enumerate(K_PART):
                            sp.dma_start(kstack[DK * i:DK * (i + 1), b, :, :],
                                         kscr[b, c].rearrange("(h d) k -> d h k", d=DK)).then_inc(k_stacked[b], 16)
                    sp.wait_ge(s["kv_ready"], (it + 1) * 4 * NB)
                    settle(sp)
                    sp.wait_ge(s["hide_ready"], (it + 1) * 2)
                    settle(sp)
                    nxt = sp.value_load(chunk_list[0:1, bass.ds(it + 1, 1)], min_val=0, max_val=NCH - 1)
                    sp.wait_ge(s["chunk_loaded"], (it + 1) * 64)
                    load_chunk(nxt)
                    for st in range(STAGES):
                        b, g = divmod(st, NG)
                        sp.wait_ge(s["mrows_ready"], it * STAGES + st + 1)
                        sp.dma_start(mscr[st], mrows[:, st % 2, :]).then_inc(s["mrows_written"], 16)
                        sp.wait_ge(s["mrows_written"], (it * STAGES + st + 1) * 16)
                        sp.dma_start(qstack[MROW:KROWS, b, G * g:G * g + G, :],
                                     mscr[st].rearrange("(c h) q -> c h q", c=3)).then_inc(s["mrows_loaded"], 16)

            for t in range(TT):
                sp.wait_ge(s["out_done"], t + 1)
                sp.dma_start(a["out"][t * P:(t + 1) * P, :], x_in[:, t, :]).then_inc(s["out_written"], 16)
            sp.wait_ge(s["out_written"], 16 * TT)

        @block.gpsimd
        def _(pool):
            constants = ((vals[:, :, :, :, :], 0.0), (vals[:, :, :, :, DK:DK + 1], 1.0), (kstack[MROW:P, :, :, :], 1.0),
                         (ones[:, :], 1.0), (mrun[:, :, :], MAX_FLOOR), (acc[:, :, :, :], 0.0))
            for i, (where, value) in enumerate(constants):
                if i:
                    pool.wait_ge(s["const_ready"], i)
                pool.memset(where, value).then_inc(s["const_ready"], 1)
            pool.wait_ge(s["const_ready"], len(constants))
            pool.wait_ge(s["list_ready"], 2)
            n = pool.value_load(n_active[0:1, 0:1], min_val=1, max_val=NCH)
            with pool.Fori(0, NCH) as it:
                with pool.If(it < n):
                    pool.wait_ge(s["chunk_loaded"], (it + 1) * 64)
                    pool.wait_ge(s["max_read"], it * A_PER + CREDIT)
                    settle(pool)
                    pool.tensor_scalar(hide_q[:, :, :], mask_q[:, :, :], HIDDEN, None, ALU.mult).then_inc(s["hide_ready"], 1)
                    pool.wait_ge(s["prob_ready"], it * U_PER + CREDIT)
                    pool.wait_ge(s["hide_ready"], it * 2 + 1)
                    settle(pool)
                    pool.tensor_scalar(hide_k[:, :, :], mask_k[:, :, :], HIDDEN, None, ALU.mult).then_inc(s["hide_ready"], 1)
            for t in range(TT):
                pool.wait_ge(s["vg_evac"], 2 * t + 2)
                pool.wait_ge(s["e_ready"], t + 1)
                pool.tensor_scalar(e_tok[:, t % 2, :], e_tok[:, t % 2, :], 1.0, None, ALU.add).then_inc(s["gate_half"], 1)
                pool.wait_ge(s["gate_rcp"], t + 1)
                pool.tensor_tensor(g_tok[:, t, :], g_tok[:, t, :], e_tok[:, t % 2, :], ALU.mult).then_inc(s["gate_half"], 1)
                pool.wait_ge(s["gate_half"], 2 * t + 2)
                gv = g_tok[:, t, :].rearrange("p (h v) -> p h v", h=RH)
                gw = gn_row[:, :].unsqueeze(1).to_broadcast([P, RH, RDV])
                pool.tensor_tensor(gv, gv, gw, ALU.mult).then_inc(s["gate_done"], 1)

        @block.tensor
        def _(pe):
            pe.sem_inc(s["prob_used"], CREDIT)
            pe.wait_ge(s["ident_ready"], 16 + 1)
            pe.wait_ge(s["const_ready"], 4)
            pe.wait_ge(s["seen_ready"], 1)
            pe.matmul(bank[0:1, XB, 0:QT * NCH], ones[:, :], seen[:, :, :], start=True, stop=True).then_inc(s["seen_summed"], 1)
            for t in range(TT):
                pe.wait_ge(s["xn_ready"], t + 1)
                for f in range(KIN):
                    mm = pe.transpose(bank[:, A0 + f, t * P:(t + 1) * P], xn[:, t, f * P:(f + 1) * P], ident[:, :])
            mm.then_inc(s["xnT_ready"], 1)
            pe.wait_ge(s["w_loaded"], 8 * 16)
            pe.wait_ge(s["xnT_evac"], 2)
            for f in range(KIN):
                for c in range(KIN):
                    mm = pe.matmul(bank[:, S0 + f, :], wq[:, c, f * P:(f + 1) * P], xnT[:, c, :], start=(c == 0), stop=(c == KIN - 1))
                mm.then_inc(s["q_ready"], 1)
            pe.wait_ge(s["q_stacked"], 16 * NPROD * NB)
            pe.wait_ge(s["const_ready"], 6)
            pe.wait_ge(s["list_ready"], 2)
            n = pe.value_load(n_active[0:1, 0:1], min_val=1, max_val=NCH)

            def project(it, b):
                for f in range(KIN):
                    if b:
                        pe.wait_ge(s["k_evac"], it * 8 + 2 * f + 2)
                    for c in range(KIN):
                        mm = pe.matmul(bank[:, S0 + f, :], wk[:, c, f * P:(f + 1) * P], ctxT[:, b, c, :],
                                       start=(c == 0), stop=(c == KIN - 1))
                    mm.then_inc(s["kv_ready"], 1)
                for pr in range(2):
                    if b:
                        pe.wait_ge(s["v_evac"], it * 4 + pr + 1)
                    for kt in (2 * pr, 2 * pr + 1):
                        for c in range(KIN):
                            mm = pe.matmul(bank[:, S0 + 2 + pr, (kt % 2) * D:(kt % 2 + 1) * D],
                                           ctxT[:, b, c, kt * P:(kt + 1) * P], wv[:, c, :],
                                           start=(c == 0), stop=(c == KIN - 1))
                    mm.then_inc(s["kv_ready"], 1)

            def max_tile(it, st, i):
                b, g = divmod(st, NG)
                qt, j = divmod(i, G)
                n_ = st * QT * G + i
                pe.wait_ge(s["max_read"], it * A_PER + n_ - 1 + CREDIT)
                pe.matmul(bank[:, A0 + n_ % 2, :], qstack[0:MROW, b, G * g + j, qt * P:(qt + 1) * P],
                          kstack[0:MROW, b, G * g + j, :], start=True, stop=True).then_inc(s["max_ready"], 1)

            def score_unit(it, st, kt):
                b, g = divmod(st, NG)
                u = st * KT + kt
                pe.wait_ge(s["prob_ready"], it * U_PER + u - 1 + CREDIT)
                for jj in range(2):
                    out = bank[:, S0 + 2 * (u % 2) + jj, :]
                    for hh in range(2):
                        h = G * g + 2 * jj + hh
                        pe.matmul(out[:, hh * NQ:(hh + 1) * NQ], kstack[0:KROWS, b, h, kt * P:(kt + 1) * P],
                                  qstack[0:KROWS, b, h, :], start=(hh == 0), stop=False, skip_group_check=True)
                    mm = pe.matmul(out, identb[:, :], hide_k[:, kt, :].unsqueeze(1).to_broadcast([P, 2, NQ]),
                                   start=False, stop=True, skip_group_check=True)
                mm.then_inc(s["score_ready"], 1)

            def value_unit(it, u):
                st, kt = divmod(u, KT)
                b, g = divmod(st, NG)
                if kt == 0:
                    pe.wait_ge(s["out_read"], it * STAGES + st + 1)
                pe.wait_ge(s["prob_ready"], it * U_PER + u + 1 + CREDIT)
                for j in range(G):
                    mm = pe.matmul(bank[32 * j:32 * j + PADV, OB, 0:NQ], vals[:, b, kt, G * g + j, :],
                                   prob[:, u % 3, j * NQ:(j + 1) * NQ], start=(kt == 0), stop=(kt == KT - 1),
                                   tile_position=(0, 32 * j), skip_group_check=True)
                mm.then_inc(s["prob_used"], 1)

            with pe.Fori(0, NCH) as it:
                with pe.If(it < n):
                    pe.wait_ge(s["chunk_loaded"], (it + 1) * 64)
                    pe.wait_ge(s["prob_ready"], it * U_PER + CREDIT)
                    for b in range(NB):
                        project(it, b)
                    for t in range(STEPS):
                        for k in range(KT):
                            if t < STAGES:
                                if k == 0 and t % NG == 0:
                                    pe.wait_ge(k_stacked[t // NG], (it + 1) * 16 * NPROD)
                                max_tile(it, t, 2 * k)
                                max_tile(it, t, 2 * k + 1)
                            u = (t - 2) * KT + k
                            if 0 <= u < U_PER:
                                if u == 0:
                                    pe.wait_ge(s["k_evac"], it * 8 + 8)
                                    pe.wait_ge(s["v_evac"], it * 4 + 4)
                                    pe.wait_ge(s["hide_ready"], it * 2 + 2)
                                if k == 0:
                                    pe.wait_ge(s["mrows_loaded"], (it * STAGES + t - 1) * 16)
                                score_unit(it, t - 2, k)
                            if 0 <= u - 1 < U_PER:
                                value_unit(it, u - 1)
                            if (t, k) in X_INDEX:
                                pe.wait_ge(s["x_read"], it * X_PER + X_INDEX[t, k] + 1)
                            if k == 1 and 1 <= t <= STAGES:
                                pe.wait_ge(s["max_cut"], it * STAGES + t)
                                for qt in range(QT):
                                    mm = pe.transpose(xbank_b[0:3 * G, qt * P:(qt + 1) * P],
                                                      mpart[:, (t - 1) % 2, qt, :, :].rearrange("p c h -> p (c h)"), identb[:, :])
                                mm.then_inc(s["x_ready"], 1)
                            if k == 2 and t >= 3:
                                pe.wait_ge(s["outT_ready"], it * STAGES + t - 2)
                                for qt in range(QT):
                                    mm = pe.transpose(bank[:, XB, qt * P:(qt + 1) * P], outT[:, (t - 3) % 2, qt * P:(qt + 1) * P], ident[:, :])
                                mm.then_inc(s["x_ready"], 1)

            for t in range(TT):
                pe.wait_ge(s["at_ready"], t + 1)
                if t >= 2:
                    pe.wait_ge(s["atT_evac"], t - 1)
                for f in range(KIN):
                    mm = pe.transpose(bank[:, t % 2, f * P:(f + 1) * P], at_tok[:, t, f * P:(f + 1) * P], ident[:, :])
                mm.then_inc(s["atT_ready"], 1)
                pe.wait_ge(s["atT_evac"], t + 1)
                if t >= 2:
                    pe.wait_ge(s["x1_ready"], t - 1)
                for c in range(KIN):
                    mm = pe.matmul(bank[:, 2 + t % 2, 0:D], atT[:, c, t * P:(t + 1) * P], wo[:, c, :], start=(c == 0), stop=(c == KIN - 1))
                mm.then_inc(s["o_ready"], 1)

            pe.wait_ge(s["late_loaded"], 16 * 10)
            pe.wait_ge(s["x1_ready"], TT)
            for t in range(TT):
                pe.wait_ge(s["n2_ready"], t + 1)
                if t:
                    pe.wait_ge(s["n2T_evac"], t)
                for f in range(KIN):
                    mm = pe.transpose(bank[:, 0, f * P:(f + 1) * P], xn[:, t, f * P:(f + 1) * P], ident[:, :])
                mm.then_inc(s["n2T_ready"], 1)
                pe.wait_ge(s["n2T_evac"], t + 1)
                if t:
                    pe.wait_ge(s["rope_ready"], t)
                    pe.wait_ge(s["vg_evac"], 2 * t)
                    pe.wait_ge(s["e_ready"], t)
                for m in range(3):
                    for c in range(KIN):
                        mm = pe.matmul(bank[:, 1 + m, :], xnT[:, c, t * P:(t + 1) * P], w_ret[:, c, m * 512:(m + 1) * 512],
                                       start=(c == 0), stop=(c == KIN - 1))
                    mm.then_inc(s["proj_ready"], 1)
                pe.wait_ge(s["rope_ready"], t + 1)
                if t:
                    pe.wait_ge(s["qkT_evac"], t)
                for f in range(4):
                    mm = pe.transpose(bank[:, 4, f * P:(f + 1) * P], qk_rot[:, t % 2, f * P:(f + 1) * P], ident[:, :])
                mm.then_inc(s["qkT_ready"], 1)

            pe.wait_ge(s["qkT_evac"], TT)
            pe.wait_ge(s["vg_evac"], 2 * TT)
            pe.wait_ge(s["e_ready"], TT)
            pe.wait_ge(s["rope_ready"], TT)

            def ret_scores(r):
                b, h = divmod(r, RH)
                lo = RDK * (h % 2)
                if r >= 2:
                    pe.wait_ge(s["att_done"], r - 1)
                tk = b * NQ
                pe.matmul(bank[:, 6 + r % 2, 0:NQ], qkT[lo:lo + RDK, 2 + h // 2, tk:tk + P], qkT[lo:lo + RDK, h // 2, tk:tk + NQ],
                          start=True, stop=True)
                pe.matmul(bank[:, 6 + r % 2, NQ:NQ + P], qkT[lo:lo + RDK, 2 + h // 2, tk + P:tk + NQ],
                          qkT[lo:lo + RDK, h // 2, tk + P:tk + NQ], start=True, stop=True).then_inc(s["att_ready"], 1)

            def ret_values(r):
                b, h = divmod(r, RH)
                pe.wait_ge(s["att_done"], r + 1)
                cols = slice(h * RDV, (h + 1) * RDV)
                w = attn[:, r % 2, :]
                pe.matmul(bank[:, 2 * b, cols], w[:, 0:P], v_tok[:, 2 * b, cols], start=True, stop=True)
                pe.matmul(bank[:, 2 * b + 1, cols], w[:, P:2 * P], v_tok[:, 2 * b, cols], start=True, stop=False)
                pe.matmul(bank[:, 2 * b + 1, cols], w[:, 2 * P:3 * P], v_tok[:, 2 * b + 1, cols],
                          start=False, stop=True).then_inc(s["ret_ready"], 1)

            for r in range(NB * RH + 1):
                if r < NB * RH:
                    ret_scores(r)
                if r:
                    ret_values(r - 1)

            for t in range(TT):
                pe.wait_ge(s["y_ready"], t + 1)
                if t:
                    pe.wait_ge(s["yT_evac"], t)
                for f in range(4):
                    mm = pe.transpose(bank[:, 4, f * P:(f + 1) * P], y_tok[:, t, f * P:(f + 1) * P], ident[:, :])
                mm.then_inc(s["yT_ready"], 1)
                pe.wait_ge(s["yT_evac"], t + 1)
                if t:
                    pe.wait_ge(s["x2_ready"], t)
                for c in range(4):
                    mm = pe.matmul(bank[:, 5, 0:D], yT[:, c, t * P:(t + 1) * P], w_reto[:, c, :], start=(c == 0), stop=(c == 3))
                mm.then_inc(s["ro_ready"], 1)

            pe.wait_ge(s["x2_ready"], TT)
            for t in range(TT):
                pe.wait_ge(s["n3_ready"], t + 1)
                if t:
                    pe.wait_ge(s["n3T_evac"], t)
                for f in range(KIN):
                    mm = pe.transpose(bank[:, 0, f * P:(f + 1) * P], xn[:, t, f * P:(f + 1) * P], ident[:, :])
                mm.then_inc(s["n3T_ready"], 1)
                pe.wait_ge(s["n3T_evac"], t + 1)
                if t:
                    pe.wait_ge(s["w_ready"], t)
                for c in range(KIN):
                    mm = pe.matmul(bank[:, 1, 0:NE], xnT[:, c, t * P:(t + 1) * P], w_gate[:, c, :], start=(c == 0), stop=(c == KIN - 1))
                mm.then_inc(s["logit_ready"], 1)
                for pr in range(NE // 2):
                    m = t * (NE // 2) + pr
                    if m >= 4:
                        pe.wait_ge(s["pair_read"], 2 * (m - 3))
                    for c in range(KIN):
                        mm = pe.matmul(bank[:, 4 + m % 4, :], xnT[:, c, t * P:(t + 1) * P],
                                       w_exp[:, c, 2 * pr:2 * pr + 2, :], start=(c == 0), stop=(c == KIN - 1))
                    mm.then_inc(s["pair_ready"], 1)
                    if pr == 2:
                        pe.wait_ge(s["w_ready"], t + 1)
                        if t:
                            pe.wait_ge(s["wT_evac"], t)
                        pe.transpose(bank[0:NE, 2, 0:P], nwts[:, t, :], ident[:, :]).then_inc(s["wT_ready"], 1)
                pe.wait_ge(s["wT_evac"], t + 1)
                if t:
                    pe.wait_ge(s["pair_read"], 2 * (4 * (t - 1)) + 1)
                pe.matmul(bank[:, 3, 0:D], wT[:, t % 2, :], b_exp[:, :], start=True, stop=True).then_inc(s["bias_ready"], 1)

        @block.scalar
        def _(act):
            act.sem_inc(s["prob_ready"], CREDIT)
            act.sem_inc(s["out_read"], 1)
            act.wait_ge(s["ident_ready"], 16)
            act.copy(identb[:, :], ident[:, :]).then_inc(s["ident_ready"], 1)
            act.wait_ge(s["xnT_ready"], 1)
            for f in range(KIN):
                act.copy(xnT[:, f, :], bank[:, A0 + f, :]).then_inc(s["xnT_evac"], 1)
            act.wait_ge(s["w_loaded"], 8 * 16)
            act.mul(bq4[:, :], bq[:, :], DK ** -0.5).then_inc(s["q_evac"], 1)
            act.wait_ge(s["q_evac"], 1)
            for f in range(KIN):
                act.wait_ge(s["q_ready"], f + 1)
                act.activation(q32[:, f, :], bank[:, S0 + f, :], ACT.Identity, bias=bq4[:, f:f + 1], scale=DK ** -0.5).then_inc(s["q_evac"], 1)
                act.activation(qpart[:, 0, f, :], bank[:, S0 + f, :], ACT.Identity, bias=bq4[:, f:f + 1], scale=DK ** -0.5).then_inc(s["q_evac"], 1)
            act.wait_ge(s["list_ready"], 2)
            n = act.value_load(n_active[0:1, 0:1], min_val=1, max_val=NCH)

            with act.Fori(0, NCH) as it:
                with act.If(it < n):
                    for b in range(NB):
                        for f in range(KIN):
                            act.wait_ge(s["kv_ready"], it * 8 + 4 * b + f + 1)
                            act.activation(k32[:, b, f, :], bank[:, S0 + f, :], ACT.Identity, bias=bk[:, f:f + 1]).then_inc(s["k_evac"], 1)
                            act.activation(kpart[:, b, 0, f, :], bank[:, S0 + f, :], ACT.Identity, bias=bk[:, f:f + 1]).then_inc(s["k_evac"], 1)
                        for pr in range(2):
                            act.wait_ge(s["kv_ready"], it * 8 + 4 * b + 3 + pr)
                            act.copy(vals[:, b, 2 * pr:2 * pr + 2, :, 0:DK],
                                     bank[:, S0 + 2 + pr, :].rearrange("p (k h d) -> p k h d", k=2, h=NH)).then_inc(s["v_evac"], 1)
                    for t in range(STEPS):
                        for k in range(KT):
                            u = (t - 2) * KT + k
                            if 0 <= u < U_PER:
                                act.wait_ge(s["score_ready"], it * U_PER + u + 1)
                                act.wait_ge(s["prob_used"], it * U_PER + u - 2 + CREDIT)
                                act.activation(prob[:, u % 3, :], bank[:, S0 + 2 * (u % 2):S0 + 2 * (u % 2) + 2, :].rearrange("p b n -> p (b n)"),
                                               ACT.Exp).then_inc(s["prob_ready"], 1)
                            if k == 0 and 3 <= t:
                                act.wait_ge(s["prob_used"], it * U_PER + (t - 2) * KT + CREDIT)
                                act.copy(outT[:, (t - 3) % 2, :], bank[:, OB, 0:NQ]).then_inc(s["outT_ready"], 1)
                                act.wait_ge(s["outT_ready"], it * STAGES + t - 2)
                                act.sem_inc(s["out_read"], 1)
                            if k == 1 and 1 <= t <= STAGES:
                                act.wait_ge(s["diff_ready"], it * STAGES + t)
                                act.activation(alpha[:, (t - 1) % 4, :], mdiff[:, (t - 1) % 2, :], ACT.Exp).then_inc(s["alpha_ready"], 1)

            for t in range(TT):
                act.wait_ge(s["atT_ready"], t + 1)
                act.copy(atT[:, :, t * P:(t + 1) * P], bank[:, t % 2, 0:D].rearrange("p (f q) -> p f q", f=KIN)).then_inc(s["atT_evac"], 1)
            for t in range(TT):
                act.wait_ge(s["n2T_ready"], t + 1)
                if t == 0:
                    act.wait_ge(s["o_ready"], TT)
                act.copy(xnT[:, :, t * P:(t + 1) * P], bank[:, 0, 0:D].rearrange("p (f q) -> p f q", f=KIN)).then_inc(s["n2T_evac"], 1)
                act.wait_ge(s["proj_ready"], 3 * t + 3)
                act.copy(v_tok[:, t, :], bank[:, 2, :]).then_inc(s["vg_evac"], 1)
                act.copy(g_tok[:, t, :], bank[:, 3, :]).then_inc(s["vg_evac"], 1)
                if t >= 2:
                    act.wait_ge(s["gate_half"], 2 * (t - 1))
                act.activation(e_tok[:, t % 2, :], bank[:, 3, :], ACT.Exp, scale=-1.0).then_inc(s["e_ready"], 1)
                act.wait_ge(s["qkT_ready"], t + 1)
                act.copy(qkT[:, :, t * P:(t + 1) * P], bank[:, 4, :].rearrange("p (f q) -> p f q", f=4)).then_inc(s["qkT_evac"], 1)
            for t in range(TT):
                act.wait_ge(s["ret_ready"], RH * (t // 2 + 1))
                if t >= 2:
                    act.wait_ge(s["y_ready"], t - 1)
                act.activation(gsq[:, t % 2, :], bank[:, t, :], ACT.Square).then_inc(s["sq_ready"], 1)
                if t:
                    act.wait_ge(s["yT_ready"], t)
                    act.copy(yT[:, :, (t - 1) * P:t * P], bank[:, 4, :].rearrange("p (f q) -> p f q", f=4)).then_inc(s["yT_evac"], 1)
            act.wait_ge(s["yT_ready"], TT)
            act.copy(yT[:, :, (TT - 1) * P:TT * P], bank[:, 4, :].rearrange("p (f q) -> p f q", f=4)).then_inc(s["yT_evac"], 1)
            for t in range(TT):
                act.wait_ge(s["n3T_ready"], t + 1)
                act.copy(xnT[:, :, t * P:(t + 1) * P], bank[:, 0, 0:D].rearrange("p (f q) -> p f q", f=KIN)).then_inc(s["n3T_evac"], 1)
                act.wait_ge(s["neg_max"], t + 1)
                act.activation(gexp[:, t, :], glog[:, t, :], ACT.Exp, bias=gmax[:, t:t + 1], accum_out=gsum[:, t:t + 1]).then_inc(s["exp_ready"], 1)
                act.wait_ge(s["wT_ready"], t + 1)
                if t >= 2:
                    act.wait_ge(s["bias_ready"], t - 1)
                act.copy(wT[:, t % 2, :], bank[0:NE, 2, 0:P]).then_inc(s["wT_evac"], 1)

        @block.vector
        def _(dve):
            count = {"dve_pre": 0, "dve_post": 0}

            def then(which, ins):
                count[which] += 1
                ins.then_inc(s[which], 1)
                dve.wait_ge(s[which], count[which])

            def rsqrt(which, arg, c1, c2, res):
                then(which, dve.tensor_scalar(res.bitcast(I32), arg.bitcast(I32), -0.5, RSQRT_MAGIC, ALU.mult, ALU.add))
                for _ in range(NEWTON):
                    then(which, dve.scalar_tensor_tensor(c1, res, -0.5, arg, ALU.mult, ALU.mult))
                    then(which, dve.tensor_tensor(c2, c1, res, ALU.mult))
                    then(which, dve.scalar_tensor_tensor(res, c2, 1.5, res, ALU.add, ALU.mult))

            def layernorm(which, src, t, done):
                then(which, dve.bn_stats(stats[:, t, :], src[:, t, :]))
                then(which, dve.bn_aggr(moments[:, t, :], stats[:, t, :]))
                then(which, dve.tensor_scalar(nw[:, 0, 0:1], moments[:, t, 1:2], EPS, None, ALU.add))
                rsqrt(which, nw[:, 0, 0:1], nw[:, 1, 0:1], nw[:, 2, 0:1], nw[:, 3, 0:1])
                dve.tensor_scalar(xn[:, t, :], src[:, t, :], moments[:, t, 0:1], nw[:, 3, 0:1],
                                  ALU.subtract, ALU.mult).then_inc(s[done], 1)
                dve.wait_ge(s[done], t + 1)

            dve.sem_inc(s["max_read"], CREDIT)
            dve.sem_inc(s["x_read"], 1)
            for t in range(TT):
                dve.wait_ge(s["x_loaded"], 16 * TT)
                layernorm("dve_pre", x_in, t, "xn_ready")
            dve.wait_ge(s["mask_loaded"], 32)
            then("dve_pre", dve.tensor_reduce(hid_min[:, :, :], mask_all[:, :, :].bitcast(U16).rearrange("p t (c k) -> p t c k", c=NCH), AXX, ALU.min))
            dve.tensor_scalar(seen[:, :, :], hid_min[:, :, :], 256.5, None, ALU.is_lt).then_inc(s["seen_ready"], 1)
            dve.wait_ge(s["seen_summed"], 1)
            cnt = tiny[:, 0, 0:NCH]
            then("dve_pre", dve.memset(tiny[:, :, :], 0.0))
            then("dve_pre", dve.tensor_copy(tiny[:, 7, 0:NCH], bank[0:1, XB, 0:NCH]))
            then("dve_pre", dve.tensor_tensor(cnt, tiny[:, 7, 0:NCH], bank[0:1, XB, NCH:2 * NCH], ALU.add))
            flag = tiny[:, 1, NCH:2 * NCH]
            then("dve_pre", dve.tensor_scalar(flag, cnt, 0.5, None, ALU.is_gt))
            for i, sh in enumerate((1, 2, 4)):
                then("dve_pre", dve.tensor_tensor(tiny[:, 2 + i, NCH:2 * NCH], tiny[:, 1 + i, NCH:2 * NCH],
                                                  tiny[:, 1 + i, NCH - sh:2 * NCH - sh], ALU.add))
            rank = tiny[:, 4, NCH:2 * NCH]
            numbered = tiny[:, 5, 0:NCH]
            then("dve_pre", dve.tensor_tensor(numbered, flag, index[:, :], ALU.mult))
            for r in range(NCH):
                then("dve_pre", dve.scalar_tensor_tensor(rank_eq[:, r, :], rank, float(r + 1), numbered, ALU.is_equal, ALU.mult))
            then("dve_pre", dve.tensor_reduce(tiny[:, 6, 0:NCH], rank_eq[:, :, :], AXX, ALU.add))
            dve.tensor_copy(chunk_list[:, :], tiny[:, 6, 0:NCH + 1]).then_inc(s["list_ready"], 1)
            dve.tensor_scalar(n_active[:, :], rank[:, NCH - 1:NCH], 1.0, None, ALU.max).then_inc(s["list_ready"], 1)
            dve.wait_ge(s["q_evac"], 2 * KIN + 1)
            then("dve_pre", dve.tensor_tensor(q_rest, q32, qpart[:, 0, :, :], ALU.subtract))
            then("dve_pre", dve.tensor_copy(qpart[:, 1, :, :], q_rest))
            dve.tensor_tensor(qpart[:, 2, :, :], q_rest, qpart[:, 1, :, :], ALU.subtract).then_inc(s["q_cut"], 1)
            dve.wait_ge(s["w_loaded"], 8 * 16)
            then("dve_pre", dve.tensor_tensor(xbo[:, :, :], x_in[:, :, :], bo_row[:, :].unsqueeze(1).to_broadcast([P, TT, D]), ALU.add))
            dve.wait_ge(s["const_ready"], 6)
            dve.wait_ge(s["list_ready"], 2)
            n = dve.value_load(n_active[0:1, 0:1], min_val=1, max_val=NCH)

            with dve.Fori(0, NCH) as it:
                with dve.If(it < n):
                    done = [0]

                    def link(ins):
                        done[0] += 1
                        ins.then_inc(s["dve_loop"], 1)
                        dve.wait_ge(s["dve_loop"], it * DVE_PER + done[0])

                    for b in range(NB):
                        dve.wait_ge(s["k_evac"], it * 8 + 4 * b + 4)
                        link(dve.tensor_tensor(k_rest[:, :, :], k32[:, b, :, :], kpart[:, b, 0, :, :], ALU.subtract))
                        link(dve.tensor_copy(kpart[:, b, 1, :, :], k_rest[:, :, :]))
                        ins = dve.tensor_tensor(kpart[:, b, 2, :, :], k_rest[:, :, :], kpart[:, b, 1, :, :], ALU.subtract)
                        link(ins)
                        dve.sem_inc(s["k_cut"], 1)
                    dve.wait_ge(s["hide_ready"], it * 2 + 1)
                    for t in range(STEPS):
                        for k in range(KT):
                            if t < STAGES:
                                for i in (2 * k, 2 * k + 1):
                                    n_ = t * QT * G + i
                                    dve.wait_ge(s["max_ready"], it * A_PER + n_ + 1)
                                    dve.wait_ge(s["max_read"], it * A_PER + n_ - 1 + CREDIT)
                                    settle(dve)
                                    dve.tensor_tensor_reduce(junk[:, n_ % 2, :], bank[:, A0 + n_ % 2, :], hide_q[:, i // G, :],
                                                             1.0, -3e38, ALU.add, ALU.max, cmax[:, t % 2, i:i + 1]).then_inc(s["max_read"], 1)
                            if k == 1 and 1 <= t <= STAGES:
                                dve.wait_ge(s["x_ready"], it * X_PER + X_INDEX[t, k] + 1)
                                dve.tensor_copy(mrows[:, (t - 1) % 2, :], xbank_b[0:3 * G, 0:NQ]).then_inc(s["mrows_ready"], 1)
                                dve.wait_ge(s["mrows_ready"], it * STAGES + t)
                                dve.sem_inc(s["x_read"], 1)
                            if k == 2 and t >= 3:
                                st = t - 3
                                dve.wait_ge(s["alpha_ready"], it * STAGES + st + 1)
                                link(dve.tensor_tensor(acc[:, st, :, :], acc[:, st, :, :],
                                                       alpha[:, st % 4, :].unsqueeze(2).to_broadcast([P, QT * G, DK + 1]), ALU.mult))
                                dve.wait_ge(s["x_ready"], it * X_PER + X_INDEX[t, k] + 1)
                                link(dve.tensor_tensor(acc[:, st, :, :], acc[:, st, :, :],
                                                       bank[:, XB, 0:NQ].rearrange("p (i e) -> p i e", e=PADV)[:, :, 0:DK + 1], ALU.add))
                                dve.sem_inc(s["x_read"], 1)
                        if t < STAGES:
                            dve.wait_ge(s["max_read"], it * A_PER + (t + 1) * QT * G + CREDIT)
                            link(dve.tensor_tensor(mnew[:, :], mrun[:, t, :], cmax[:, t % 2, :], ALU.max))
                            dve.tensor_tensor(mdiff[:, t % 2, :], mrun[:, t, :], mnew[:, :], ALU.subtract).then_inc(s["diff_ready"], 1)
                            dve.wait_ge(s["diff_ready"], it * STAGES + t + 1)
                            link(dve.tensor_copy(mrun[:, t, :], mnew[:, :]))
                            mp, mv = mpart[:, t % 2, :, :, :], mnew[:, :].rearrange("p (t h) -> p t h", t=QT)
                            link(dve.tensor_scalar(mp[:, :, 0, :], mv, -1.0, None, ALU.mult))
                            link(dve.scalar_tensor_tensor(mrest[:, :, :], mv, -1.0, mp[:, :, 0, :], ALU.mult, ALU.subtract))
                            link(dve.tensor_copy(mp[:, :, 1, :], mrest[:, :, :]))
                            link(dve.tensor_tensor(mp[:, :, 2, :], mrest[:, :, :], mp[:, :, 1, :], ALU.subtract))
                            dve.sem_inc(s["max_cut"], 1)
                    assert done[0] == DVE_PER, done[0]

            then("dve_post", dve.reciprocal(rsum[:, :, :], acc[:, :, :, DK]))
            for t in range(TT):
                b, qt = divmod(t, QT)
                av = acc[:, b * NG:(b + 1) * NG, qt * G:(qt + 1) * G, 0:DK]
                rv = rsum[:, b * NG:(b + 1) * NG, qt * G:(qt + 1) * G].unsqueeze(3).to_broadcast([P, NG, G, DK])
                then("dve_post", dve.tensor_tensor(at_tok[:, t, :].rearrange("p (g h d) -> p g h d", g=NG, h=G), av, rv, ALU.mult))
                dve.tensor_tensor(at_tok[:, t, :], at_tok[:, t, :], bv_row[:, :], ALU.add).then_inc(s["at_ready"], 1)
            for t in range(TT):
                dve.wait_ge(s["o_ready"], t + 1)
                dve.tensor_tensor(x1[:, t, :], bank[:, 2 + t % 2, 0:D], xbo[:, t, :], ALU.add).then_inc(s["x1_ready"], 1)
                dve.wait_ge(s["x1_ready"], t + 1)
                layernorm("dve_post", x1, t, "n2_ready")

            dve.wait_ge(s["late_loaded"], 16 * 10)
            HP = 2 * RH
            for t in range(TT):
                dve.wait_ge(s["proj_ready"], 3 * t + 1)
                if t >= 2:
                    dve.wait_ge(s["qkT_ready"], t - 1)
                qk = bank[:, 1, :].rearrange("p (h e) -> p h e", e=RDK // 2)
                co, si = (rope[:, i, t % 2, :].unsqueeze(1).to_broadcast([P, 2 * HP, RDK // 2]) for i in (0, 1))
                xc, xs = (ropes[:, i, :].rearrange("p (h e) -> p h e", e=RDK // 2) for i in (0, 1))
                then("dve_post", dve.tensor_tensor(xc, qk, co, ALU.mult))
                then("dve_post", dve.tensor_tensor(xs, qk, si, ALU.mult))
                c4, s4 = (ropes[:, i, :].rearrange("p (h two e) -> p h two e", two=2, e=RDK // 2) for i in (0, 1))
                r4 = qk_rot[:, t % 2, :].rearrange("p (h two e) -> p h two e", two=2, e=RDK // 2)
                then("dve_post", dve.tensor_tensor(r4[:, :, 0, :], c4[:, :, 0, :], s4[:, :, 1, :], ALU.subtract))
                then("dve_post", dve.tensor_tensor(r4[:, :, 1, :], c4[:, :, 1, :], s4[:, :, 0, :], ALU.add))
                dve.sem_inc(s["rope_ready"], 1)
                dve.wait_ge(s["gate_half"], 2 * t + 1)
                dve.reciprocal(e_tok[:, t % 2, :], e_tok[:, t % 2, :]).then_inc(s["gate_rcp"], 1)

            for r in range(NB * RH):
                dve.wait_ge(s["att_ready"], r + 1)
                if r >= 2:
                    dve.wait_ge(s["ret_ready"], r - 1)
                dve.tensor_tensor(attn[:, r % 2, :], bank[:, 6 + r % 2, 0:3 * P], decay[:, r % RH, :], ALU.mult).then_inc(s["att_done"], 1)

            for t in range(TT):
                dve.wait_ge(s["sq_ready"], t + 1)
                then("dve_post", dve.tensor_reduce(nw[:, 1, :], gsq[:, t % 2, :].rearrange("p (h v) -> p h v", h=RH), AXX, ALU.add))
                then("dve_post", dve.tensor_scalar(nw[:, 0, :], nw[:, 1, :], 1.0 / RDV, EPS, ALU.mult, ALU.add))
                rsqrt("dve_post", nw[:, 0, :], nw[:, 1, :], nw[:, 2, :], nw[:, 3, :])
                yv = y_tok[:, t, :].rearrange("p (h v) -> p h v", h=RH)
                then("dve_post", dve.tensor_tensor(yv, bank[:, t, :].rearrange("p (h v) -> p h v", h=RH),
                                                   nw[:, 3, :].unsqueeze(2).to_broadcast([P, RH, RDV]), ALU.mult))
                dve.wait_ge(s["gate_done"], t + 1)
                dve.tensor_tensor(y_tok[:, t, :], y_tok[:, t, :], g_tok[:, t, :], ALU.mult).then_inc(s["y_ready"], 1)
            for t in range(TT):
                dve.wait_ge(s["ro_ready"], t + 1)
                dve.tensor_tensor(x2[:, t, :], bank[:, 5, 0:D], x1[:, t, :], ALU.add).then_inc(s["x2_ready"], 1)
                dve.wait_ge(s["x2_ready"], t + 1)
                layernorm("dve_post", x2, t, "n3_ready")

            for t in range(TT):
                dve.wait_ge(s["logit_ready"], t + 1)
                then("dve_post", dve.tensor_tensor(glog[:, t, :], bank[:, 1, 0:NE], gb_row[:, :], ALU.add))
                dve.tensor_reduce(gmax[:, t:t + 1], glog[:, t, :], AXX, ALU.max, negate=True).then_inc(s["neg_max"], 1)
                dve.wait_ge(s["exp_ready"], t + 1)
                then("dve_post", dve.reciprocal(gw1[:, 0:1], gsum[:, t:t + 1]))
                then("dve_post", dve.tensor_scalar(glog[:, t, :], gexp[:, t, :], gw1[:, 0:1], None, ALU.mult))
                then("dve_post", dve.scalar_tensor_tensor(gexp[:, t, :], glog[:, t, :], 0.1, glog[:, t, :], ALU.is_ge, ALU.mult))
                then("dve_post", dve.tensor_reduce(gw1[:, 1:2], gexp[:, t, :], AXX, ALU.add))
                then("dve_post", dve.scalar_tensor_tensor(gw1[:, 2:3], gw1[:, 1:2], 0.0, gw1[:, 1:2], ALU.is_equal, ALU.add))
                then("dve_post", dve.reciprocal(gw1[:, 3:4], gw1[:, 2:3]))
                dve.tensor_scalar(nwts[:, t, :], gexp[:, t, :], gw1[:, 3:4], None, ALU.mult).then_inc(s["w_ready"], 1)
                dve.wait_ge(s["w_ready"], t + 1)
                for e in range(NE):
                    m = t * (NE // 2) + e // 2
                    if e % 2 == 0:
                        dve.wait_ge(s["pair_ready"], m + 1)
                    src = bank[:, 4 + m % 4, (e % 2) * D:(e % 2 + 1) * D]
                    base = x2[:, t, :] if e == 0 else x_in[:, t, :]
                    dve.scalar_tensor_tensor(x_in[:, t, :], src, nwts[:, t, e:e + 1], base, ALU.mult, ALU.add).then_inc(s["pair_read"], 1)
                    dve.wait_ge(s["pair_read"], t * NE + e + 1)
                dve.wait_ge(s["bias_ready"], t + 1)
                dve.tensor_tensor(x_in[:, t, :], x_in[:, t, :], bank[:, 3, 0:D], ALU.add).then_inc(s["out_done"], 1)


def _shape_constants():
    half = RDK // 2
    inv = 1.0 / 10000.0 ** (np.arange(0, RDK, 2, dtype=np.float32) / np.float32(RDK))
    ang = (np.arange(NQ, dtype=np.float32)[:, None] * inv[None, :].astype(np.float32)).astype(np.float32)
    rope = np.stack([np.cos(ang), np.sin(ang)]).astype(np.float32)
    rope = np.ascontiguousarray(rope.reshape(2, QT, P, half).transpose(2, 0, 1, 3))
    gamma = 1.0 - 2.0 ** (-5.0 - np.arange(RH))
    j = np.arange(P)[:, None, None]
    i = np.concatenate([np.arange(NQ), np.arange(P)])[None, None, :]
    diff = i - j
    decay = np.where(diff >= 0, gamma[None, :, None] ** np.maximum(diff, 0), 0.0) * RDK ** -0.5
    return {"ident": np.eye(P, dtype=np.float32), "index": np.arange(NCH, dtype=np.float32)[None, :],
            "rope": rope, "decay": decay.astype(np.float32)}


def kernel(**inputs):
    import concourse.bacc as bacc
    from concourse.bass_utils import run_bass_kernel_spmd as run

    g = {k: np.asarray(v) for k, v in inputs.items()}
    mask = np.ascontiguousarray(g["mask_1x1xSxS2_bk1"].reshape(NQ, NKEY))
    arrays = {
        "x": g["x"].reshape(NB * NQ, D),
        "ctxT": np.ascontiguousarray(g["ctx_1024"].transpose(0, 2, 1)),
        "mask": mask, "maskT": np.ascontiguousarray(mask.T),
        "wq": g["L0_xattn_w_q"].T, "bq": g["L0_xattn_b_q"].reshape(KIN, P).T, "wk": g["L0_xattn_w_k"].T, "bk": g["L0_xattn_b_k"].reshape(KIN, P).T,
        "wv": g["L0_xattn_w_v"].T, "bv": g["L0_xattn_b_v"], "wo": g["L0_xattn_w_o"].T, "bo": g["L0_xattn_b_o"],
        "w_ret": np.concatenate([g["L0_attn_W" + n].T for n in "qkvg"], axis=1),
        "w_reto": g["L0_attn_Wo"].T, "gn": g["L0_attn_gnorm_w"],
        "w_gate": g["L0_ffn_gate_w"], "gb": g["L0_ffn_gate_b"],
        "w_exp": g["L0_ffn_expert_w"], "b_exp": g["L0_ffn_expert_b"],
        **_shape_constants(),
    }
    arrays = {k: np.ascontiguousarray(v) for k, v in arrays.items()}
    nc = bacc.Bacc("TRN2", target_bir_lowering=False, num_devices=1)
    args = {k: nc.dram_tensor(f"in_{k}", v.shape, mybir.dt.from_np(v.dtype), kind="ExternalInput").ap() for k, v in arrays.items()}
    args["kscr"] = nc.dram_tensor("kscr", (NB, 3, D, CH), BF16, kind="Internal").ap()
    args["qscr"] = nc.dram_tensor("qscr", (3, D, TT * P), BF16, kind="Internal").ap()
    args["mscr"] = nc.dram_tensor("mscr", (STAGES, 3 * G, NQ), BF16, kind="Internal").ap()
    args["out"] = nc.dram_tensor("out_x", (NB * NQ, D), F32, kind="ExternalOutput").ap()
    build(nc, args)
    r = run(nc, [{f"in_{k}": v for k, v in arrays.items()}], core_ids=[0])
    return r.results[0]["out_x"].reshape(NB, NQ, D)
```

```python
from contextlib import ExitStack, contextmanager

import numpy as np
import concourse.bass as bass
from concourse import mybir

F32 = mybir.dt.float32
BF16 = mybir.dt.bfloat16
I32 = mybir.dt.int32
U8 = mybir.dt.uint8
U16 = mybir.dt.uint16
ALU = mybir.AluOpType
ACT = mybir.ActivationFunctionType
AXX = mybir.AxisListType.X

P = 128
NB = 2
NQ = 256
D = 256
NKEY = 4096
NH, DK = 16, 16
QT = NQ // P
TT = NB * QT
KIN = D // P
CH = 512
NCH = NKEY // CH
KT = CH // P
G = 4
NG = NH // G
STAGES = NB * NG
PADV = 32
K_PART = (0, 1, 2, 0, 1, 0)
K_RUNS = ((0, 3), (3, 2), (5, 1))
Q_PART = (0, 0, 0, 1, 1, 2)
NPROD = len(K_PART)
MROW = NPROD * DK
KROWS = MROW + 3
HF = P // DK
HIDDEN = -1e30
MAX_FLOOR = -1e20

RH, RDK, RDV = 4, 64, 128
NV = RH * RDV
NE = 8
EPS = 1e-5
RSQRT_MAGIC = float(0x5F3759DF)
NEWTON = 3

AHEAD = 2
TILES = QT * G
A_PER = STAGES * TILES
A_FIRST = AHEAD * TILES
U_PER = STAGES * KT
X_PER = 2 * STAGES
MAX_OPS = 5
FIRST_PIECES = (("k", 0, 0), ("k", 0, 1), ("k", 1, 0), ("k", 1, 1), ("v", 0, 0), ("v", 0, 1))
PIECES = {(0, 0): ("v", 1, 0), (0, 2): ("v", 1, 1), (2, 0): ("k", 0, 0), (2, 2): ("k", 0, 1),
          (4, 1): ("v", 0, 0), (4, 3): ("v", 0, 1), (5, 1): ("k", 1, 0), (5, 3): ("k", 1, 1)}
PIECE_AT = {where: n for n, where in enumerate(PIECES)}
KV_FIRST, KV_PER = 6, 8
KE_FIRST, KE_PER = 8, 8
VE_FIRST, VE_PER = 2, 4


def ring(more):
    place, n = {}, 0
    reads = {"max": A_FIRST, "k": KE_FIRST, "v": VE_FIRST}
    last = [("max", A_FIRST - 1), ("max", A_FIRST)]
    for t in range(STAGES):
        for k in range(KT):
            uses = [("max", t, 2 * k), ("max", t, 2 * k + 1)] if more or t + AHEAD < STAGES else []
            if (t, k) in PIECES and (more or t == 0):
                uses.append((PIECES[t, k][0], t, k))
            for use in uses:
                place[use] = (n % 2,) + last[n % 2]
                reads[use[0]] += 2 if use[0] == "k" else 1
                last[n % 2] = (use[0], reads[use[0]])
                n += 1
    return place


RING = {more: ring(more) for more in (True, False)}


def turned(t):
    return max(2 * t - 1, 0)


def out_turned(st, more):
    return min(2 * st + 2, X_PER - 1) if more or st < STAGES - 2 else 2 * STAGES - 3 + st - (STAGES - 2)


DVE_PER = STAGES * (MAX_OPS + 1) + 1
CREDIT = 3


TURNS = [("at", 0), ("at", 1), ("at", 2), ("at", 3), ("n2", 0), ("n2", 1), ("qk", 0), ("n2", 2), ("qk", 1),
         ("n2", 3), ("qk", 2), ("qk", 3), ("y", 0), ("y", 1), ("n3", 0), ("n3", 1), ("w", 0),
         ("y", 2), ("y", 3), ("w", 1), ("n3", 2), ("n3", 3), ("w", 2), ("w", 3)]
SIDES = [("ro", 0), ("ro", 1), ("logit", 0), ("logit", 1), ("bias", 0), ("ro", 2), ("ro", 3), ("bias", 1),
         ("logit", 2), ("logit", 3), ("bias", 2), ("bias", 3)]
TURN_AT = {use: n for n, use in enumerate(TURNS)}
SIDE_AT = {use: n for n, use in enumerate(SIDES)}
TB, SIDE = 0, 2
PAIR_BANKS = (5, 6, 1, 7)
RET_BANKS = (1, 7, 3, 4)


def build(nc, a):
    with ExitStack() as ctx:
        def sb(name, shape, dt=F32):
            return ctx.enter_context(nc.sbuf_tensor(name, shape, dt))

        def sem(name):
            return ctx.enter_context(nc.semaphore(name))

        ident = sb("ident", [P, P])
        identb = sb("identb", [P, P], BF16)
        ones = sb("ones", [P, 1])
        x_in = sb("x_in", [P, TT, D])
        xbo = sb("xbo", [P, TT, D])
        xn = sb("xn", [P, TT, D])
        xnT = sb("xnT", [P, KIN, TT * P])
        wq = sb("wq", [P, KIN, D])
        wk = sb("wk", [P, KIN, D])
        wv = sb("wv", [P, KIN, D])
        wo = sb("wo", [P, KIN, D])
        bq = sb("bq", [P, KIN])
        bq4 = sb("bq4", [P, KIN])
        bk = sb("bk", [P, KIN])
        bv = sb("bv", [P, KIN])
        bo_row = sb("bo_row", [P, D])
        w_ret = sb("w_ret", [P, KIN, 2 * D + 2 * NV])
        w_reto = sb("w_reto", [P, NV // P, D])
        gn = sb("gn", [P, 1])
        rope = sb("rope", [P, 2, QT, RDK // 2])
        decay = sb("decay", [P, RH, 3 * P])
        w_gate = sb("w_gate", [P, KIN, NE])
        gb_row = sb("gb_row", [P, NE])
        w_exp = sb("w_exp", [P, KIN, NE, D])
        b_exp = sb("b_exp", [NE, D])
        index = sb("index", [1, NCH])

        mask_all = sb("mask_all", [P, QT, NKEY], U8)
        mask_room = mask_all[:, :, :].rearrange("p t k -> p (t k)").bitcast(F32)
        x1 = mask_room[:, 0:TT * D].rearrange("p (t c) -> p t c", t=TT)
        x2 = mask_room[:, TT * D:2 * TT * D].rearrange("p (t c) -> p t c", t=TT)
        hid_min = sb("hid_min", [P, QT, NCH])
        seen = sb("seen", [P, QT, NCH])
        tiny = sb("tiny", [1, 8, 2 * NCH])
        rank_eq = sb("rank_eq", [1, NCH, NCH])
        chunk_list = sb("chunk_list", [1, NCH + 1], I32)
        n_more = sb("n_more", [1, 1], I32)

        ctxT = sb("ctxT", [P, NB, KIN, CH])
        mask_q = sb("mask_q", [P, QT, CH], U8)
        mask_k = sb("mask_k", [P, KT, NQ], U8)
        hide_q = sb("hide_q", [P, QT, CH], BF16)
        hide_k = sb("hide_k", [P, KT, NQ], BF16)
        k32 = sb("k32", [P, NB, KIN, CH])
        k_rest = sb("k_rest", [P, KIN, CH])
        kpart = sb("kpart", [P, NB, 3, KIN, CH], BF16)
        kstack = sb("kstack", [P, NB, NH, CH], BF16)
        qpart = sb("qpart", [P, 3, KIN, TT * P], BF16)
        qstack = sb("qstack", [P, NH, NB, NQ], BF16)
        vals = sb("vals", [P, NB, KT, NH, PADV])
        prob = sb("prob", [P, 3, G * NQ])
        junk = sb("junk", [P, 2, CH], BF16)
        outT = sb("outT", [P, 2, NQ])
        cmax = sb("cmax", [P, 2, QT * G])
        mnew = sb("mnew", [P, QT * G])
        mrun = sb("mrun", [P, STAGES, QT * G])
        mdiff = sb("mdiff", [P, 2, QT * G])
        alpha = sb("alpha", [P, 4, QT * G])
        mrest = sb("mrest", [P, QT, G])
        mpart = sb("mpart", [P, 2, QT, 3, G], BF16)
        mrows = sb("mrows", [3 * G, 2, NQ], BF16)
        acc = sb("acc", [P, STAGES, QT * G, DK + 1])
        rsum = sb("rsum", [P, STAGES, QT * G])
        stats = sb("stats", [P, TT, 6])
        moments = sb("moments", [P, TT, 2])
        glog = sb("glog", [P, TT, NE])
        gexp = sb("gexp", [P, TT, NE])
        nwts = sb("nwts", [P, TT, NE])
        gmax = sb("gmax", [P, TT])
        gsum = sb("gsum", [P, TT])
        gw1 = sb("gw1", [P, 4, QT])
        wT = sb("wT", [NE, TT, P])
        nw = sb("nw", [P, 4, QT * RH])
        sumsq = sb("sumsq", [P, TT, RH])
        prob_flat = prob[:, :, :].rearrange("p a b -> p (a b)")
        q32 = prob_flat[:, 0:KIN * TT * P].rearrange("p (f t) -> p f t", f=KIN)
        q_rest = prob_flat[:, KIN * TT * P:2 * KIN * TT * P].rearrange("p (f t) -> p f t", f=KIN)

        late0 = kstack[:, 0, :, :].rearrange("p h k -> p (h k)").bitcast(F32)
        late1 = kstack[:, 1, :, :].rearrange("p h k -> p (h k)").bitcast(F32)
        late2 = k32[:, :, :, :].rearrange("p b f k -> p (b f k)")
        late3 = kpart[:, :, :, :, :].rearrange("p b c f k -> p (b c f k)").bitcast(F32)
        late4 = vals[:, :, :, :, :].rearrange("p b k h e -> p (b k h e)")
        v_tok = late0[:, 0:TT * NV].rearrange("p (t c) -> p t c", t=TT)
        gated = late0[:, TT * NV:2 * TT * NV].rearrange("p (t c) -> p t c", t=TT)
        qkT = late1[:, 0:4 * TT * P].rearrange("p (f t) -> p f t", f=4)
        yT = late1[:, 2048:4096].rearrange("p (f t) -> p f t", f=4)
        tanh_g = late2[:, 0:2 * NV].rearrange("p (t c) -> p t c", t=2)
        ropes = late3[:, 0:1024].rearrange("p (t c) -> p t c", t=2)
        at_tok = late4[:, 0:TT * D].rearrange("p (t c) -> p t c", t=TT)
        squares = late4[:, 1024:2048].rearrange("p (t c) -> p t c", t=2)
        y_tok = late4[:, 2048:4096].rearrange("p (t c) -> p t c", t=TT)
        attn = late2[:, 1024:1024 + 2 * 384].rearrange("p (r c) -> p r c", r=2)
        qk_rot = late3[:, 2048:3072].rearrange("p (t c) -> p t c", t=2)

        bank = ctx.enter_context(nc.psum_tensor("bank", [P, 8, 512], F32))
        A0, S0, OB, XB = 0, 2, 6, 7
        xbank_b = bank[:, XB, :].bitcast(BF16)

        names = """x_loaded index_loaded w_loaded late_loaded const_ready ident_ready dve_pre xn_ready
            xnT_ready xnT_evac q_ready q_evac q_cut q_written q_stacked seen_ready seen_summed
            list_ready masks_loaded kv_ready k_evac v_evac k_cut k_written hideq_ready hidek_ready max_ready
            max_read max_cut dve_loop pool_cut diff_ready alpha_ready x_ready mrows_ready mrows_written mrows_loaded
            score_ready prob_ready prob_used outT_ready combined
            at_ready at_half o_ready x1_taken n2_ready n3_ready turned turn_taken proj_ready v_taken tanh_ready
            rope_read rope_ready gated_ready att_ready att_done ret_ready sq_ready y_ready side_ready side_taken
            neg_max exp_ready w_ready pair_ready pair_read out_done dve_post out_written settled""".split()
        s = {n: sem(n) for n in names}
        k_stacked = [sem(f"k_stacked{b}") for b in range(NB)]
        mask_loaded = [sem(f"mask_loaded{t}") for t in range(QT)]
        ctx_loaded = [sem(f"ctx_loaded{b}") for b in range(NB)]
        K_READS = 16 * len(K_RUNS)
        evacuated = {"max": (s["max_read"], A_PER), "k": (s["k_evac"], KE_PER), "v": (s["v_evac"], VE_PER)}

        kscr, qscr, mscr = a["kscr"], a["qscr"], a["mscr"]
        block = ctx.enter_context(nc.Block())

        def settle(eng):
            eng.sem_inc(s["settled"], 1)

        @contextmanager
        def each_chunk(eng, count):
            with eng.Fori(0, 2) as fours:
                with eng.If(fours * 4 < count):
                    with eng.Fori(0, 2) as twos:
                        with eng.If(fours * 4 + twos * 2 < count):
                            with eng.Fori(0, 2) as ones_:
                                with eng.If(fours * 4 + twos * 2 + ones_ < count):
                                    yield fours * 4 + twos * 2 + ones_

        @block.sync
        def _(sp):
            for t in range(QT):
                sp.dma_start(mask_all[:, t, :], a["mask"][t * P:(t + 1) * P, :]).then_inc(mask_loaded[t], 16)
            sp.dma_start(index[:, :], a["index"]).then_inc(s["index_loaded"], 16)

            def load_ctx(c, b):
                sp.dma_start(ctxT[:, b, :, :], a["ctxT"][b, :, bass.ds(c * CH, CH)].rearrange("(f p) k -> p f k", p=P)
                             ).then_inc(ctx_loaded[b], 16)

            def load_masks(c):
                sp.dma_start(mask_q[:, :, :], a["mask"][:, bass.ds(c * CH, CH)].rearrange("(t p) k -> p t k", p=P)
                             ).then_inc(s["masks_loaded"], 16)
                sp.dma_start(mask_k[:, :, :], a["maskT"][bass.ds(c * CH, CH), :].rearrange("(t p) q -> p t q", p=P)
                             ).then_inc(s["masks_loaded"], 16)

            def write_k(b):
                for c in range(3):
                    sp.dma_start(kscr[b, :, c].rearrange("f r k -> r f k"), kpart[:, b, c, :, :]).then_inc(s["k_written"], 16)

            def read_k(b):
                for i, parts in K_RUNS:
                    sp.dma_start(kstack[DK * i:DK * (i + parts), b, :, :].rearrange("r (f h) k -> r f (h k)", f=KIN),
                                 kscr[b, :, 0:parts].rearrange("f c (d h) k -> (c d) f (h k)", h=HF)).then_inc(k_stacked[b], 16)

            def turn_maximum(nth, st, before):
                b, g = divmod(st, NG)
                if before is not None:
                    sp.wait_ge(s["mrows_loaded"], before)
                    settle(sp)
                sp.wait_ge(s["mrows_ready"], nth)
                sp.dma_start(mscr[st], mrows[:, st % 2, :]).then_inc(s["mrows_written"], 16)
                sp.wait_ge(s["mrows_written"], nth * 16)
                sp.dma_start(qstack[MROW:KROWS, G * g:G * g + G, b, :],
                             mscr[st].rearrange("(c h) q -> c h q", c=3)).then_inc(s["mrows_loaded"], 16)

            sp.wait_ge(s["list_ready"], 2)
            more_chunks = sp.value_load(n_more[0:1, 0:1], min_val=0, max_val=NCH - 1)
            first = sp.value_load(chunk_list[0:1, 0:1], min_val=0, max_val=NCH - 1)
            for b in range(NB):
                load_ctx(first, b)
            load_masks(first)
            sp.dma_start(w_ret[:, :, :], a["w_ret"].rearrange("(c p) n -> p c n", p=P)).then_inc(s["late_loaded"], 16)
            sp.dma_start(w_exp[:, 0, :, :], a["w_exp"][:, 0:P, :].rearrange("e p n -> p e n")).then_inc(s["late_loaded"], 16)
            sp.wait_ge(s["k_cut"], 1)
            write_k(0)
            sp.wait_ge(s["q_cut"], 1)
            for c in range(3):
                sp.dma_start(qscr[:, c].rearrange("f r t -> r f t"), qpart[:, c, :, :]).then_inc(s["q_written"], 16)
            sp.wait_ge(s["k_written"], 48)
            read_k(0)
            sp.wait_ge(s["q_written"], 48)
            for i, c in enumerate(Q_PART):
                sp.dma_start(qstack[DK * i:DK * (i + 1), :, :, :].rearrange("r (f h) b q -> r f (h b q)", f=KIN),
                             qscr[:, c].rearrange("f (d h) t -> d f (h t)", h=HF)).then_inc(s["q_stacked"], 16)
            sp.wait_ge(s["k_cut"], 2)
            write_k(1)
            turn_maximum(1, 0, None)

            def chunk(it, more):
                if more:
                    nxt = sp.value_load(chunk_list[0:1, bass.ds(it + 1, 1)], min_val=0, max_val=NCH - 1)
                for t in range(STAGES):
                    if t < STAGES - 1:
                        turn_maximum(it * STAGES + t + 2, t + 1, (it * STAGES + t + 1) * 16)
                    if t == 0:
                        sp.wait_ge(s["k_written"], it * 96 + 96)
                        settle(sp)
                        sp.wait_ge(s["score_ready"], it * U_PER + 1)
                        read_k(1)
                        if more:
                            sp.wait_ge(ctx_loaded[0], it * 16 + 16)
                            load_ctx(nxt, 0)
                    if t == 3 and more:
                        sp.wait_ge(s["k_cut"], it * 2 + 3)
                        settle(sp)
                        sp.wait_ge(k_stacked[0], (it + 1) * K_READS)
                        write_k(0)
                    if t == 4 and more:
                        sp.wait_ge(s["k_written"], it * 96 + 144)
                        settle(sp)
                        sp.wait_ge(s["score_ready"], it * U_PER + U_PER // NB + 1)
                        read_k(0)
                    if t == 6 and more:
                        sp.wait_ge(s["k_cut"], it * 2 + 4)
                        settle(sp)
                        sp.wait_ge(k_stacked[1], (it + 1) * K_READS)
                        write_k(1)
                    if t == 1 and more:
                        sp.wait_ge(s["kv_ready"], it * KV_PER + KV_FIRST + 2)
                        settle(sp)
                        sp.wait_ge(ctx_loaded[1], it * 16 + 16)
                        load_ctx(nxt, 1)
                        sp.wait_ge(s["hideq_ready"], it + 1)
                        settle(sp)
                        sp.wait_ge(s["hidek_ready"], it * KT + KT)
                        settle(sp)
                        sp.wait_ge(s["masks_loaded"], it * 32 + 32)
                        load_masks(nxt)
                if more:
                    turn_maximum(it * STAGES + STAGES + 1, 0, (it + 1) * STAGES * 16)
                    sp.wait_ge(s["k_written"], it * 96 + 192)
                    settle(sp)
                    sp.wait_ge(s["mrows_loaded"], (it + 1) * STAGES * 16 + 16)
                    settle(sp)

            with each_chunk(sp, more_chunks) as it:
                chunk(it, True)
            chunk(more_chunks, False)


            for t in range(TT):
                sp.wait_ge(s["out_done"], t + 1)
                sp.dma_start(a["out"][t * P:(t + 1) * P, :], x_in[:, t, :]).then_inc(s["out_written"], 16)
            sp.wait_ge(s["out_written"], 16 * TT)

        @block.gpsimd
        def _(pool):
            constants = ((ones[:, :], 1.0), (vals[:, :, :, :, :], 0.0), (vals[:, :, :, :, DK:DK + 1], 1.0),
                         (kstack[MROW:KROWS, :, :, :], 1.0), (mrun[:, :, :], MAX_FLOOR), (acc[:, :, :, :], 0.0))
            for i, (where, value) in enumerate(constants):
                if i:
                    pool.wait_ge(s["const_ready"], i)
                pool.memset(where, value).then_inc(s["const_ready"], 1)
            pool.wait_ge(s["const_ready"], len(constants))

            def split_k(b, nth):
                rest = pool.tensor_tensor(k_rest[:, :, :], k32[:, b, :, :], kpart[:, b, 0, :, :], ALU.subtract)
                rest.then_inc(s["pool_cut"], 1)
                pool.wait_ge(s["pool_cut"], nth * 2 - 1)
                pool.tensor_tensor(kpart[:, b, 1, :, :], k32[:, b, :, :], kpart[:, b, 0, :, :], ALU.subtract).then_inc(s["pool_cut"], 1)
                pool.wait_ge(s["pool_cut"], nth * 2)
                pool.tensor_tensor(kpart[:, b, 2, :, :], k_rest[:, :, :], kpart[:, b, 1, :, :], ALU.subtract).then_inc(s["k_cut"], 1)

            pool.wait_ge(s["k_evac"], 8)
            pool.wait_ge(s["k_cut"], 1)
            split_k(1, 1)
            pool.wait_ge(s["list_ready"], 2)
            more_chunks = pool.value_load(n_more[0:1, 0:1], min_val=0, max_val=NCH - 1)
            with each_chunk(pool, more_chunks) as it:
                for b in range(NB):
                    pool.wait_ge(s["k_evac"], it * KE_PER + KE_FIRST + 4 * (b + 1))
                    pool.wait_ge(s["k_cut"], it * NB + NB + b)
                    settle(pool)
                    split_k(b, it * NB + b + 2)
                settle(pool)

        def first_bank(i):
            return A0 + i % 6

        @block.tensor
        def _(pe):
            pe.sem_inc(s["prob_used"], CREDIT)
            pe.sem_inc(s["score_ready"], 1)
            pe.wait_ge(s["const_ready"], 1)
            pe.wait_ge(s["seen_ready"], 1)
            pe.matmul(bank[0:1, XB, 0:QT * NCH], ones[:, :], seen[:, :, :], start=True, stop=True).then_inc(s["seen_summed"], 1)

            def project(kind, b, half, bk_):
                if kind == "k":
                    for c in range(KIN):
                        mm = pe.matmul(bank[:, bk_, :], wk[:, c, half * P:(half + 1) * P], ctxT[:, b, c, :],
                                       start=(c == 0), stop=(c == KIN - 1))
                else:
                    for kt in (2 * half, 2 * half + 1):
                        for c in range(KIN):
                            mm = pe.matmul(bank[:, bk_, (kt % 2) * D:(kt % 2 + 1) * D],
                                           ctxT[:, b, c, kt * P:(kt + 1) * P], wv[:, c, :],
                                           start=(c == 0), stop=(c == KIN - 1))
                mm.then_inc(s["kv_ready"], 1)

            def max_tile(st, i, bk_):
                b, g = divmod(st, NG)
                qt, j = divmod(i, G)
                pe.matmul(bank[:, bk_, :], qstack[0:MROW, G * g + j, b, qt * P:(qt + 1) * P],
                          kstack[0:MROW, b, G * g + j, :], start=True, stop=True).then_inc(s["max_ready"], 1)

            def turn_maximum(st):
                for qt in range(QT):
                    mm = pe.transpose(xbank_b[0:3 * G, qt * P:(qt + 1) * P],
                                      mpart[:, st % 2, qt, :, :].rearrange("p c h -> p (c h)"), identb[:, :])
                mm.then_inc(s["x_ready"], 1)

            pe.wait_ge(s["ident_ready"], 16 + 1)
            for t in range(TT):
                pe.wait_ge(s["xn_ready"], t + 1)
                for f in range(KIN):
                    mm = pe.transpose(bank[:, S0 + f, t * P:(t + 1) * P], xn[:, t, f * P:(f + 1) * P], ident[:, :])
            mm.then_inc(s["xnT_ready"], 1)
            pe.wait_ge(s["w_loaded"], 8 * 16)
            for n_, (kind, b, half) in enumerate(FIRST_PIECES):
                pe.wait_ge(ctx_loaded[b], 16)
                if n_ == 2:
                    pe.wait_ge(s["xnT_evac"], 2)
                    for f in range(KIN):
                        for c in range(KIN):
                            mm = pe.matmul(bank[:, S0 + 2 + f, :], wq[:, c, f * P:(f + 1) * P], xnT[:, c, :], start=(c == 0), stop=(c == KIN - 1))
                        mm.then_inc(s["q_ready"], 1)
                if n_ >= 2:
                    pe.wait_ge(s["k_evac"], 2 * (n_ - 1))
                project(kind, b, half, A0 + n_ % 2)
            pe.wait_ge(k_stacked[0], K_READS)
            pe.wait_ge(s["q_stacked"], 16 * NPROD)
            for i in range(A_FIRST):
                if i < 2:
                    pe.wait_ge(s["v_evac"], i + 1)
                elif i < 6:
                    pe.wait_ge(s["q_evac"], 2 * KIN + 1)
                else:
                    pe.wait_ge(s["max_read"], i + 1 - 6)
                max_tile(i // TILES, i % TILES, first_bank(i))
                if i == TILES + 1:
                    pe.wait_ge(s["max_cut"], 1)
                    turn_maximum(0)
            pe.wait_ge(s["const_ready"], 6)
            more_chunks = pe.value_load(n_more[0:1, 0:1], min_val=0, max_val=NCH - 1)

            def score_pair(it, st, kt, jj):
                b, g = divmod(st, NG)
                u = st * KT + kt
                if jj == 0:
                    pe.wait_ge(s["prob_ready"], it * U_PER + u - 1 + CREDIT)
                out = bank[:, S0 + 2 * (u % 2) + jj, :]
                for hh in range(2):
                    h = G * g + 2 * jj + hh
                    pe.matmul(out[:, hh * NQ:(hh + 1) * NQ], kstack[0:KROWS, b, h, kt * P:(kt + 1) * P],
                              qstack[0:KROWS, h, b, :], start=(hh == 0), stop=False, skip_group_check=True)
                mm = pe.matmul(out, identb[:, :], hide_k[:, kt, :].unsqueeze(1).to_broadcast([P, 2, NQ]),
                               start=False, stop=True, skip_group_check=True)
                if jj == 1:
                    mm.then_inc(s["score_ready"], 1)

            def value_unit(it, u):
                st, kt = divmod(u, KT)
                b, g = divmod(st, NG)
                if kt == 0:
                    pe.wait_ge(s["outT_ready"], it * STAGES + st + 1)
                pe.wait_ge(s["prob_ready"], it * U_PER + u + 1 + CREDIT)
                for j in range(G):
                    mm = pe.matmul(bank[32 * j:32 * j + PADV, OB, 0:NQ], vals[:, b, kt, G * g + j, :],
                                   prob[:, u % 3, j * NQ:(j + 1) * NQ], start=(kt == 0), stop=(kt == KT - 1),
                                   tile_position=(0, 32 * j), skip_group_check=True)
                mm.then_inc(s["prob_used"], 1)

            def turn_outputs(it, st):
                pe.wait_ge(s["outT_ready"], it * STAGES + st + 2)
                for qt in range(QT):
                    mm = pe.transpose(bank[:, XB, qt * P:(qt + 1) * P], outT[:, st % 2, qt * P:(qt + 1) * P], ident[:, :])
                mm.then_inc(s["x_ready"], 1)

            def chunk(it, more):
                for t in range(STAGES):
                    for k in range(KT):
                        if t == 2 and k == 0:
                            pe.wait_ge(k_stacked[1], (it + 1) * K_READS)
                        ahead = more or t + AHEAD < STAGES
                        if t == 6 and k == 0 and more:
                            pe.wait_ge(k_stacked[0], (it + 2) * K_READS)
                        def next_tile(i):
                            bk_, kind, count = RING[more]["max", t, i]
                            sem_, per = evacuated[kind]
                            pe.wait_ge(sem_, it * per + count)
                            max_tile((t + AHEAD) % STAGES, i, A0 + bk_)

                        if ahead:
                            next_tile(2 * k)
                        if k == 0:
                            pe.wait_ge(s["mrows_loaded"], (it * STAGES + t + 1) * 16)
                        if t == 0:
                            pe.wait_ge(s["hidek_ready"], it * KT + k + 1)
                        score_pair(it, t, k, 0)
                        if ahead:
                            next_tile(2 * k + 1)
                        score_pair(it, t, k, 1)
                        if (t, k) in PIECES and (more or t == 0):
                            kind_, b, half = PIECES[t, k]
                            if (t, k) == (2, 0):
                                pe.wait_ge(ctx_loaded[0], (it + 2) * 16)
                            if (t, k) == (5, 1):
                                pe.wait_ge(ctx_loaded[1], (it + 2) * 16)
                            bk_, kind, count = RING[more][kind_, t, k]
                            sem_, per = evacuated[kind]
                            pe.wait_ge(sem_, it * per + count)
                            project(kind_, b, half, A0 + bk_)
                        u = t * KT + k - 1
                        if u >= 0:
                            if k == 1 and t % NG == 0:
                                pe.wait_ge(s["v_evac"], it * VE_PER + VE_FIRST + 2 * (t // NG))
                            value_unit(it, u)
                        if k == 0 and (more or t + 1 < STAGES):
                            pe.wait_ge(s["max_cut"], it * STAGES + t + 2)
                            if t == 1:
                                pe.wait_ge(s["mrows_ready"], it * STAGES + 2)
                            else:
                                pe.wait_ge(s["combined"], it * STAGES + max(t - 1, 0) + 1)
                            turn_maximum((t + 1) % STAGES)
                        if k == 2 and t >= 1:
                            if more or t + 1 < STAGES:
                                pe.wait_ge(s["mrows_ready"], it * STAGES + t + 2)
                            else:
                                pe.wait_ge(s["combined"], it * STAGES + t)
                            turn_outputs(it, t - 1)
                value_unit(it, U_PER - 1)
                pe.wait_ge(s["combined"], it * STAGES + STAGES)
                turn_outputs(it, STAGES - 1)

            with each_chunk(pe, more_chunks) as it:
                chunk(it, True)
            chunk(more_chunks, False)

            turns, sides = [], []

            def turn(kind, t, out, src, blocks, width=P):
                assert TURNS[len(turns)] == (kind, t)
                if turns:
                    pe.wait_ge(s["turn_taken"], len(turns))
                for f in range(blocks):
                    mm = pe.transpose(out[:, f * P:(f + 1) * P], src[:, f * width:(f + 1) * width], ident[:, :])
                mm.then_inc(s["turned"], 1)
                turns.append((kind, t))

            def taken(kind, t):
                pe.wait_ge(s["turn_taken"], TURN_AT[kind, t] + 1)

            def side(kind, t):
                assert SIDES[len(sides)] == (kind, t)
                if sides:
                    pe.wait_ge(s["side_taken"], len(sides))
                sides.append((kind, t))
                return bank[:, SIDE, :]

            def attention_out(t):
                taken("at", t)
                for c in range(KIN):
                    mm = pe.matmul(bank[:, 2 + t, 0:D], xnT[:, c, t * P:(t + 1) * P], wo[:, c, :], start=(c == 0), stop=(c == KIN - 1))
                mm.then_inc(s["o_ready"], 1)

            def turn_at(t):
                pe.wait_ge(s["at_ready"], t + 1)
                turn("at", t, bank[:, TB, :], at_tok[:, t, :], KIN)

            turn_at(0)
            turn_at(1)
            attention_out(0)
            turn_at(2)
            attention_out(1)
            turn_at(3)
            attention_out(2)
            attention_out(3)

            def turn_xn(kind, t):
                pe.wait_ge(s[kind + "_ready"], t + 1)
                turn(kind, t, bank[:, TB, :], xn[:, t, :], KIN)

            def project_ret(t, m):
                taken("n2", t)
                pe.wait_ge(s["x1_taken"], min(m + 1, TT))
                if t:
                    pe.wait_ge(s[("rope_read", "v_taken", "gated_ready")[m]], t)
                for c in range(KIN):
                    mm = pe.matmul(bank[:, 2 + m, :], xnT[:, c, t * P:(t + 1) * P], w_ret[:, c, m * 512:(m + 1) * 512],
                                   start=(c == 0), stop=(c == KIN - 1))
                mm.then_inc(s["proj_ready"], 1)

            def turn_qk(t):
                pe.wait_ge(s["rope_ready"], t + 1)
                turn("qk", t, bank[:, TB, :], qk_rot[:, t % 2, :], 4)

            pe.wait_ge(s["late_loaded"], 16 * 10)
            turn_xn("n2", 0)
            turn_xn("n2", 1)
            for t in range(TT):
                project_ret(t, 0)
                if t:
                    turn_qk(t - 1)
                    if t + 1 < TT:
                        turn_xn("n2", t + 1)
                project_ret(t, 1)
                project_ret(t, 2)

            def ret_scores(r):
                b, h = divmod(r, RH)
                lo = RDK * (h % 2)
                taken("qk", 2 * b + 1)
                if r >= 2:
                    pe.wait_ge(s["att_done"], r - 1)
                else:
                    pe.wait_ge(s["x1_taken"], TT)
                out = bank[:, 5 + r % 2, :]
                tk = b * NQ
                pe.matmul(out[:, 0:NQ], qkT[lo:lo + RDK, 2 + h // 2, tk:tk + P], qkT[lo:lo + RDK, h // 2, tk:tk + NQ],
                          start=True, stop=True)
                pe.matmul(out[:, NQ:NQ + P], qkT[lo:lo + RDK, 2 + h // 2, tk + P:tk + NQ],
                          qkT[lo:lo + RDK, h // 2, tk + P:tk + NQ], start=True, stop=True).then_inc(s["att_ready"], 1)

            def ret_values(r):
                b, h = divmod(r, RH)
                pe.wait_ge(s["v_taken"], TT if b else QT)
                if b:
                    pe.wait_ge(s["gated_ready"], TT)
                pe.wait_ge(s["att_done"], r + 1)
                cols = slice(h * RDV, (h + 1) * RDV)
                w = attn[:, r % 2, :]
                early, late_ = bank[:, RET_BANKS[2 * b], cols], bank[:, RET_BANKS[2 * b + 1], cols]
                pe.matmul(early, w[:, 0:P], v_tok[:, 2 * b, cols], start=True, stop=True)
                pe.matmul(late_, w[:, P:2 * P], v_tok[:, 2 * b, cols], start=True, stop=False)
                pe.matmul(late_, w[:, 2 * P:3 * P], v_tok[:, 2 * b + 1, cols],
                          start=False, stop=True).then_inc(s["ret_ready"], 1)

            ret_scores(0)
            ret_scores(1)
            ret_values(0)
            turn_qk(TT - 1)
            for r in range(2, NB * RH):
                ret_scores(r)
                ret_values(r - 1)
            ret_values(NB * RH - 1)

            def retention_out(t):
                taken("y", t)
                pe.wait_ge(s["rope_read"], TT)
                out = side("ro", t)
                for c in range(4):
                    mm = pe.matmul(out[:, 0:D], yT[:, c, t * P:(t + 1) * P], w_reto[:, c, :], start=(c == 0), stop=(c == 3))
                mm.then_inc(s["side_ready"], 1)

            def turn_y(t):
                pe.wait_ge(s["y_ready"], RH * (t + 1))
                turn("y", t, bank[:, TB, :], y_tok[:, t, :], 4)

            def logits(t):
                taken("n3", t)
                out = side("logit", t)
                for c in range(KIN):
                    mm = pe.matmul(out[:, 0:NE], xnT[:, c, t * P:(t + 1) * P], w_gate[:, c, :], start=(c == 0), stop=(c == KIN - 1))
                mm.then_inc(s["side_ready"], 1)

            def pair(t, pr):
                m = t * (NE // 2) + pr
                if m >= len(PAIR_BANKS):
                    pe.wait_ge(s["pair_read"], 2 * (m - len(PAIR_BANKS) + 1))
                for c in range(KIN):
                    mm = pe.matmul(bank[:, PAIR_BANKS[m % 4], :], xnT[:, c, t * P:(t + 1) * P],
                                   w_exp[:, c, 2 * pr:2 * pr + 2, :], start=(c == 0), stop=(c == KIN - 1))
                mm.then_inc(s["pair_ready"], 1)

            def turn_weights(t):
                pe.wait_ge(s["w_ready"], t // QT + 1)
                turn("w", t, bank[0:NE, TB, :], nwts[:, t, :], 1, NE)

            def biases(t):
                taken("w", t)
                out = side("bias", t)
                pe.matmul(out[:, 0:D], wT[:, t, :], b_exp[:, :], start=True, stop=True).then_inc(s["side_ready"], 1)

            turn_y(0)
            turn_y(1)
            retention_out(0)
            retention_out(1)
            turn_xn("n3", 0)
            turn_xn("n3", 1)
            logits(0)
            logits(1)
            pe.wait_ge(s["att_done"], NB * RH)
            for pr in range(4):
                pair(0, pr)
            turn_weights(0)
            turn_y(2)
            biases(0)
            turn_y(3)
            retention_out(2)
            retention_out(3)
            pair(1, 0)
            turn_weights(1)
            pair(1, 1)
            biases(1)
            turn_xn("n3", 2)
            turn_xn("n3", 3)
            pair(1, 2)
            logits(2)
            logits(3)
            pair(1, 3)
            pair(2, 0)
            pair(2, 1)
            turn_weights(2)
            pair(2, 2)
            turn_weights(3)
            biases(2)
            pair(2, 3)
            for pr in range(4):
                pair(3, pr)
                if pr == 1:
                    biases(3)

        @block.scalar
        def _(act):
            act.sem_inc(s["prob_ready"], CREDIT)
            act.sem_inc(s["outT_ready"], 1)
            for t in range(TT):
                act.dma_start(x_in[:, t, :], a["x"][t * P:(t + 1) * P, :]).then_inc(s["x_loaded"], 16)
            act.dma_start(ident[:, :], a["ident"]).then_inc(s["ident_ready"], 16)
            for w, nm in ((wk, "wk"), (wq, "wq"), (wv, "wv"), (wo, "wo")):
                act.dma_start(w[:, :, :], a[nm].rearrange("(c p) n -> p c n", p=P)).then_inc(s["w_loaded"], 16)
            for w, nm in ((bk, "bk"), (bq, "bq"), (bv, "bv")):
                act.dma_start(w[:, :], a[nm]).then_inc(s["w_loaded"], 16)
            act.dma_start(bo_row[:, :], a["bo"].rearrange("(a n) -> a n", a=1).to_broadcast([P, D])).then_inc(s["w_loaded"], 16)
            act.wait_ge(s["ident_ready"], 16)
            act.copy(identb[:, :], ident[:, :]).then_inc(s["ident_ready"], 1)
            act.wait_ge(s["w_loaded"], 8 * 16)
            act.mul(bq4[:, :], bq[:, :], DK ** -0.5).then_inc(s["q_evac"], 1)
            act.wait_ge(s["q_evac"], 1)

            def take(kind, b, half, bk_):
                if kind == "k":
                    act.activation(k32[:, b, half, :], bank[:, bk_, :], ACT.Identity, bias=bk[:, half:half + 1]).then_inc(s["k_evac"], 1)
                    act.activation(kpart[:, b, 0, half, :], bank[:, bk_, :], ACT.Identity, bias=bk[:, half:half + 1]).then_inc(s["k_evac"], 1)
                else:
                    act.copy(vals[:, b, 2 * half:2 * half + 2, :, 0:DK],
                             bank[:, bk_, :].rearrange("p (k h d) -> p k h d", k=2, h=NH)).then_inc(s["v_evac"], 1)

            act.wait_ge(s["xnT_ready"], 1)
            for f in range(KIN):
                act.copy(xnT[:, f, :], bank[:, S0 + f, :]).then_inc(s["xnT_evac"], 1)
            for n_, (kind, b, half) in enumerate(FIRST_PIECES):
                if n_ == 2:
                    for f in range(KIN):
                        act.wait_ge(s["q_ready"], f + 1)
                        act.activation(q32[:, f, :], bank[:, S0 + 2 + f, :], ACT.Identity, bias=bq4[:, f:f + 1], scale=DK ** -0.5).then_inc(s["q_evac"], 1)
                        act.activation(qpart[:, 0, f, :], bank[:, S0 + 2 + f, :], ACT.Identity, bias=bq4[:, f:f + 1], scale=DK ** -0.5).then_inc(s["q_evac"], 1)
                if n_ == 4:
                    act.wait_ge(s["const_ready"], 3)
                act.wait_ge(s["kv_ready"], n_ + 1)
                take(kind, b, half, A0 + n_ % 2)
            act.wait_ge(k_stacked[0], K_READS)
            act.wait_ge(s["q_stacked"], 16 * NPROD)
            for w, nm in ((w_reto, "w_reto"), (w_gate, "w_gate")):
                act.dma_start(w[:, :, :], a[nm].rearrange("(c p) n -> p c n", p=P)).then_inc(s["late_loaded"], 16)
            act.dma_start(w_exp[:, 1, :, :], a["w_exp"][:, P:2 * P, :].rearrange("e p n -> p e n")).then_inc(s["late_loaded"], 16)
            act.dma_start(b_exp[:, :], a["b_exp"]).then_inc(s["late_loaded"], 16)
            act.dma_start(rope[:, :, :, :], a["rope"]).then_inc(s["late_loaded"], 16)
            act.dma_start(decay[:, :, :], a["decay"]).then_inc(s["late_loaded"], 16)
            act.dma_start(gn[:, :], a["gn"].rearrange("(p a) -> p a", a=1)).then_inc(s["late_loaded"], 16)
            act.dma_start(gb_row[:, :], a["gb"].rearrange("(a n) -> a n", a=1).to_broadcast([P, NE])).then_inc(s["late_loaded"], 16)
            act.wait_ge(s["diff_ready"], 1)
            act.activation(alpha[:, 0, :], mdiff[:, 0, :], ACT.Exp).then_inc(s["alpha_ready"], 1)
            act.wait_ge(s["list_ready"], 2)
            more_chunks = act.value_load(n_more[0:1, 0:1], min_val=0, max_val=NCH - 1)

            def take_outputs(it, st):
                act.wait_ge(s["prob_used"], it * U_PER + (st + 1) * KT + CREDIT)
                act.copy(outT[:, st % 2, :], bank[:, OB, 0:NQ]).then_inc(s["outT_ready"], 1)

            def chunk(it, more):
                for t in range(STAGES):
                    for k in range(KT):
                        u = t * KT + k
                        act.wait_ge(s["score_ready"], it * U_PER + u + 2)
                        act.wait_ge(s["prob_used"], it * U_PER + u - 2 + CREDIT)
                        act.activation(prob[:, u % 3, :], bank[:, S0 + 2 * (u % 2):S0 + 2 * (u % 2) + 2, :].rearrange("p b n -> p (b n)"),
                                       ACT.Exp).then_inc(s["prob_ready"], 1)
                        if (t, k) in PIECES and (more or t == 0):
                            kind, b, half = PIECES[t, k]
                            act.wait_ge(s["kv_ready"], it * KV_PER + KV_FIRST + PIECE_AT[t, k] + 1)
                            take(kind, b, half, A0 + RING[more][kind, t, k][0])
                        if k == 0 and t >= 1:
                            take_outputs(it, t - 1)
                        if k == 1 and (more or t + 1 < STAGES):
                            st = (t + 1) % STAGES
                            act.wait_ge(s["diff_ready"], it * STAGES + t + 2)
                            act.activation(alpha[:, st % 4, :], mdiff[:, st % 2, :], ACT.Exp).then_inc(s["alpha_ready"], 1)
                take_outputs(it, STAGES - 1)

            with each_chunk(act, more_chunks) as it:
                chunk(it, True)
            chunk(more_chunks, False)

            takes = []

            def take_turn(kind, t, out, src, **how):
                assert TURNS[len(takes)] == (kind, t)
                act.wait_ge(s["turned"], len(takes) + 1)
                act.activation(out, src, ACT.Identity if "bias" in how else ACT.Copy, **how).then_inc(s["turn_taken"], 1)
                takes.append((kind, t))

            def take_xn(kind, t):
                take_turn(kind, t, xnT[:, :, t * P:(t + 1) * P], bank[:, TB, 0:D].rearrange("p (f q) -> p f q", f=KIN))

            for t in range(TT):
                act.wait_ge(s["turned"], t + 1)
                act.activation(xnT[:, 0, t * P:(t + 1) * P], bank[:, TB, 0:P], ACT.Identity, bias=bv[:, 0:1]).then_inc(s["at_half"], 1)
                take_turn("at", t, xnT[:, 1, t * P:(t + 1) * P], bank[:, TB, P:2 * P], bias=bv[:, 1:2])

            def take_v(t):
                act.wait_ge(s["proj_ready"], 3 * t + 2)
                act.copy(v_tok[:, t, :], bank[:, 3, :]).then_inc(s["v_taken"], 1)

            def gate(t):
                act.wait_ge(s["proj_ready"], 3 * t + 3)
                if t >= 2:
                    act.wait_ge(s["gated_ready"], t - 1)
                act.activation(tanh_g[:, t % 2, :], bank[:, 4, :], ACT.Tanh, scale=0.5).then_inc(s["tanh_ready"], 1)

            def take_qk(t):
                take_turn("qk", t, qkT[:, :, t * P:(t + 1) * P], bank[:, TB, :].rearrange("p (f q) -> p f q", f=4))

            def squares_of(t):
                act.wait_ge(s["ret_ready"], RH * (t // QT + 1))
                if t >= 2:
                    act.wait_ge(s["sq_ready"], RH * (t - 1))
                for h in range(RH):
                    act.activation(squares[:, t % 2, h * RDV:(h + 1) * RDV], bank[:, RET_BANKS[t], h * RDV:(h + 1) * RDV],
                                   ACT.Square, accum_out=sumsq[:, t, h:h + 1]).then_inc(s["sq_ready"], 1)

            def take_y(t):
                take_turn("y", t, yT[:, :, t * P:(t + 1) * P], bank[:, TB, :].rearrange("p (f q) -> p f q", f=4), scale=gn[:, 0:1])

            def gate_exp(t):
                act.wait_ge(s["neg_max"], t // QT + 1)
                act.activation(gexp[:, t, :], glog[:, t, :], ACT.Exp, bias=gmax[:, t:t + 1], accum_out=gsum[:, t:t + 1]).then_inc(s["exp_ready"], 1)

            def take_weights(t):
                take_turn("w", t, wT[:, t, :], bank[0:NE, TB, 0:P])

            take_xn("n2", 0)
            take_xn("n2", 1)
            for t in range(TT):
                if t:
                    take_qk(t - 1)
                    if t + 1 < TT:
                        take_xn("n2", t + 1)
                take_v(t)
                gate(t)
            take_qk(TT - 1)
            squares_of(0)
            squares_of(1)
            act.wait_ge(s["late_loaded"], 16 * 10)
            take_y(0)
            take_y(1)
            squares_of(2)
            squares_of(3)
            take_xn("n3", 0)
            take_xn("n3", 1)
            gate_exp(0)
            gate_exp(1)
            take_weights(0)
            take_y(2)
            take_y(3)
            take_weights(1)
            take_xn("n3", 2)
            take_xn("n3", 3)
            gate_exp(2)
            gate_exp(3)
            take_weights(2)
            take_weights(3)

        @block.vector
        def _(dve):
            count = {"dve_pre": 0, "dve_post": 0}

            def then(which, ins, wait=True):
                count[which] += 1
                ins.then_inc(s[which], 1)
                if wait:
                    dve.wait_ge(s[which], count[which])

            def rsqrt(which, arg, c1, c2, res, between=()):
                others = list(between)
                then(which, dve.tensor_scalar(res.bitcast(I32), arg.bitcast(I32), -0.5, RSQRT_MAGIC, ALU.mult, ALU.add))
                for _ in range(NEWTON):
                    then(which, dve.scalar_tensor_tensor(c1, res, -0.5, arg, ALU.mult, ALU.mult))
                    if others:
                        others.pop(0)()
                    then(which, dve.tensor_tensor(c2, c1, res, ALU.mult))
                    then(which, dve.scalar_tensor_tensor(res, c2, 1.5, res, ALU.add, ALU.mult))
                assert not others

            def layernorms(which, src, tiles, done):
                t0, m = tiles[0], len(tiles)
                for t in tiles:
                    then(which, dve.bn_stats(stats[:, t, :], src[:, t, :]), t == tiles[-1])
                for t in tiles:
                    then(which, dve.bn_aggr(moments[:, t, :], stats[:, t, :]), t == tiles[-1])
                then(which, dve.tensor_scalar(nw[:, 0, 0:m], moments[:, t0:t0 + m, 1], EPS, None, ALU.add))
                rsqrt(which, nw[:, 0, 0:m], nw[:, 1, 0:m], nw[:, 2, 0:m], nw[:, 3, 0:m])
                for t in tiles:
                    dve.tensor_scalar(xn[:, t, :], src[:, t, :], moments[:, t, 0:1], nw[:, 3, t - t0:t - t0 + 1],
                                      ALU.subtract, ALU.mult).then_inc(s[done], 1)
                dve.wait_ge(s[done], tiles[-1] + 1)

            dve.sem_inc(s["combined"], 1)
            then("dve_pre", dve.memset(tiny[:, :, :], 0.0), False)
            for t in range(QT):
                dve.wait_ge(mask_loaded[t], 16)
                then("dve_pre", dve.tensor_reduce(hid_min[:, t, :], mask_all[:, t, :].bitcast(U16).rearrange("p (c k) -> p c k", c=NCH), AXX, ALU.min), t == QT - 1)
            dve.wait_ge(s["index_loaded"], 16)
            dve.tensor_scalar(seen[:, :, :], hid_min[:, :, :], 256.5, None, ALU.is_lt).then_inc(s["seen_ready"], 1)
            dve.wait_ge(s["seen_summed"], 1)
            cnt = tiny[:, 0, 0:NCH]
            then("dve_pre", dve.tensor_copy(tiny[:, 7, 0:NCH], bank[0:1, XB, 0:NCH]))
            then("dve_pre", dve.tensor_tensor(cnt, tiny[:, 7, 0:NCH], bank[0:1, XB, NCH:2 * NCH], ALU.add))
            flag = tiny[:, 1, NCH:2 * NCH]
            then("dve_pre", dve.tensor_scalar(flag, cnt, 0.5, None, ALU.is_gt))
            for i, sh in enumerate((1, 2, 4)):
                then("dve_pre", dve.tensor_tensor(tiny[:, 2 + i, NCH:2 * NCH], tiny[:, 1 + i, NCH:2 * NCH],
                                                  tiny[:, 1 + i, NCH - sh:2 * NCH - sh], ALU.add))
            rank = tiny[:, 4, NCH:2 * NCH]
            numbered = tiny[:, 5, 0:NCH]
            then("dve_pre", dve.tensor_tensor(numbered, flag, index[:, :], ALU.mult))
            for r in range(NCH):
                then("dve_pre", dve.scalar_tensor_tensor(rank_eq[:, r, :], rank, float(r + 1), numbered, ALU.is_equal, ALU.mult), r == NCH - 1)
            then("dve_pre", dve.tensor_reduce(tiny[:, 6, 0:NCH], rank_eq[:, :, :], AXX, ALU.add))
            dve.tensor_copy(chunk_list[:, :], tiny[:, 6, 0:NCH + 1]).then_inc(s["list_ready"], 1)
            dve.tensor_scalar(n_more[:, :], rank[:, NCH - 1:NCH], 1.0, 1.0, ALU.max, ALU.subtract).then_inc(s["list_ready"], 1)
            dve.wait_ge(s["x_loaded"], 16 * TT)
            layernorms("dve_pre", x_in, range(TT), "xn_ready")

            def take_maximum(st, i, bk_):
                dve.tensor_tensor_reduce(junk[:, i % 2, :], bank[:, bk_, :], hide_q[:, i // G, :],
                                         1.0, -3e38, ALU.add, ALU.max, cmax[:, st % 2, i:i + 1]).then_inc(s["max_read"], 1)

            def new_maximum(st, nth, link):
                mp, mv = mpart[:, st % 2, :, :, :], mnew[:, :].rearrange("p (t h) -> p t h", t=QT)
                link(dve.tensor_tensor(mnew[:, :], mrun[:, st, :], cmax[:, st % 2, :], ALU.max))
                dve.tensor_tensor(mdiff[:, st % 2, :], mrun[:, st, :], mnew[:, :], ALU.subtract).then_inc(s["diff_ready"], 1)
                link(dve.tensor_scalar(mp[:, :, 0, :], mv, -1.0, None, ALU.mult))
                dve.wait_ge(s["diff_ready"], nth)
                link(dve.tensor_copy(mrun[:, st, :], mnew[:, :]), wait=False)
                link(dve.scalar_tensor_tensor(mrest[:, :, :], mv, -1.0, mp[:, :, 0, :], ALU.mult, ALU.subtract), wait=False)
                link(dve.scalar_tensor_tensor(mp[:, :, 1, :], mv, -1.0, mp[:, :, 0, :], ALU.mult, ALU.subtract))
                dve.tensor_tensor(mp[:, :, 2, :], mrest[:, :, :], mp[:, :, 1, :], ALU.subtract).then_inc(s["max_cut"], 1)

            def pre(ins, wait=True):
                then("dve_pre", ins, wait)

            def cut_half(rest, whole, parts, last):
                pre(dve.tensor_tensor(rest, whole, parts(0), ALU.subtract))
                pre(dve.tensor_copy(parts(1), rest))
                if last is None:
                    pre(dve.tensor_tensor(parts(2), rest, parts(1), ALU.subtract), False)
                else:
                    dve.tensor_tensor(parts(2), rest, parts(1), ALU.subtract).then_inc(last, 1)

            dve.wait_ge(s["masks_loaded"], 32)
            dve.tensor_scalar(hide_q[:, :, :], mask_q[:, :, :], HIDDEN, None, ALU.mult).then_inc(s["hideq_ready"], 1)
            for f in range(KIN):
                dve.wait_ge(s["k_evac"], 2 * f + 2)
                cut_half(k_rest[:, f, :], k32[:, 0, f, :], lambda c: kpart[:, 0, c, f, :], s["k_cut"] if f == KIN - 1 else None)
            for f in range(KIN):
                dve.wait_ge(s["q_evac"], 2 * f + 3)
                cut_half(q_rest[:, f, :], q32[:, f, :], lambda c: qpart[:, c, f, :], s["q_cut"] if f == KIN - 1 else None)
            for kt in range(KT):
                dve.tensor_scalar(hide_k[:, kt, :], mask_k[:, kt, :], HIDDEN, None, ALU.mult).then_inc(s["hidek_ready"], 1)
            dve.wait_ge(s["w_loaded"], 8 * 16)
            pre(dve.tensor_tensor(xbo[:, :, :], x_in[:, :, :], bo_row[:, :].unsqueeze(1).to_broadcast([P, TT, D]), ALU.add))
            dve.wait_ge(s["const_ready"], 6)
            dve.wait_ge(s["hideq_ready"], 1)
            for i in range(A_FIRST):
                dve.wait_ge(s["max_ready"], i + 1)
                if i >= 2:
                    dve.wait_ge(s["max_read"], i - 1)
                take_maximum(i // TILES, i % TILES, first_bank(i))
                if i % TILES == TILES - 1:
                    dve.wait_ge(s["max_read"], i + 1)
                    new_maximum(i // TILES, i // TILES + 1, pre)
                if i == TILES + 1:
                    dve.wait_ge(s["x_ready"], 1)
                    dve.tensor_copy(mrows[:, 0, :], xbank_b[0:3 * G, 0:NQ]).then_inc(s["mrows_ready"], 1)
            dve.wait_ge(s["list_ready"], 2)
            more_chunks = dve.value_load(n_more[0:1, 0:1], min_val=0, max_val=NCH - 1)

            def chunk(it, more):
                done = [0]

                def link(ins, wait=True):
                    done[0] += 1
                    ins.then_inc(s["dve_loop"], 1)
                    if wait:
                        dve.wait_ge(s["dve_loop"], it * DVE_PER + done[0])

                def combine(st):
                    dve.wait_ge(s["alpha_ready"], it * STAGES + st + 1)
                    link(dve.tensor_tensor(acc[:, st, :, :], acc[:, st, :, :],
                                           alpha[:, st % 4, :].unsqueeze(2).to_broadcast([P, QT * G, DK + 1]), ALU.mult))
                    dve.wait_ge(s["x_ready"], it * X_PER + 1 + out_turned(st, more) + 1)
                    dve.tensor_tensor(acc[:, st, :, :], acc[:, st, :, :],
                                      bank[:, XB, 0:NQ].rearrange("p (i e) -> p i e", e=PADV)[:, :, 0:DK + 1], ALU.add).then_inc(s["combined"], 1)
                    dve.wait_ge(s["combined"], it * STAGES + st + 2)

                def hide_next(kt):
                    dve.wait_ge(s["score_ready"], it * U_PER + (STAGES - 1) * KT + kt + 2)
                    settle(dve)
                    dve.tensor_scalar(hide_k[:, kt, :], mask_k[:, kt, :], HIDDEN, None, ALU.mult).then_inc(s["hidek_ready"], 1)

                for t in range(STAGES):
                    ahead = more or t + AHEAD < STAGES
                    for k in range(KT):
                        if k == 1 and (more or t + 1 < STAGES):
                            dve.wait_ge(s["x_ready"], it * X_PER + 1 + turned(t) + 1)
                            dve.wait_ge(s["mrows_written"], (it * STAGES + t + 1) * 16)
                            dve.tensor_copy(mrows[:, (t + 1) % 2, :], xbank_b[0:3 * G, 0:NQ]).then_inc(s["mrows_ready"], 1)
                        for i in (2 * k, 2 * k + 1) if ahead else ():
                            n_ = A_FIRST + t * TILES + i
                            dve.wait_ge(s["max_ready"], it * A_PER + n_ + 1)
                            dve.wait_ge(s["max_read"], it * A_PER + n_ - 1)
                            settle(dve)
                            take_maximum((t + AHEAD) % STAGES, i, A0 + RING[more]["max", t, i][0])
                        if t == STAGES - 1 and k >= 1 and more:
                            hide_next(k - 1)
                        if k == 2 and t >= 1:
                            combine(t - 1)
                    if ahead:
                        dve.wait_ge(s["max_read"], it * A_PER + A_FIRST + (t + 1) * TILES)
                        dve.wait_ge(s["alpha_ready"], it * STAGES + t + 1)
                        new_maximum((t + AHEAD) % STAGES, it * STAGES + t + AHEAD + 1, link)
                    if t == STAGES - AHEAD - 1 and more:
                        dve.wait_ge(s["masks_loaded"], (it + 2) * 32)
                        link(dve.tensor_scalar(hide_q[:, :, :], mask_q[:, :, :], HIDDEN, None, ALU.mult))
                        dve.sem_inc(s["hideq_ready"], 1)
                if more:
                    hide_next(KT - 1)
                combine(STAGES - 1)
                settle(dve)
                assert done[0] == DVE_PER or not more, done[0]

            with each_chunk(dve, more_chunks) as it:
                chunk(it, True)
            chunk(more_chunks, False)

            def post(ins, wait=True):
                then("dve_post", ins, wait)

            post(dve.reciprocal(rsum[:, :, :], acc[:, :, :, DK]))
            for t in range(TT):
                b, qt = divmod(t, QT)
                av = acc[:, b * NG:(b + 1) * NG, qt * G:(qt + 1) * G, 0:DK]
                rv = rsum[:, b * NG:(b + 1) * NG, qt * G:(qt + 1) * G].unsqueeze(3).to_broadcast([P, NG, G, DK])
                dve.tensor_tensor(at_tok[:, t, :].rearrange("p (g h d) -> p g h d", g=NG, h=G), av, rv, ALU.mult).then_inc(s["at_ready"], 1)
            for b in range(NB):
                tiles = range(QT * b, QT * b + QT)
                for t in tiles:
                    dve.wait_ge(s["o_ready"], t + 1)
                    dve.tensor_tensor(x1[:, t, :], bank[:, 2 + t, 0:D], xbo[:, t, :], ALU.add).then_inc(s["x1_taken"], 1)
                dve.wait_ge(s["x1_taken"], tiles[-1] + 1)
                layernorms("dve_post", x1, tiles, "n2_ready")

            dve.wait_ge(s["late_loaded"], 16 * 10)
            HP = 2 * RH
            for t in range(TT):
                dve.wait_ge(s["proj_ready"], 3 * t + 1)
                if t >= 2:
                    dve.wait_ge(s["turned"], TURN_AT["qk", t - 2] + 1)
                qk = bank[:, 2, :].rearrange("p (h e) -> p h e", e=RDK // 2)
                co, si = (rope[:, i, t % 2, :].unsqueeze(1).to_broadcast([P, 2 * HP, RDK // 2]) for i in (0, 1))
                xc, xs = (ropes[:, i, :].rearrange("p (h e) -> p h e", e=RDK // 2) for i in (0, 1))
                post(dve.tensor_tensor(xc, qk, co, ALU.mult))
                dve.tensor_tensor(xs, qk, si, ALU.mult).then_inc(s["rope_read"], 1)
                dve.wait_ge(s["rope_read"], t + 1)
                c4, s4 = (ropes[:, i, :].rearrange("p (h two e) -> p h two e", two=2, e=RDK // 2) for i in (0, 1))
                r4 = qk_rot[:, t % 2, :].rearrange("p (h two e) -> p h two e", two=2, e=RDK // 2)
                post(dve.tensor_tensor(r4[:, :, 0, :], c4[:, :, 0, :], s4[:, :, 1, :], ALU.subtract))
                dve.tensor_tensor(r4[:, :, 1, :], c4[:, :, 1, :], s4[:, :, 0, :], ALU.add).then_inc(s["rope_ready"], 1)
                dve.wait_ge(s["rope_ready"], t + 1)
                dve.wait_ge(s["tanh_ready"], t + 1)
                dve.scalar_tensor_tensor(gated[:, t, :], tanh_g[:, t % 2, :], 1.0, bank[:, 4, :], ALU.add, ALU.mult).then_inc(s["gated_ready"], 1)

            def decay_weights(r):
                dve.wait_ge(s["att_ready"], r + 1)
                if r >= 2:
                    dve.wait_ge(s["ret_ready"], r - 1)
                dve.tensor_tensor(attn[:, r % 2, :], bank[:, 5 + r % 2, 0:3 * P], decay[:, r % RH, :], ALU.mult).then_inc(s["att_done"], 1)

            def norm_and_gate(b, between=()):
                tiles = range(QT * b, QT * b + QT)
                dve.wait_ge(s["sq_ready"], RH * (tiles[-1] + 1))
                sums = sumsq[:, QT * b:QT * (b + 1), :].rearrange("p t h -> p (t h)")
                post(dve.tensor_scalar(nw[:, 0, :], sums, 4.0 / RDV, 4.0 * EPS, ALU.mult, ALU.add))
                rsqrt("dve_post", nw[:, 0, :], nw[:, 1, :], nw[:, 2, :], nw[:, 3, :], between)
                dve.wait_ge(s["gated_ready"], tiles[-1] + 1)
                for t in tiles:
                    for h in range(RH):
                        cols = slice(h * RDV, (h + 1) * RDV)
                        i = (t % QT) * RH + h
                        dve.scalar_tensor_tensor(y_tok[:, t, cols], bank[:, RET_BANKS[t], cols], nw[:, 3, i:i + 1],
                                                 gated[:, t, cols], ALU.mult, ALU.mult).then_inc(s["y_ready"], 1)

            def second_stream(b):
                tiles = range(QT * b, QT * b + QT)
                for t in tiles:
                    n_ = SIDE_AT["ro", t] + 1
                    dve.wait_ge(s["side_ready"], n_)
                    dve.tensor_tensor(x2[:, t, :], bank[:, SIDE, 0:D], x1[:, t, :], ALU.add).then_inc(s["side_taken"], 1)
                dve.wait_ge(s["side_taken"], n_)
                dve.wait_ge(s["y_ready"], RH * QT * (b + 1))
                layernorms("dve_post", x2, tiles, "n3_ready")

            def gate_logits(b):
                tiles = range(QT * b, QT * b + QT)
                both = slice(QT * b, QT * b + QT)
                for t in tiles:
                    n_ = SIDE_AT["logit", t] + 1
                    dve.wait_ge(s["side_ready"], n_)
                    dve.tensor_tensor(glog[:, t, :], bank[:, SIDE, 0:NE], gb_row[:, :], ALU.add).then_inc(s["side_taken"], 1)
                dve.wait_ge(s["side_taken"], n_)
                dve.tensor_reduce(gmax[:, both], glog[:, both, :], AXX, ALU.max, negate=True).then_inc(s["neg_max"], 1)

            def gate_weights(b):
                both = slice(QT * b, QT * b + QT)

                def wide(i):
                    return gw1[:, i, :].unsqueeze(2).to_broadcast([P, QT, NE])

                dve.wait_ge(s["exp_ready"], QT * (b + 1))
                post(dve.reciprocal(gw1[:, 0, :], gsum[:, both]))
                post(dve.tensor_tensor(glog[:, both, :], gexp[:, both, :], wide(0), ALU.mult))
                post(dve.scalar_tensor_tensor(gexp[:, both, :], glog[:, both, :], 0.1, glog[:, both, :], ALU.is_ge, ALU.mult))
                post(dve.tensor_reduce(gw1[:, 1, :], gexp[:, both, :], AXX, ALU.add))
                post(dve.scalar_tensor_tensor(gw1[:, 2, :], gw1[:, 1, :], 0.0, gw1[:, 1, :], ALU.is_equal, ALU.add))
                post(dve.reciprocal(gw1[:, 3, :], gw1[:, 2, :]))
                dve.tensor_tensor(nwts[:, both, :], gexp[:, both, :], wide(3), ALU.mult).then_inc(s["w_ready"], 1)
                dve.wait_ge(s["w_ready"], b + 1)

            def add_experts(t, experts):
                for e in experts:
                    m = t * (NE // 2) + e // 2
                    dve.wait_ge(s["pair_ready"], m + 1)
                    src = bank[:, PAIR_BANKS[m % 4], (e % 2) * D:(e % 2 + 1) * D]
                    base = x2[:, t, :] if e == 0 else x_in[:, t, :]
                    dve.scalar_tensor_tensor(x_in[:, t, :], src, nwts[:, t, e:e + 1], base, ALU.mult, ALU.add).then_inc(s["pair_read"], 1)
                    dve.wait_ge(s["pair_read"], t * NE + e + 1)

            def add_biases(t):
                n_ = SIDE_AT["bias", t] + 1
                dve.wait_ge(s["side_ready"], n_)
                dve.tensor_tensor(x_in[:, t, :], x_in[:, t, :], bank[:, SIDE, 0:D], ALU.add).then_inc(s["side_taken"], 1)
                dve.wait_ge(s["side_taken"], n_)

            for r in range(RH + 1):
                decay_weights(r)
            norm_and_gate(0, [lambda r=r: decay_weights(r) for r in range(RH + 1, NB * RH)])
            second_stream(0)
            norm_and_gate(1)
            gate_logits(0)
            gate_weights(0)
            add_experts(0, range(0, 4))
            add_biases(0)
            add_experts(0, range(4, NE))
            dve.sem_inc(s["out_done"], 1)
            second_stream(1)
            add_experts(1, range(0, 4))
            add_biases(1)
            gate_logits(1)
            add_experts(1, range(4, NE))
            dve.sem_inc(s["out_done"], 1)
            gate_weights(1)
            for t in (2, 3):
                add_experts(t, range(0, 4))
                add_biases(t)
                add_experts(t, range(4, NE))
                dve.sem_inc(s["out_done"], 1)


def _shape_constants():
    half = RDK // 2
    inv = 1.0 / 10000.0 ** (np.arange(0, RDK, 2, dtype=np.float32) / np.float32(RDK))
    ang = (np.arange(NQ, dtype=np.float32)[:, None] * inv[None, :].astype(np.float32)).astype(np.float32)
    rope = np.stack([np.cos(ang), np.sin(ang)]).astype(np.float32)
    rope = np.ascontiguousarray(rope.reshape(2, QT, P, half).transpose(2, 0, 1, 3))
    gamma = 1.0 - 2.0 ** (-5.0 - np.arange(RH))
    j = np.arange(P)[:, None, None]
    i = np.concatenate([np.arange(NQ), np.arange(P)])[None, None, :]
    diff = i - j
    decay = np.where(diff >= 0, gamma[None, :, None] ** np.maximum(diff, 0), 0.0) * RDK ** -0.5
    return {"ident": np.eye(P, dtype=np.float32), "index": np.arange(NCH, dtype=np.float32)[None, :],
            "rope": rope, "decay": decay.astype(np.float32)}


def by_head(w):
    return w.reshape(KIN, HF, DK, *w.shape[1:]).swapaxes(1, 2).reshape(w.shape)


def kernel(**inputs):
    import concourse.bacc as bacc
    from concourse.bass_utils import run_bass_kernel_spmd as run

    g = {k: np.asarray(v) for k, v in inputs.items()}
    mask = np.ascontiguousarray(g["mask_1x1xSxS2_bk1"].reshape(NQ, NKEY))
    arrays = {
        "x": g["x"].reshape(NB * NQ, D),
        "ctxT": np.ascontiguousarray(g["ctx_1024"].transpose(0, 2, 1)),
        "mask": mask, "maskT": np.ascontiguousarray(mask.T),
        "wq": by_head(g["L0_xattn_w_q"]).T, "bq": by_head(g["L0_xattn_b_q"]).reshape(KIN, P).T,
        "wk": by_head(g["L0_xattn_w_k"]).T, "bk": by_head(g["L0_xattn_b_k"]).reshape(KIN, P).T,
        "wv": g["L0_xattn_w_v"].T, "bv": g["L0_xattn_b_v"].reshape(KIN, P).T, "wo": g["L0_xattn_w_o"].T, "bo": g["L0_xattn_b_o"],
        "w_ret": np.concatenate([g["L0_attn_W" + n].T for n in "qkvg"], axis=1),
        "w_reto": g["L0_attn_Wo"].T, "gn": g["L0_attn_gnorm_w"],
        "w_gate": g["L0_ffn_gate_w"], "gb": g["L0_ffn_gate_b"],
        "w_exp": g["L0_ffn_expert_w"], "b_exp": g["L0_ffn_expert_b"],
        **_shape_constants(),
    }
    arrays = {k: np.ascontiguousarray(v) for k, v in arrays.items()}
    nc = bacc.Bacc("TRN2", target_bir_lowering=False, num_devices=1)
    args = {k: nc.dram_tensor(f"in_{k}", v.shape, mybir.dt.from_np(v.dtype), kind="ExternalInput").ap() for k, v in arrays.items()}
    args["kscr"] = nc.dram_tensor("kscr", (NB, KIN, 3, P, CH), BF16, kind="Internal").ap()
    args["qscr"] = nc.dram_tensor("qscr", (KIN, 3, P, TT * P), BF16, kind="Internal").ap()
    args["mscr"] = nc.dram_tensor("mscr", (STAGES, 3 * G, NQ), BF16, kind="Internal").ap()
    args["out"] = nc.dram_tensor("out_x", (NB * NQ, D), F32, kind="ExternalOutput").ap()
    build(nc, args)
    r = run(nc, [{f"in_{k}": v for k, v in arrays.items()}], core_ids=[0])
    return r.results[0]["out_x"].reshape(NB, NQ, D)
```

```python
from contextlib import ExitStack, contextmanager

import numpy as np
import concourse.bass as bass
from concourse import mybir

F32 = mybir.dt.float32
BF16 = mybir.dt.bfloat16
I32 = mybir.dt.int32
U8 = mybir.dt.uint8
U16 = mybir.dt.uint16
ALU = mybir.AluOpType
ACT = mybir.ActivationFunctionType
AXX = mybir.AxisListType.X

P = 128
NB = 2
NQ = 256
D = 256
NKEY = 4096
NH, DK = 16, 16
QT = NQ // P
TT = NB * QT
KIN = D // P
CH = 512
NCH = NKEY // CH
KT = CH // P
G = 4
NG = NH // G
STAGES = NB * NG
PADV = 32
K_PART = (0, 1, 2, 0, 1, 0)
K_RUNS = ((0, 3), (3, 2), (5, 1))
Q_PART = (0, 0, 0, 1, 1, 2)
NPROD = len(K_PART)
MROW = NPROD * DK
KROWS = MROW + 3
HF = P // DK
HIDDEN = -1e30
MAX_FLOOR = -1e20

RH, RDK, RDV = 4, 64, 128
NV = RH * RDV
NE = 8
EPS = 1e-5
RSQRT_MAGIC = float(0x5F3759DF)
NEWTON = 3

AHEAD = 2
TILES = QT * G
A_PER = STAGES * TILES
A_FIRST = AHEAD * TILES
U_PER = STAGES * KT
X_PER = 2 * STAGES
MAX_OPS = 5
FIRST_PIECES = (("k", 0, 0), ("k", 0, 1), ("k", 1, 0), ("k", 1, 1), ("v", 0, 0), ("v", 0, 1))
PIECES = {(0, 0): ("v", 1, 0), (0, 2): ("v", 1, 1), (2, 0): ("k", 0, 0), (2, 2): ("k", 0, 1),
          (4, 1): ("v", 0, 0), (4, 3): ("v", 0, 1), (5, 1): ("k", 1, 0), (5, 3): ("k", 1, 1)}
PIECE_AT = {where: n for n, where in enumerate(PIECES)}
KV_FIRST, KV_PER = 6, 8
KE_FIRST, KE_PER = 8, 8
VE_FIRST, VE_PER = 2, 4


def ring(more):
    place, n = {}, 0
    reads = {"max": A_FIRST, "k": KE_FIRST, "v": VE_FIRST}
    last = [("max", A_FIRST - 1), ("max", A_FIRST)]
    for t in range(STAGES):
        for k in range(KT):
            uses = [("max", t, 2 * k), ("max", t, 2 * k + 1)] if more or t + AHEAD < STAGES else []
            if (t, k) in PIECES and (more or t == 0):
                uses.append((PIECES[t, k][0], t, k))
            for use in uses:
                place[use] = (n % 2,) + last[n % 2]
                reads[use[0]] += 2 if use[0] == "k" else 1
                last[n % 2] = (use[0], reads[use[0]])
                n += 1
    return place


RING = {more: ring(more) for more in (True, False)}


def turned(t):
    return max(2 * t - 1, 0)


def out_turned(st, more):
    return min(2 * st + 2, X_PER - 1) if more or st < STAGES - 2 else 2 * STAGES - 3 + st - (STAGES - 2)


DVE_PER = STAGES * MAX_OPS
WARM_UP = 10
CREDIT = 3


TURNS = [("at", 0), ("at", 1), ("n2", 0), ("n2", 1), ("at", 2), ("at", 3), ("qk", 0), ("n2", 2), ("qk", 1),
         ("n2", 3), ("qk", 2), ("qk", 3), ("y", 0), ("y", 1), ("n3", 0), ("n3", 1), ("w", 0),
         ("y", 2), ("y", 3), ("w", 1), ("n3", 2), ("n3", 3), ("w", 2), ("w", 3)]
SIDES = [("ro", 0), ("ro", 1), ("logit", 0), ("logit", 1), ("bias", 0), ("ro", 2), ("ro", 3), ("bias", 1),
         ("logit", 2), ("logit", 3), ("bias", 2), ("bias", 3)]
TURN_AT = {use: n for n, use in enumerate(TURNS)}
SIDE_AT = {use: n for n, use in enumerate(SIDES)}
TB, SIDE = 0, 2
AT_BANKS = (0, 1, 5, 6)
TWO_BANKS = 6


def turn_bank(kind, t):
    n = TURN_AT[kind, t]
    return n % 2 if n < TWO_BANKS else TB


PAIR_BANKS = (5, 6, 1, 7)
RET_BANKS = (1, 7, 3, 4)


def build(nc, a):
    with ExitStack() as ctx:
        def sb(name, shape, dt=F32):
            return ctx.enter_context(nc.sbuf_tensor(name, shape, dt))

        def sem(name):
            return ctx.enter_context(nc.semaphore(name))

        ident = sb("ident", [P, P])
        identb = sb("identb", [P, P], BF16)
        ones = sb("ones", [P, 1])
        x_in = sb("x_in", [P, TT, D])
        xbo = sb("xbo", [P, TT, D])
        xn = sb("xn", [P, TT, D])
        xnT = sb("xnT", [P, KIN, TT * P])
        wq = sb("wq", [P, KIN, D])
        wk = sb("wk", [P, KIN, D])
        wv = sb("wv", [P, KIN, D])
        wo = sb("wo", [P, KIN, D])
        bq = sb("bq", [P, KIN])
        bq4 = sb("bq4", [P, KIN])
        bk = sb("bk", [P, KIN])
        bv = sb("bv", [P, KIN])
        bo_row = sb("bo_row", [P, D])
        w_ret = sb("w_ret", [P, KIN, 2 * D + 2 * NV])
        w_reto = sb("w_reto", [P, NV // P, D])
        gn = sb("gn", [P, 1])
        rope = sb("rope", [P, 2, QT, RDK // 2])
        decay = sb("decay", [P, RH, 3 * P])
        w_gate = sb("w_gate", [P, KIN, NE])
        gb_row = sb("gb_row", [P, NE])
        w_exp = sb("w_exp", [P, KIN, NE, D])
        b_exp = sb("b_exp", [NE, D])
        index = sb("index", [1, NCH])

        mask_all = sb("mask_all", [P, QT, NKEY], U8)
        mask_room = mask_all[:, :, :].rearrange("p t k -> p (t k)").bitcast(F32)
        x1 = mask_room[:, 0:TT * D].rearrange("p (t c) -> p t c", t=TT)
        x2 = mask_room[:, TT * D:2 * TT * D].rearrange("p (t c) -> p t c", t=TT)
        hid_end = sb("hid_end", [P, QT, NCH])
        seen = sb("seen", [P, QT, NCH])
        hidden = sb("hidden", [P, QT, NCH])
        clear = sb("clear", [1, 2, NCH])
        clear_list = sb("clear_list", [1, NCH], I32)
        tiny = sb("tiny", [1, 8, 2 * NCH])
        rank_eq = sb("rank_eq", [1, NCH, NCH])
        chunk_list = sb("chunk_list", [1, NCH + 1], I32)
        n_more = sb("n_more", [1, 1], I32)

        ctxT = sb("ctxT", [P, NB, KIN, CH])
        mask_q = sb("mask_q", [P, QT, CH], U8)
        mask_k = sb("mask_k", [P, KT, NQ], U8)
        hide_q = sb("hide_q", [P, QT, CH], BF16)
        hide_k = sb("hide_k", [P, KT, NQ], BF16)
        k32 = sb("k32", [P, NB, KIN, CH])
        k_rest = sb("k_rest", [P, KIN, CH])
        kpart = sb("kpart", [P, NB, KIN, 3, CH], BF16)
        kstack = sb("kstack", [P, NB, NH, CH], BF16)
        qpart = sb("qpart", [P, KIN, 3, TT * P], BF16)
        qstack = sb("qstack", [P, NH, NB, NQ], BF16)
        vals = sb("vals", [P, NB, KT, NH, PADV])
        prob = sb("prob", [P, 3, G * NQ])
        junk = sb("junk", [P, 2, CH], BF16)
        outT = sb("outT", [P, 2, NQ])
        cmax = sb("cmax", [P, 2, QT * G])
        mnew = sb("mnew", [P, QT * G])
        mrun = sb("mrun", [P, STAGES, QT * G])
        mdiff = sb("mdiff", [P, 2, QT * G])
        alpha = sb("alpha", [P, 4, QT * G])
        mrest = sb("mrest", [P, QT, G])
        mpart = sb("mpart", [P, 2, QT, 3, G], BF16)
        mrows = sb("mrows", [3 * G, 2, NQ], BF16)
        acc = sb("acc", [P, STAGES, QT * G, DK + 1])
        rsum = sb("rsum", [P, STAGES, QT * G])
        stats = sb("stats", [P, TT, 6])
        moments = sb("moments", [P, TT, 2])
        glog = sb("glog", [P, TT, NE])
        gexp = sb("gexp", [P, TT, NE])
        nwts = sb("nwts", [P, TT, NE])
        gmax = sb("gmax", [P, TT])
        gsum = sb("gsum", [P, TT])
        gw1 = sb("gw1", [P, 4, QT])
        wT = sb("wT", [NE, TT, P])
        nw = sb("nw", [P, 4, QT * RH])
        sumsq = sb("sumsq", [P, TT, RH])
        prob_flat = prob[:, :, :].rearrange("p a b -> p (a b)")
        q32 = prob_flat[:, 0:KIN * TT * P].rearrange("p (f t) -> p f t", f=KIN)
        q_rest = prob_flat[:, KIN * TT * P:2 * KIN * TT * P].rearrange("p (f t) -> p f t", f=KIN)

        late0 = kstack[:, 0, :, :].rearrange("p h k -> p (h k)").bitcast(F32)
        late1 = kstack[:, 1, :, :].rearrange("p h k -> p (h k)").bitcast(F32)
        late2 = k32[:, :, :, :].rearrange("p b f k -> p (b f k)")
        late3 = kpart[:, :, :, :, :].rearrange("p b f c k -> p (b f c k)").bitcast(F32)
        late4 = vals[:, :, :, :, :].rearrange("p b k h e -> p (b k h e)")
        v_tok = late0[:, 0:TT * NV].rearrange("p (t c) -> p t c", t=TT)
        gated = late0[:, TT * NV:2 * TT * NV].rearrange("p (t c) -> p t c", t=TT)
        qkT = late1[:, 0:4 * TT * P].rearrange("p (f t) -> p f t", f=4)
        yT = late1[:, 2048:4096].rearrange("p (f t) -> p f t", f=4)
        tanh_g = late2[:, 0:2 * NV].rearrange("p (t c) -> p t c", t=2)
        ropes = late3[:, 0:1024].rearrange("p (t c) -> p t c", t=2)
        at_tok = late4[:, 0:TT * D].rearrange("p (t c) -> p t c", t=TT)
        squares = late4[:, 1024:2048].rearrange("p (t c) -> p t c", t=2)
        y_tok = late4[:, 2048:4096].rearrange("p (t c) -> p t c", t=TT)
        attn = late2[:, 1024:1024 + 2 * 384].rearrange("p (r c) -> p r c", r=2)
        qk_rot = late3[:, 2048:3072].rearrange("p (t c) -> p t c", t=2)

        bank = ctx.enter_context(nc.psum_tensor("bank", [P, 8, 512], F32))
        A0, S0, OB, XB = 0, 2, 6, 7
        xbank_b = bank[:, XB, :].bitcast(BF16)

        names = """x_loaded index_loaded w_loaded late_loaded const_ready ident_ready dve_pre xn_ready
            xnT_ready xnT_evac q_ready q_evac q_cut k_half seen_ready seen_summed hidden_ready
            hidden_summed clear_ready list_ready masks_loaded kv_ready k_evac v_evac k_cut k_written
            hideq_ready hidek_ready max_ready max_read max_cut dve_loop pool_cut diff_ready alpha_ready
            x_ready mrows_ready mrows_written mrows_loaded score_ready prob_ready prob_used outT_ready
            scaled combined at_ready at_half o_ready x1_taken n2_ready n3_ready turned turn_taken
            proj_ready v_taken tanh_ready rope_read rope_ready gated_ready att_ready att_done ret_ready
            sq_ready y_ready side_ready side_taken neg_max exp_ready w_ready pair_ready pair_read
            dve_post out_written settled""".split()
        s = {n: sem(n) for n in names}
        k_stacked = [sem(f"k_stacked{b}") for b in range(NB)]
        mask_loaded = [sem(f"mask_loaded{t}") for t in range(QT)]
        k_half_written = [sem(f"k_half_written{f}") for f in range(KIN)]
        q_half_written = [sem(f"q_half_written{f}") for f in range(KIN)]
        half_stacked = [sem(f"half_stacked{f}") for f in range(KIN)]
        ctx_loaded = [sem(f"ctx_loaded{b}") for b in range(NB)]
        K_READS = 16 * len(K_RUNS)
        evacuated = {"max": (s["max_read"], A_PER), "k": (s["k_evac"], KE_PER), "v": (s["v_evac"], VE_PER)}

        kscr, qscr, mscr = a["kscr"], a["qscr"], a["mscr"]
        block = ctx.enter_context(nc.Block())

        def settle(eng):
            eng.sem_inc(s["settled"], 1)

        @contextmanager
        def each_chunk(eng, count):
            with eng.Fori(0, 2) as fours:
                with eng.If(fours * 4 < count):
                    with eng.Fori(0, 2) as twos:
                        with eng.If(fours * 4 + twos * 2 < count):
                            with eng.Fori(0, 2) as ones_:
                                with eng.If(fours * 4 + twos * 2 + ones_ < count):
                                    yield fours * 4 + twos * 2 + ones_

        @block.sync
        def _(sp):
            for t in range(QT):
                sp.dma_start(mask_all[:, t, :], a["mask"][t * P:(t + 1) * P, :]).then_inc(mask_loaded[t], 16)
            sp.dma_start(index[:, :], a["index"]).then_inc(s["index_loaded"], 16)

            def load_ctx(c, b):
                sp.dma_start(ctxT[:, b, :, :], a["ctxT"][b, :, bass.ds(c * CH, CH)].rearrange("(f p) k -> p f k", p=P)
                             ).then_inc(ctx_loaded[b], 16)

            def load_masks(c):
                sp.dma_start(mask_q[:, :, :], a["mask"][:, bass.ds(c * CH, CH)].rearrange("(t p) k -> p t k", p=P)
                             ).then_inc(s["masks_loaded"], 16)
                sp.dma_start(mask_k[:, :, :], a["maskT"][bass.ds(c * CH, CH), :].rearrange("(t p) q -> p t q", p=P)
                             ).then_inc(s["masks_loaded"], 16)

            def write_k(b):
                sp.dma_start(kscr[b].rearrange("f c r k -> r (f c) k"), kpart[:, b, :, :, :].rearrange("p f c k -> p (f c) k")
                             ).then_inc(s["k_written"], 16)

            def read_k(b):
                for i, parts in K_RUNS:
                    sp.dma_start(kstack[DK * i:DK * (i + parts), b, :, :].rearrange("r (f h) k -> r f (h k)", f=KIN),
                                 kscr[b, :, 0:parts].rearrange("f c (d h) k -> (c d) f (h k)", h=HF)).then_inc(k_stacked[b], 16)

            def turn_maximum(nth, st, before):
                b, g = divmod(st, NG)
                if before is not None:
                    sp.wait_ge(s["mrows_loaded"], before)
                    settle(sp)
                sp.wait_ge(s["mrows_ready"], nth)
                sp.dma_start(mscr[st], mrows[:, st % 2, :]).then_inc(s["mrows_written"], 16)
                sp.wait_ge(s["mrows_written"], nth * 16)
                sp.dma_start(qstack[MROW:KROWS, G * g:G * g + G, b, :],
                             mscr[st].rearrange("(c h) q -> c h q", c=3)).then_inc(s["mrows_loaded"], 16)

            sp.wait_ge(s["list_ready"], 2)
            more_chunks = sp.value_load(n_more[0:1, 0:1], min_val=0, max_val=NCH - 1)
            first = sp.value_load(chunk_list[0:1, 0:1], min_val=0, max_val=NCH - 1)
            for b in range(NB):
                load_ctx(first, b)
            load_masks(first)
            sp.dma_start(w_ret[:, :, :], a["w_ret"].rearrange("(c p) n -> p c n", p=P)).then_inc(s["late_loaded"], 16)
            sp.dma_start(w_exp[:, 0, :, :], a["w_exp"][:, 0:P, :].rearrange("e p n -> p e n")).then_inc(s["late_loaded"], 16)
            for f in range(KIN):
                sp.wait_ge(s["k_half"], f + 1)
                sp.dma_start(kscr[0, f].rearrange("c r k -> r c k"), kpart[:, 0, f, :, :]).then_inc(k_half_written[f], 16)
            for f in range(KIN):
                sp.wait_ge(s["q_cut"], f + 1)
                sp.dma_start(qscr[f].rearrange("c r t -> r c t"), qpart[:, f, :, :]).then_inc(q_half_written[f], 16)
                sp.wait_ge(k_half_written[f], 16)
                for i, parts in K_RUNS:
                    sp.dma_start(kstack[DK * i:DK * (i + parts), 0, f * HF:(f + 1) * HF, :].rearrange("r h k -> r (h k)"),
                                 kscr[0, f, 0:parts].rearrange("c (d h) k -> (c d) (h k)", h=HF)).then_inc(half_stacked[f], 16)
                sp.wait_ge(q_half_written[f], 16)
                for i, c in enumerate(Q_PART):
                    sp.dma_start(qstack[DK * i:DK * (i + 1), f * HF:(f + 1) * HF, :, :].rearrange("r h b q -> r (h b q)"),
                                 qscr[f, c].rearrange("(d h) t -> d (h t)", h=HF)).then_inc(half_stacked[f], 16)
            for f in range(KIN):
                sp.wait_ge(half_stacked[f], 16 * (len(K_RUNS) + NPROD))
            sp.sem_inc(k_stacked[0], K_READS)
            sp.sem_inc(s["k_written"], 16)
            sp.wait_ge(s["k_cut"], 1)
            write_k(1)
            turn_maximum(1, 0, None)
            for w, nm in ((w_reto, "w_reto"), (w_gate, "w_gate")):
                sp.dma_start(w[:, :, :], a[nm].rearrange("(c p) n -> p c n", p=P)).then_inc(s["late_loaded"], 16)
            sp.dma_start(w_exp[:, 1, :, :], a["w_exp"][:, P:2 * P, :].rearrange("e p n -> p e n")).then_inc(s["late_loaded"], 16)
            sp.dma_start(b_exp[:, :], a["b_exp"]).then_inc(s["late_loaded"], 16)
            sp.dma_start(rope[:, :, :, :], a["rope"]).then_inc(s["late_loaded"], 16)
            sp.dma_start(decay[:, :, :], a["decay"]).then_inc(s["late_loaded"], 16)
            sp.dma_start(gn[:, :], a["gn"].rearrange("(p a) -> p a", a=1)).then_inc(s["late_loaded"], 16)
            sp.dma_start(gb_row[:, :], a["gb"].rearrange("(a n) -> a n", a=1).to_broadcast([P, NE])).then_inc(s["late_loaded"], 16)
            def chunk(it, more):
                if more:
                    nxt = sp.value_load(chunk_list[0:1, bass.ds(it + 1, 1)], min_val=0, max_val=NCH - 1)
                for t in range(STAGES):
                    if t < STAGES - 1:
                        turn_maximum(it * STAGES + t + 2, t + 1, (it * STAGES + t + 1) * 16)
                    if t == 0:
                        sp.wait_ge(s["k_written"], it * 32 + 32)
                        settle(sp)
                        sp.wait_ge(s["score_ready"], it * U_PER + 1)
                        read_k(1)
                        if more:
                            sp.wait_ge(ctx_loaded[0], it * 16 + 16)
                            load_ctx(nxt, 0)
                    if t == 3 and more:
                        sp.wait_ge(s["k_cut"], it * 2 + 2)
                        settle(sp)
                        sp.wait_ge(k_stacked[0], (it + 1) * K_READS)
                        write_k(0)
                    if t == 4 and more:
                        sp.wait_ge(s["k_written"], it * 32 + 48)
                        settle(sp)
                        sp.wait_ge(s["score_ready"], it * U_PER + U_PER // NB + 1)
                        read_k(0)
                    if t == 6 and more:
                        sp.wait_ge(s["k_cut"], it * 2 + 3)
                        settle(sp)
                        sp.wait_ge(k_stacked[1], (it + 1) * K_READS)
                        write_k(1)
                    if t == 1 and more:
                        sp.wait_ge(s["kv_ready"], it * KV_PER + KV_FIRST + 2)
                        settle(sp)
                        sp.wait_ge(ctx_loaded[1], it * 16 + 16)
                        load_ctx(nxt, 1)
                        sp.wait_ge(s["hideq_ready"], it + 1)
                        settle(sp)
                        sp.wait_ge(s["hidek_ready"], it * KT + KT)
                        settle(sp)
                        sp.wait_ge(s["masks_loaded"], it * 32 + 32)
                        load_masks(nxt)
                if more:
                    turn_maximum(it * STAGES + STAGES + 1, 0, (it + 1) * STAGES * 16)
                    sp.wait_ge(s["k_written"], it * 32 + 64)
                    settle(sp)
                    sp.wait_ge(s["mrows_loaded"], (it + 1) * STAGES * 16 + 16)
                    settle(sp)

            with each_chunk(sp, more_chunks) as it:
                chunk(it, True)
            chunk(more_chunks, False)


            for t in range(TT):
                sp.wait_ge(s["pair_read"], NE * (t + 1))
                sp.dma_start(a["out"][t * P:(t + 1) * P, :], x_in[:, t, :]).then_inc(s["out_written"], 16)
            sp.wait_ge(s["out_written"], 16 * TT)

        @block.gpsimd
        def _(pool):
            constants = ((ones[:, :], 1.0), (vals[:, :, :, :, :], 0.0), (vals[:, :, :, :, DK:DK + 1], 1.0),
                         (kstack[MROW:KROWS, :, :, :], 1.0), (mrun[:, :, :], MAX_FLOOR), (acc[:, :, :, :], 0.0))
            for i, (where, value) in enumerate(constants):
                if i:
                    pool.wait_ge(s["const_ready"], i)
                pool.memset(where, value).then_inc(s["const_ready"], 1)
            pool.wait_ge(s["const_ready"], len(constants))

            def split_k(b, nth):
                rest = pool.tensor_tensor(k_rest[:, :, :], k32[:, b, :, :], kpart[:, b, :, 0, :], ALU.subtract)
                rest.then_inc(s["pool_cut"], 1)
                pool.wait_ge(s["pool_cut"], nth * 2 - 1)
                pool.tensor_tensor(kpart[:, b, :, 1, :], k32[:, b, :, :], kpart[:, b, :, 0, :], ALU.subtract).then_inc(s["pool_cut"], 1)
                pool.wait_ge(s["pool_cut"], nth * 2)
                pool.tensor_tensor(kpart[:, b, :, 2, :], k_rest[:, :, :], kpart[:, b, :, 1, :], ALU.subtract).then_inc(s["k_cut"], 1)

            pool.wait_ge(s["k_evac"], 8)
            pool.wait_ge(s["k_half"], KIN)
            split_k(1, 1)
            pool.wait_ge(s["list_ready"], 2)
            more_chunks = pool.value_load(n_more[0:1, 0:1], min_val=0, max_val=NCH - 1)
            def scale(it, st):
                pool.wait_ge(s["alpha_ready"], it * STAGES + st + 1)
                settle(pool)
                pool.tensor_tensor(acc[:, st, :, :], acc[:, st, :, :],
                                   alpha[:, st % 4, :].unsqueeze(2).to_broadcast([P, QT * G, DK + 1]), ALU.mult).then_inc(s["scaled"], 1)

            def chunk(it, more):
                pool.wait_ge(s["combined"], it * STAGES + 1)
                for st in range(STAGES):
                    scale(it, st)
                    if st in (2, 5) and more:
                        b = st // 3
                        pool.wait_ge(s["k_evac"], it * KE_PER + KE_FIRST + 4 * (b + 1))
                        pool.wait_ge(s["k_cut"], it * NB + 1 + b)
                        settle(pool)
                        split_k(b, it * NB + b + 2)
                settle(pool)

            with each_chunk(pool, more_chunks) as it:
                chunk(it, True)
            chunk(more_chunks, False)

        def first_bank(i):
            return A0 + i % 6

        @block.tensor
        def _(pe):
            pe.sem_inc(s["prob_used"], CREDIT)
            pe.sem_inc(s["score_ready"], 1)
            pe.wait_ge(s["const_ready"], 1)
            pe.wait_ge(s["seen_ready"], 1)
            for t in range(QT):
                mm = pe.matmul(bank[0:1, XB, 0:NCH], ones[:, :], seen[:, t, :], start=(t == 0), stop=(t == QT - 1))
            mm.then_inc(s["seen_summed"], 1)

            def project(kind, b, half, bk_):
                if kind == "k":
                    for c in range(KIN):
                        mm = pe.matmul(bank[:, bk_, :], wk[:, c, half * P:(half + 1) * P], ctxT[:, b, c, :],
                                       start=(c == 0), stop=(c == KIN - 1))
                else:
                    for kt in (2 * half, 2 * half + 1):
                        for c in range(KIN):
                            mm = pe.matmul(bank[:, bk_, (kt % 2) * D:(kt % 2 + 1) * D],
                                           ctxT[:, b, c, kt * P:(kt + 1) * P], wv[:, c, :],
                                           start=(c == 0), stop=(c == KIN - 1))
                mm.then_inc(s["kv_ready"], 1)

            def max_tile(st, i, bk_):
                b, g = divmod(st, NG)
                qt, j = divmod(i, G)
                pe.matmul(bank[:, bk_, :], qstack[0:MROW, G * g + j, b, qt * P:(qt + 1) * P],
                          kstack[0:MROW, b, G * g + j, :], start=True, stop=True).then_inc(s["max_ready"], 1)

            def turn_maximum(st):
                for qt in range(QT):
                    mm = pe.transpose(xbank_b[0:3 * G, qt * P:(qt + 1) * P],
                                      mpart[:, st % 2, qt, :, :].rearrange("p c h -> p (c h)"), identb[:, :])
                mm.then_inc(s["x_ready"], 1)

            pe.wait_ge(s["ident_ready"], 16 + 1)
            for _ in range(WARM_UP):
                pe.matmul(bank[:, OB, 0:P], ident[:, :], ident[:, :], start=True, stop=True)
            for t in range(TT):
                pe.wait_ge(s["xn_ready"], t + 1)
                for f in range(KIN):
                    mm = pe.transpose(bank[:, S0 + f, t * P:(t + 1) * P], xn[:, t, f * P:(f + 1) * P], ident[:, :])
            mm.then_inc(s["xnT_ready"], 1)
            pe.wait_ge(s["w_loaded"], 8 * 16)
            for n_, (kind, b, half) in enumerate(FIRST_PIECES):
                pe.wait_ge(ctx_loaded[b], 16)
                if n_ == 2:
                    pe.wait_ge(s["hidden_ready"], 1)
                    for t in range(QT):
                        mm = pe.matmul(bank[0:1, XB, 0:NCH], ones[:, :], hidden[:, t, :], start=(t == 0), stop=(t == QT - 1))
                    mm.then_inc(s["hidden_summed"], 1)
                    pe.wait_ge(s["xnT_evac"], 2)
                    for f in range(KIN):
                        for c in range(KIN):
                            mm = pe.matmul(bank[:, S0 + 2 + f, :], wq[:, c, f * P:(f + 1) * P], xnT[:, c, :], start=(c == 0), stop=(c == KIN - 1))
                        mm.then_inc(s["q_ready"], 1)
                if n_ >= 2:
                    pe.wait_ge(s["k_evac"], 2 * (n_ - 1))
                project(kind, b, half, A0 + n_ % 2)
            pe.wait_ge(half_stacked[0], 16 * (len(K_RUNS) + NPROD))
            for i in range(A_FIRST):
                if i < 2:
                    pe.wait_ge(s["v_evac"], i + 1)
                elif i < 6:
                    pe.wait_ge(s["q_evac"], 2 * KIN + 1)
                else:
                    pe.wait_ge(s["max_read"], i + 1 - 6)
                max_tile(i // TILES, i % TILES, first_bank(i))
                if i == TILES + 5:
                    pe.wait_ge(s["clear_ready"], 1)
                    pe.wait_ge(s["max_cut"], 1)
                    turn_maximum(0)
            pe.wait_ge(s["const_ready"], 6)
            pe.wait_ge(k_stacked[0], K_READS)
            more_chunks = pe.value_load(n_more[0:1, 0:1], min_val=0, max_val=NCH - 1)

            def score_pair(it, st, kt, jj, masked):
                b, g = divmod(st, NG)
                u = st * KT + kt
                if jj == 0:
                    pe.wait_ge(s["prob_ready"], it * U_PER + u - 1 + CREDIT)
                out = bank[:, S0 + 2 * (u % 2) + jj, :]
                for hh in range(2):
                    h = G * g + 2 * jj + hh
                    mm = pe.matmul(out[:, hh * NQ:(hh + 1) * NQ], kstack[0:KROWS, b, h, kt * P:(kt + 1) * P],
                                   qstack[0:KROWS, h, b, :], start=(hh == 0 or not masked), stop=not masked, skip_group_check=True)
                if masked:
                    mm = pe.matmul(out, identb[:, :], hide_k[:, kt, :].unsqueeze(1).to_broadcast([P, 2, NQ]),
                                   start=False, stop=True, skip_group_check=True)
                if jj == 1:
                    mm.then_inc(s["score_ready"], 1)

            def value_unit(it, u):
                st, kt = divmod(u, KT)
                b, g = divmod(st, NG)
                if kt == 0:
                    pe.wait_ge(s["outT_ready"], it * STAGES + st + 1)
                pe.wait_ge(s["prob_ready"], it * U_PER + u + 1 + CREDIT)
                for j in range(G):
                    mm = pe.matmul(bank[32 * j:32 * j + PADV, OB, 0:NQ], vals[:, b, kt, G * g + j, :],
                                   prob[:, u % 3, j * NQ:(j + 1) * NQ], start=(kt == 0), stop=(kt == KT - 1),
                                   tile_position=(0, 32 * j), skip_group_check=True)
                mm.then_inc(s["prob_used"], 1)

            def turn_outputs(it, st):
                pe.wait_ge(s["outT_ready"], it * STAGES + st + 2)
                for qt in range(QT):
                    mm = pe.transpose(bank[:, XB, qt * P:(qt + 1) * P], outT[:, st % 2, qt * P:(qt + 1) * P], ident[:, :])
                mm.then_inc(s["x_ready"], 1)

            turns, sides = [], []

            def turn(kind, t, out, src, blocks, width=P):
                assert TURNS[len(turns)] == (kind, t)
                before = len(turns) - 1 if len(turns) < TWO_BANKS else len(turns)
                if before > 0:
                    pe.wait_ge(s["turn_taken"], before)
                for f in range(blocks):
                    mm = pe.transpose(out[:, f * P:(f + 1) * P], src[:, f * width:(f + 1) * width], ident[:, :])
                mm.then_inc(s["turned"], 1)
                turns.append((kind, t))

            def taken(kind, t):
                pe.wait_ge(s["turn_taken"], TURN_AT[kind, t] + 1)

            def side(kind, t):
                assert SIDES[len(sides)] == (kind, t)
                if sides:
                    pe.wait_ge(s["side_taken"], len(sides))
                sides.append((kind, t))
                return bank[:, SIDE, :]

            def attention_out(t):
                taken("at", t)
                for c in range(KIN):
                    mm = pe.matmul(bank[:, AT_BANKS[t], 0:D], xnT[:, c, t * P:(t + 1) * P], wo[:, c, :], start=(c == 0), stop=(c == KIN - 1))
                mm.then_inc(s["o_ready"], 1)

            def turn_at(t):
                pe.wait_ge(s["at_ready"], t + 1)
                turn("at", t, bank[:, turn_bank("at", t), :], at_tok[:, t, :], KIN)

            def turn_xn(kind, t):
                pe.wait_ge(s[kind + "_ready"], t + 1)
                turn(kind, t, bank[:, turn_bank(kind, t), :], xn[:, t, :], KIN)

            def steps(it, more, masked):
                for t in range(STAGES):
                    for k in range(KT):
                        if t == 2 and k == 0:
                            pe.wait_ge(k_stacked[1], (it + 1) * K_READS)
                        ahead = more or t + AHEAD < STAGES
                        if t == 6 and k == 0 and more:
                            pe.wait_ge(k_stacked[0], (it + 2) * K_READS)
                        def next_tile(i):
                            bk_, kind, count = RING[more]["max", t, i]
                            sem_, per = evacuated[kind]
                            pe.wait_ge(sem_, it * per + count)
                            max_tile((t + AHEAD) % STAGES, i, A0 + bk_)

                        if ahead:
                            next_tile(2 * k)
                        if k == 0:
                            pe.wait_ge(s["mrows_loaded"], (it * STAGES + t + 1) * 16)
                        if t == 0:
                            pe.wait_ge(s["hidek_ready"], it * KT + k + 1)
                        score_pair(it, t, k, 0, masked)
                        if ahead:
                            next_tile(2 * k + 1)
                        score_pair(it, t, k, 1, masked)
                        if (t, k) in PIECES and (more or t == 0):
                            kind_, b, half = PIECES[t, k]
                            if (t, k) == (2, 0):
                                pe.wait_ge(ctx_loaded[0], (it + 2) * 16)
                            if (t, k) == (5, 1):
                                pe.wait_ge(ctx_loaded[1], (it + 2) * 16)
                            bk_, kind, count = RING[more][kind_, t, k]
                            sem_, per = evacuated[kind]
                            pe.wait_ge(sem_, it * per + count)
                            project(kind_, b, half, A0 + bk_)
                        u = t * KT + k - 1
                        if u >= 0:
                            if k == 1 and t % NG == 0:
                                pe.wait_ge(s["v_evac"], it * VE_PER + VE_FIRST + 2 * (t // NG))
                            value_unit(it, u)
                        if k == 0 and (more or t + 1 < STAGES):
                            pe.wait_ge(s["max_cut"], it * STAGES + t + 2)
                            if t == 1:
                                pe.wait_ge(s["mrows_ready"], it * STAGES + 2)
                            else:
                                pe.wait_ge(s["combined"], it * STAGES + max(t - 1, 0) + 1)
                            turn_maximum((t + 1) % STAGES)
                        if k == 2 and t >= 1:
                            if more or t + 1 < STAGES:
                                pe.wait_ge(s["mrows_ready"], it * STAGES + t + 2)
                            else:
                                pe.wait_ge(s["combined"], it * STAGES + t)
                            turn_outputs(it, t - 1)
                        if not more and (t, k) == (6, 1):
                            turn_at(0)
                            turn_at(1)
                        if not more and (t, k) == (6, 3):
                            attention_out(0)
                            attention_out(1)
                value_unit(it, U_PER - 1)
                pe.wait_ge(s["combined"], it * STAGES + STAGES)
                turn_outputs(it, STAGES - 1)

            def chunk(it, more):
                no_hidden = pe.value_load(clear_list[0:1, bass.ds(it, 1)], min_val=0, max_val=1)
                with pe.If(no_hidden < 1):
                    steps(it, more, True)
                turns.clear()
                with pe.If(no_hidden > 0):
                    steps(it, more, False)

            with each_chunk(pe, more_chunks) as it:
                chunk(it, True)
            chunk(more_chunks, False)

            def project_ret(t, m):
                taken("n2", t)
                if t:
                    pe.wait_ge(s[("rope_read", "v_taken", "gated_ready")[m]], t)
                for c in range(KIN):
                    mm = pe.matmul(bank[:, 2 + m, :], xnT[:, c, t * P:(t + 1) * P], w_ret[:, c, m * 512:(m + 1) * 512],
                                   start=(c == 0), stop=(c == KIN - 1))
                mm.then_inc(s["proj_ready"], 1)

            def turn_qk(t):
                pe.wait_ge(s["rope_ready"], t + 1)
                turn("qk", t, bank[:, TB, :], qk_rot[:, t % 2, :], 4)

            pe.wait_ge(s["late_loaded"], 16 * 10)
            turn_xn("n2", 0)
            turn_xn("n2", 1)
            for t in range(TT - 1):
                project_ret(t, 0)
                if t == 0:
                    turn_at(2)
                    turn_at(3)
                if t:
                    turn_qk(t - 1)
                project_ret(t, 1)
                if t == 0:
                    attention_out(2)
                    attention_out(3)
                if t:
                    turn_xn("n2", t + 1)
                project_ret(t, 2)
            turn_qk(TT - 2)

            def ret_scores(r):
                b, h = divmod(r, RH)
                lo = RDK * (h % 2)
                taken("qk", 2 * b + 1)
                if r >= 2:
                    pe.wait_ge(s["att_done"], r - 1)
                else:
                    pe.wait_ge(s["x1_taken"], TT)
                out = bank[:, 5 + r % 2, :]
                tk = b * NQ
                pe.matmul(out[:, 0:NQ], qkT[lo:lo + RDK, 2 + h // 2, tk:tk + P], qkT[lo:lo + RDK, h // 2, tk:tk + NQ],
                          start=True, stop=True)
                pe.matmul(out[:, NQ:NQ + P], qkT[lo:lo + RDK, 2 + h // 2, tk + P:tk + NQ],
                          qkT[lo:lo + RDK, h // 2, tk + P:tk + NQ], start=True, stop=True).then_inc(s["att_ready"], 1)

            def ret_values(r):
                b, h = divmod(r, RH)
                pe.wait_ge(s["v_taken"], TT if b else QT)
                if b:
                    pe.wait_ge(s["gated_ready"], TT)
                pe.wait_ge(s["att_done"], r + 1)
                cols = slice(h * RDV, (h + 1) * RDV)
                w = attn[:, r % 2, :]
                early, late_ = bank[:, RET_BANKS[2 * b], cols], bank[:, RET_BANKS[2 * b + 1], cols]
                pe.matmul(early, w[:, 0:P], v_tok[:, 2 * b, cols], start=True, stop=True)
                pe.matmul(late_, w[:, P:2 * P], v_tok[:, 2 * b, cols], start=True, stop=False)
                pe.matmul(late_, w[:, 2 * P:3 * P], v_tok[:, 2 * b + 1, cols],
                          start=False, stop=True).then_inc(s["ret_ready"], 1)

            ret_scores(0)
            for r in range(1, RH):
                ret_scores(r)
                ret_values(r - 1)
            ret_values(RH - 1)
            for m in range(3):
                project_ret(TT - 1, m)
            turn_qk(TT - 1)
            ret_scores(RH)

            def retention_out(t):
                taken("y", t)
                pe.wait_ge(s["rope_read"], TT)
                out = side("ro", t)
                for c in range(4):
                    mm = pe.matmul(out[:, 0:D], yT[:, c, t * P:(t + 1) * P], w_reto[:, c, :], start=(c == 0), stop=(c == 3))
                mm.then_inc(s["side_ready"], 1)

            def turn_y(t):
                pe.wait_ge(s["y_ready"], RH * (t + 1))
                turn("y", t, bank[:, TB, :], y_tok[:, t, :], 4)

            def logits(t):
                taken("n3", t)
                out = side("logit", t)
                for c in range(KIN):
                    mm = pe.matmul(out[:, 0:NE], xnT[:, c, t * P:(t + 1) * P], w_gate[:, c, :], start=(c == 0), stop=(c == KIN - 1))
                mm.then_inc(s["side_ready"], 1)

            def pair(t, pr):
                m = t * (NE // 2) + pr
                if m >= len(PAIR_BANKS):
                    pe.wait_ge(s["pair_read"], 2 * (m - len(PAIR_BANKS) + 1))
                for c in range(KIN):
                    mm = pe.matmul(bank[:, PAIR_BANKS[m % 4], :], xnT[:, c, t * P:(t + 1) * P],
                                   w_exp[:, c, 2 * pr:2 * pr + 2, :], start=(c == 0), stop=(c == KIN - 1))
                mm.then_inc(s["pair_ready"], 1)

            def turn_weights(t):
                pe.wait_ge(s["w_ready"], t // QT + 1)
                turn("w", t, bank[0:NE, TB, :], nwts[:, t, :], 1, NE)

            def biases(t):
                taken("w", t)
                out = side("bias", t)
                pe.matmul(out[:, 0:D], wT[:, t, :], b_exp[:, :], start=True, stop=True).then_inc(s["side_ready"], 1)

            turn_y(0)
            ret_scores(RH + 1)
            turn_y(1)
            retention_out(0)
            retention_out(1)
            ret_values(RH)
            for r in range(RH + 2, NB * RH):
                ret_scores(r)
                ret_values(r - 1)
            ret_values(NB * RH - 1)
            turn_xn("n3", 0)
            turn_xn("n3", 1)
            logits(0)
            pe.wait_ge(s["att_done"], NB * RH)
            pair(0, 0)
            logits(1)
            pair(0, 1)
            pair(0, 2)
            turn_weights(0)
            pair(0, 3)
            turn_y(2)
            biases(0)
            turn_y(3)
            retention_out(2)
            retention_out(3)
            turn_weights(1)
            pair(1, 0)
            biases(1)
            pair(1, 1)
            pair(1, 2)
            turn_xn("n3", 2)
            pair(1, 3)
            turn_xn("n3", 3)
            logits(2)
            pair(2, 0)
            logits(3)
            pair(2, 1)
            turn_weights(2)
            pair(2, 2)
            turn_weights(3)
            biases(2)
            pair(2, 3)
            pair(3, 0)
            biases(3)
            for pr in range(1, 4):
                pair(3, pr)

        @block.scalar
        def _(act):
            act.sem_inc(s["prob_ready"], CREDIT)
            act.sem_inc(s["outT_ready"], 1)
            for t in range(TT):
                act.dma_start(x_in[:, t, :], a["x"][t * P:(t + 1) * P, :]).then_inc(s["x_loaded"], 16)
            act.dma_start(ident[:, :], a["ident"]).then_inc(s["ident_ready"], 16)
            for w, nm in ((wk, "wk"), (wq, "wq"), (wv, "wv"), (wo, "wo")):
                act.dma_start(w[:, :, :], a[nm].rearrange("(c p) n -> p c n", p=P)).then_inc(s["w_loaded"], 16)
            for w, nm in ((bk, "bk"), (bq, "bq"), (bv, "bv")):
                act.dma_start(w[:, :], a[nm]).then_inc(s["w_loaded"], 16)
            act.dma_start(bo_row[:, :], a["bo"].rearrange("(a n) -> a n", a=1).to_broadcast([P, D])).then_inc(s["w_loaded"], 16)
            act.wait_ge(s["ident_ready"], 16)
            act.copy(identb[:, :], ident[:, :]).then_inc(s["ident_ready"], 1)
            act.wait_ge(s["w_loaded"], 8 * 16)
            act.mul(bq4[:, :], bq[:, :], DK ** -0.5).then_inc(s["q_evac"], 1)
            act.wait_ge(s["q_evac"], 1)

            def take(kind, b, half, bk_):
                if kind == "k":
                    act.activation(k32[:, b, half, :], bank[:, bk_, :], ACT.Identity, bias=bk[:, half:half + 1]).then_inc(s["k_evac"], 1)
                    act.activation(kpart[:, b, half, 0, :], bank[:, bk_, :], ACT.Identity, bias=bk[:, half:half + 1]).then_inc(s["k_evac"], 1)
                else:
                    act.copy(vals[:, b, 2 * half:2 * half + 2, :, 0:DK],
                             bank[:, bk_, :].rearrange("p (k h d) -> p k h d", k=2, h=NH)).then_inc(s["v_evac"], 1)

            act.wait_ge(s["xnT_ready"], 1)
            for f in range(KIN):
                act.copy(xnT[:, f, :], bank[:, S0 + f, :]).then_inc(s["xnT_evac"], 1)
            for n_, (kind, b, half) in enumerate(FIRST_PIECES):
                if n_ == 2:
                    for f in range(KIN):
                        act.wait_ge(s["q_ready"], f + 1)
                        act.activation(q32[:, f, :], bank[:, S0 + 2 + f, :], ACT.Identity, bias=bq4[:, f:f + 1], scale=DK ** -0.5).then_inc(s["q_evac"], 1)
                        act.activation(qpart[:, f, 0, :], bank[:, S0 + 2 + f, :], ACT.Identity, bias=bq4[:, f:f + 1], scale=DK ** -0.5).then_inc(s["q_evac"], 1)
                if n_ == 4:
                    act.wait_ge(s["const_ready"], 3)
                act.wait_ge(s["kv_ready"], n_ + 1)
                take(kind, b, half, A0 + n_ % 2)
            act.wait_ge(s["diff_ready"], 1)
            act.activation(alpha[:, 0, :], mdiff[:, 0, :], ACT.Exp).then_inc(s["alpha_ready"], 1)
            act.wait_ge(s["list_ready"], 2)
            more_chunks = act.value_load(n_more[0:1, 0:1], min_val=0, max_val=NCH - 1)

            def take_outputs(it, st):
                act.wait_ge(s["prob_used"], it * U_PER + (st + 1) * KT + CREDIT)
                act.copy(outT[:, st % 2, :], bank[:, OB, 0:NQ]).then_inc(s["outT_ready"], 1)

            takes = []

            def take_turn(kind, t, out, src, **how):
                assert TURNS[len(takes)] == (kind, t)
                act.wait_ge(s["turned"], len(takes) + 1)
                act.activation(out, src, ACT.Identity if "bias" in how else ACT.Copy, **how).then_inc(s["turn_taken"], 1)
                takes.append((kind, t))

            def take_xn(kind, t):
                take_turn(kind, t, xnT[:, :, t * P:(t + 1) * P], bank[:, turn_bank(kind, t), 0:D].rearrange("p (f q) -> p f q", f=KIN))

            def take_at(t):
                act.wait_ge(s["turned"], TURN_AT["at", t] + 1)
                act.activation(xnT[:, 0, t * P:(t + 1) * P], bank[:, turn_bank("at", t), 0:P], ACT.Identity, bias=bv[:, 0:1]).then_inc(s["at_half"], 1)
                take_turn("at", t, xnT[:, 1, t * P:(t + 1) * P], bank[:, turn_bank("at", t), P:2 * P], bias=bv[:, 1:2])

            def chunk(it, more):
                for t in range(STAGES):
                    for k in range(KT):
                        u = t * KT + k
                        act.wait_ge(s["score_ready"], it * U_PER + u + 2)
                        act.wait_ge(s["prob_used"], it * U_PER + u - 2 + CREDIT)
                        act.activation(prob[:, u % 3, :], bank[:, S0 + 2 * (u % 2):S0 + 2 * (u % 2) + 2, :].rearrange("p b n -> p (b n)"),
                                       ACT.Exp).then_inc(s["prob_ready"], 1)
                        if (t, k) in PIECES and (more or t == 0):
                            kind, b, half = PIECES[t, k]
                            act.wait_ge(s["kv_ready"], it * KV_PER + KV_FIRST + PIECE_AT[t, k] + 1)
                            take(kind, b, half, A0 + RING[more][kind, t, k][0])
                        if k == 0 and t >= 1:
                            take_outputs(it, t - 1)
                        if k == 0 and (more or t + 1 < STAGES):
                            act.wait_ge(s["x_ready"], it * X_PER + 1 + turned(t) + 1)
                            act.wait_ge(s["mrows_written"], (it * STAGES + t + 1) * 16)
                            act.copy(mrows[:, (t + 1) % 2, :], xbank_b[0:3 * G, 0:NQ]).then_inc(s["mrows_ready"], 1)
                        if k == 1 and (more or t + 1 < STAGES):
                            st = (t + 1) % STAGES
                            act.wait_ge(s["diff_ready"], it * STAGES + t + 2)
                            act.activation(alpha[:, st % 4, :], mdiff[:, st % 2, :], ACT.Exp).then_inc(s["alpha_ready"], 1)
                        if not more and (t, k) == (6, 2):
                            take_at(0)
                            take_at(1)
                take_outputs(it, STAGES - 1)

            with each_chunk(act, more_chunks) as it:
                chunk(it, True)
            chunk(more_chunks, False)

            def take_v(t):
                act.wait_ge(s["proj_ready"], 3 * t + 2)
                act.copy(v_tok[:, t, :], bank[:, 3, :]).then_inc(s["v_taken"], 1)

            def gate(t):
                act.wait_ge(s["proj_ready"], 3 * t + 3)
                if t >= 2:
                    act.wait_ge(s["gated_ready"], t - 1)
                act.activation(tanh_g[:, t % 2, :], bank[:, 4, :], ACT.Tanh, scale=0.5).then_inc(s["tanh_ready"], 1)

            def take_qk(t):
                take_turn("qk", t, qkT[:, :, t * P:(t + 1) * P], bank[:, TB, :].rearrange("p (f q) -> p f q", f=4))

            def squares_of(t):
                act.wait_ge(s["ret_ready"], RH * (t // QT + 1))
                if t >= 2:
                    act.wait_ge(s["sq_ready"], RH * (t - 1))
                for h in range(RH):
                    act.activation(squares[:, t % 2, h * RDV:(h + 1) * RDV], bank[:, RET_BANKS[t], h * RDV:(h + 1) * RDV],
                                   ACT.Square, accum_out=sumsq[:, t, h:h + 1]).then_inc(s["sq_ready"], 1)

            def take_y(t):
                take_turn("y", t, yT[:, :, t * P:(t + 1) * P], bank[:, TB, :].rearrange("p (f q) -> p f q", f=4), scale=gn[:, 0:1])

            def gate_exp(t):
                act.wait_ge(s["neg_max"], t // QT + 1)
                act.activation(gexp[:, t, :], glog[:, t, :], ACT.Exp, bias=gmax[:, t:t + 1], accum_out=gsum[:, t:t + 1]).then_inc(s["exp_ready"], 1)

            def take_weights(t):
                take_turn("w", t, wT[:, t, :], bank[0:NE, TB, 0:P])

            take_xn("n2", 0)
            take_xn("n2", 1)
            take_at(2)
            take_at(3)
            for t in range(TT - 1):
                if t:
                    take_qk(t - 1)
                take_v(t)
                if t:
                    take_xn("n2", t + 1)
                gate(t)
            take_qk(TT - 2)
            squares_of(0)
            squares_of(1)
            take_v(TT - 1)
            gate(TT - 1)
            take_qk(TT - 1)
            act.wait_ge(s["late_loaded"], 16 * 10)
            take_y(0)
            take_y(1)
            take_xn("n3", 0)
            take_xn("n3", 1)
            squares_of(2)
            squares_of(3)
            gate_exp(0)
            gate_exp(1)
            take_weights(0)
            take_y(2)
            take_y(3)
            take_weights(1)
            take_xn("n3", 2)
            take_xn("n3", 3)
            gate_exp(2)
            gate_exp(3)
            take_weights(2)
            take_weights(3)

        @block.vector
        def _(dve):
            count = {"dve_pre": 0, "dve_post": 0}

            def then(which, ins, wait=True):
                count[which] += 1
                ins.then_inc(s[which], 1)
                if wait:
                    dve.wait_ge(s[which], count[which])

            def rsqrt(which, arg, c1, c2, res, between=()):
                others = list(between)
                then(which, dve.tensor_scalar(res.bitcast(I32), arg.bitcast(I32), -0.5, RSQRT_MAGIC, ALU.mult, ALU.add))
                for _ in range(NEWTON):
                    then(which, dve.scalar_tensor_tensor(c1, res, -0.5, arg, ALU.mult, ALU.mult))
                    if others:
                        others.pop(0)()
                    then(which, dve.tensor_tensor(c2, c1, res, ALU.mult))
                    then(which, dve.scalar_tensor_tensor(res, c2, 1.5, res, ALU.add, ALU.mult))
                assert not others

            def layernorms(which, src, tiles, done, between=()):
                t0, m = tiles[0], len(tiles)
                for t in tiles:
                    then(which, dve.bn_stats(stats[:, t, :], src[:, t, :]), t == tiles[-1])
                for t in tiles:
                    then(which, dve.bn_aggr(moments[:, t, :], stats[:, t, :]), t == tiles[-1])
                then(which, dve.tensor_scalar(nw[:, 0, 0:m], moments[:, t0:t0 + m, 1], EPS, None, ALU.add))
                rsqrt(which, nw[:, 0, 0:m], nw[:, 1, 0:m], nw[:, 2, 0:m], nw[:, 3, 0:m], between)
                for t in tiles:
                    dve.tensor_scalar(xn[:, t, :], src[:, t, :], moments[:, t, 0:1], nw[:, 3, t - t0:t - t0 + 1],
                                      ALU.subtract, ALU.mult).then_inc(s[done], 1)
                dve.wait_ge(s[done], tiles[-1] + 1)

            dve.sem_inc(s["combined"], 1)
            then("dve_pre", dve.memset(tiny[:, :, :], 0.0), False)
            for t in range(QT):
                dve.wait_ge(mask_loaded[t], 16)
                then("dve_pre", dve.tensor_reduce(hid_end[:, t, :], mask_all[:, t, :].bitcast(U16).rearrange("p (c k) -> p c k", c=NCH), AXX, ALU.min), t == QT - 1)
            dve.wait_ge(s["index_loaded"], 16)
            dve.tensor_scalar(seen[:, :, :], hid_end[:, :, :], 256.5, None, ALU.is_lt).then_inc(s["seen_ready"], 1)
            dve.wait_ge(s["seen_summed"], 1)
            flag = tiny[:, 1, NCH:2 * NCH]
            then("dve_pre", dve.tensor_scalar(flag, bank[0:1, XB, 0:NCH], 0.5, None, ALU.is_gt))
            for i, sh in enumerate((1, 2, 4)):
                then("dve_pre", dve.tensor_tensor(tiny[:, 2 + i, NCH:2 * NCH], tiny[:, 1 + i, NCH:2 * NCH],
                                                  tiny[:, 1 + i, NCH - sh:2 * NCH - sh], ALU.add))
            rank = tiny[:, 4, NCH:2 * NCH]
            numbered = tiny[:, 5, 0:NCH]
            then("dve_pre", dve.tensor_tensor(numbered, flag, index[:, :], ALU.mult))
            for r in range(NCH):
                then("dve_pre", dve.scalar_tensor_tensor(rank_eq[:, r, :], rank, float(r + 1), numbered, ALU.is_equal, ALU.mult), r == NCH - 1)
            then("dve_pre", dve.tensor_reduce(tiny[:, 6, 0:NCH], rank_eq[:, :, :], AXX, ALU.add))
            dve.tensor_copy(chunk_list[:, :], tiny[:, 6, 0:NCH + 1]).then_inc(s["list_ready"], 1)
            dve.tensor_scalar(n_more[:, :], rank[:, NCH - 1:NCH], 1.0, 1.0, ALU.max, ALU.subtract).then_inc(s["list_ready"], 1)
            dve.wait_ge(s["x_loaded"], 16 * TT)
            layernorms("dve_pre", x_in, range(TT), "xn_ready")

            def take_maximum(st, i, bk_):
                dve.tensor_tensor_reduce(junk[:, i % 2, :], bank[:, bk_, :], hide_q[:, i // G, :],
                                         1.0, -3e38, ALU.add, ALU.max, cmax[:, st % 2, i:i + 1]).then_inc(s["max_read"], 1)

            def new_maximum(st, nth, link, between=None):
                mp, mv = mpart[:, st % 2, :, :, :], mnew[:, :].rearrange("p (t h) -> p t h", t=QT)
                link(dve.tensor_tensor(mnew[:, :], mrun[:, st, :], cmax[:, st % 2, :], ALU.max))
                dve.tensor_tensor(mdiff[:, st % 2, :], mrun[:, st, :], mnew[:, :], ALU.subtract).then_inc(s["diff_ready"], 1)
                link(dve.tensor_scalar(mp[:, :, 0, :], mv, -1.0, None, ALU.mult))
                if between:
                    between()
                dve.wait_ge(s["diff_ready"], nth)
                link(dve.tensor_copy(mrun[:, st, :], mnew[:, :]), wait=False)
                link(dve.scalar_tensor_tensor(mrest[:, :, :], mv, -1.0, mp[:, :, 0, :], ALU.mult, ALU.subtract), wait=False)
                link(dve.scalar_tensor_tensor(mp[:, :, 1, :], mv, -1.0, mp[:, :, 0, :], ALU.mult, ALU.subtract))
                dve.tensor_tensor(mp[:, :, 2, :], mrest[:, :, :], mp[:, :, 1, :], ALU.subtract).then_inc(s["max_cut"], 1)

            def pre(ins, wait=True):
                then("dve_pre", ins, wait)

            def cut_half(rest, whole, parts, done):
                pre(dve.tensor_tensor(rest, whole, parts(0), ALU.subtract))
                pre(dve.tensor_copy(parts(1), rest))
                dve.tensor_tensor(parts(2), rest, parts(1), ALU.subtract).then_inc(done, 1)

            for t in range(QT):
                pre(dve.tensor_reduce(hid_end[:, t, :], mask_all[:, t, :].bitcast(U16).rearrange("p (c k) -> p c k", c=NCH), AXX, ALU.max), t == QT - 1)
            dve.tensor_scalar(hidden[:, :, :], hid_end[:, :, :], 0.5, None, ALU.is_gt).then_inc(s["hidden_ready"], 1)
            dve.wait_ge(s["masks_loaded"], 32)
            dve.tensor_scalar(hide_q[:, :, :], mask_q[:, :, :], HIDDEN, None, ALU.mult).then_inc(s["hideq_ready"], 1)
            for f in range(KIN):
                dve.wait_ge(s["k_evac"], 2 * f + 2)
                cut_half(k_rest[:, f, :], k32[:, 0, f, :], lambda c: kpart[:, 0, f, c, :], s["k_half"])
            for f in range(KIN):
                dve.wait_ge(s["q_evac"], 2 * f + 3)
                cut_half(q_rest[:, f, :], q32[:, f, :], lambda c: qpart[:, f, c, :], s["q_cut"])
            for kt in range(KT):
                dve.tensor_scalar(hide_k[:, kt, :], mask_k[:, kt, :], HIDDEN, None, ALU.mult).then_inc(s["hidek_ready"], 1)
            dve.wait_ge(s["hidden_summed"], 1)
            pre(dve.tensor_scalar(clear[:, 0, :], bank[0:1, XB, 0:NCH], 0.5, None, ALU.is_lt))
            pre(dve.tensor_tensor(clear[:, 1, :], clear[:, 0, :], flag, ALU.mult))
            for r in range(NCH):
                pre(dve.scalar_tensor_tensor(rank_eq[:, r, :], rank, float(r + 1), clear[:, 1, :], ALU.is_equal, ALU.mult), r == NCH - 1)
            pre(dve.tensor_reduce(clear[:, 0, :], rank_eq[:, :, :], AXX, ALU.add))
            dve.tensor_copy(clear_list[:, :], clear[:, 0, :]).then_inc(s["clear_ready"], 1)
            dve.wait_ge(s["w_loaded"], 8 * 16)
            pre(dve.tensor_tensor(xbo[:, :, :], x_in[:, :, :], bo_row[:, :].unsqueeze(1).to_broadcast([P, TT, D]), ALU.add))
            dve.wait_ge(s["const_ready"], 6)
            dve.wait_ge(s["hideq_ready"], 1)

            def first_tile(i):
                dve.wait_ge(s["max_ready"], i + 1)
                if i >= 2:
                    dve.wait_ge(s["max_read"], i - 1)
                take_maximum(i // TILES, i % TILES, first_bank(i))

            for i in range(TILES):
                first_tile(i)
            dve.wait_ge(s["max_read"], TILES)
            new_maximum(0, 1, pre, lambda: first_tile(TILES))
            first_tile(TILES + 1)
            dve.wait_ge(s["x_ready"], 1)
            dve.tensor_copy(mrows[:, 0, :], xbank_b[0:3 * G, 0:NQ]).then_inc(s["mrows_ready"], 1)
            for i in range(TILES + 2, A_FIRST):
                first_tile(i)
            dve.wait_ge(s["max_read"], A_FIRST)
            new_maximum(1, 2, pre)
            dve.wait_ge(s["list_ready"], 2)
            more_chunks = dve.value_load(n_more[0:1, 0:1], min_val=0, max_val=NCH - 1)

            def post(ins, wait=True):
                then("dve_post", ins, wait)

            def attention_tokens(b):
                groups = slice(b * NG, (b + 1) * NG)
                post(dve.reciprocal(rsum[:, groups, :], acc[:, groups, :, DK]))
                for qt in range(QT):
                    av = acc[:, groups, qt * G:(qt + 1) * G, 0:DK]
                    rv = rsum[:, groups, qt * G:(qt + 1) * G].unsqueeze(3).to_broadcast([P, NG, G, DK])
                    dve.tensor_tensor(at_tok[:, b * QT + qt, :].rearrange("p (g h d) -> p g h d", g=NG, h=G), av, rv, ALU.mult).then_inc(s["at_ready"], 1)

            def first_stream(b):
                for t in range(QT * b, QT * b + QT):
                    dve.wait_ge(s["o_ready"], t + 1)
                    dve.tensor_tensor(x1[:, t, :], bank[:, AT_BANKS[t], 0:D], xbo[:, t, :], ALU.add).then_inc(s["x1_taken"], 1)
                dve.wait_ge(s["x1_taken"], QT * (b + 1))

            def chunk(it, more):
                done = [0]

                def link(ins, wait=True):
                    done[0] += 1
                    ins.then_inc(s["dve_loop"], 1)
                    if wait:
                        dve.wait_ge(s["dve_loop"], it * DVE_PER + done[0])

                def combine(st):
                    dve.wait_ge(s["scaled"], it * STAGES + st + 1)
                    dve.wait_ge(s["x_ready"], it * X_PER + 1 + out_turned(st, more) + 1)
                    dve.tensor_tensor(acc[:, st, :, :], acc[:, st, :, :],
                                      bank[:, XB, 0:NQ].rearrange("p (i e) -> p i e", e=PADV)[:, :, 0:DK + 1], ALU.add).then_inc(s["combined"], 1)
                    dve.wait_ge(s["combined"], it * STAGES + st + 2)

                def hide_next(kt):
                    dve.wait_ge(s["score_ready"], it * U_PER + (STAGES - 1) * KT + kt + 2)
                    settle(dve)
                    dve.tensor_scalar(hide_k[:, kt, :], mask_k[:, kt, :], HIDDEN, None, ALU.mult).then_inc(s["hidek_ready"], 1)

                for t in range(STAGES):
                    ahead = more or t + AHEAD < STAGES
                    for k in range(KT):
                        for i in (2 * k, 2 * k + 1) if ahead else ():
                            n_ = A_FIRST + t * TILES + i
                            dve.wait_ge(s["max_ready"], it * A_PER + n_ + 1)
                            dve.wait_ge(s["max_read"], it * A_PER + n_ - 1)
                            settle(dve)
                            take_maximum((t + AHEAD) % STAGES, i, A0 + RING[more]["max", t, i][0])
                        if t == STAGES - 1 and k >= 1 and more:
                            hide_next(k - 1)
                        if not more and (t, k) == (6, 0):
                            attention_tokens(0)
                        if not more and (t, k) == (7, 0):
                            first_stream(0)
                            layernorms("dve_post", x1, range(QT), "n2_ready", [lambda: None, lambda: combine(STAGES - 2)])
                        elif k == 2 and t >= 1 and (more or t < STAGES - 1):
                            combine(t - 1)
                    if ahead:
                        dve.wait_ge(s["max_read"], it * A_PER + A_FIRST + (t + 1) * TILES)
                        dve.wait_ge(s["alpha_ready"], it * STAGES + t + 1)
                        new_maximum((t + AHEAD) % STAGES, it * STAGES + t + AHEAD + 1, link)
                    if t == STAGES - AHEAD - 1 and more:
                        dve.wait_ge(s["masks_loaded"], (it + 2) * 32)
                        dve.tensor_scalar(hide_q[:, :, :], mask_q[:, :, :], HIDDEN, None, ALU.mult).then_inc(s["hideq_ready"], 1)
                        dve.wait_ge(s["hideq_ready"], it + 2)
                if more:
                    hide_next(KT - 1)
                combine(STAGES - 1)
                settle(dve)
                assert done[0] == DVE_PER or not more, done[0]

            with each_chunk(dve, more_chunks) as it:
                chunk(it, True)
            chunk(more_chunks, False)

            attention_tokens(1)
            dve.wait_ge(s["late_loaded"], 16 * 10)
            HP = 2 * RH

            def rope_products(t):
                dve.wait_ge(s["proj_ready"], 3 * t + 1)
                qk = bank[:, 2, :].rearrange("p (h e) -> p h e", e=RDK // 2)
                co, si = (rope[:, i, t % 2, :].unsqueeze(1).to_broadcast([P, 2 * HP, RDK // 2]) for i in (0, 1))
                xc, xs = (ropes[:, i, :].rearrange("p (h e) -> p h e", e=RDK // 2) for i in (0, 1))
                post(dve.tensor_tensor(xc, qk, co, ALU.mult))
                dve.tensor_tensor(xs, qk, si, ALU.mult).then_inc(s["rope_read"], 1)
                dve.wait_ge(s["rope_read"], t + 1)

            c4, s4 = (ropes[:, i, :].rearrange("p (h two e) -> p h two e", two=2, e=RDK // 2) for i in (0, 1))

            def rotated(t):
                return qk_rot[:, t % 2, :].rearrange("p (h two e) -> p h two e", two=2, e=RDK // 2)

            def rope_first(t):
                if t >= 2:
                    dve.wait_ge(s["turned"], TURN_AT["qk", t - 2] + 1)
                post(dve.tensor_tensor(rotated(t)[:, :, 0, :], c4[:, :, 0, :], s4[:, :, 1, :], ALU.subtract), False)

            def rope_second(t):
                dve.tensor_tensor(rotated(t)[:, :, 1, :], c4[:, :, 1, :], s4[:, :, 0, :], ALU.add).then_inc(s["rope_ready"], 1)

            def gate_product(t):
                dve.wait_ge(s["tanh_ready"], t + 1)
                dve.scalar_tensor_tensor(gated[:, t, :], tanh_g[:, t % 2, :], 1.0, bank[:, 4, :], ALU.add, ALU.mult).then_inc(s["gated_ready"], 1)

            for t in range(TT - 1):
                rope_products(t)
                rope_first(t)
                rope_second(t)
                dve.wait_ge(s["rope_ready"], t + 1)
                if t == 0:
                    first_stream(1)
                gate_product(t)
                if t == 0:
                    layernorms("dve_post", x1, range(QT, TT), "n2_ready")

            def decay_weights(r):
                dve.wait_ge(s["att_ready"], r + 1)
                if r >= 2:
                    dve.wait_ge(s["ret_ready"], r - 1)
                dve.tensor_tensor(attn[:, r % 2, :], bank[:, 5 + r % 2, 0:3 * P], decay[:, r % RH, :], ALU.mult).then_inc(s["att_done"], 1)

            def norm_and_gate(b, between=()):
                tiles = range(QT * b, QT * b + QT)
                dve.wait_ge(s["sq_ready"], RH * (tiles[-1] + 1))
                sums = sumsq[:, QT * b:QT * (b + 1), :].rearrange("p t h -> p (t h)")
                post(dve.tensor_scalar(nw[:, 0, :], sums, 4.0 / RDV, 4.0 * EPS, ALU.mult, ALU.add))
                rsqrt("dve_post", nw[:, 0, :], nw[:, 1, :], nw[:, 2, :], nw[:, 3, :], between)
                dve.wait_ge(s["gated_ready"], tiles[-1] + 1)
                for t in tiles:
                    for h in range(RH):
                        cols = slice(h * RDV, (h + 1) * RDV)
                        i = (t % QT) * RH + h
                        dve.scalar_tensor_tensor(y_tok[:, t, cols], bank[:, RET_BANKS[t], cols], nw[:, 3, i:i + 1],
                                                 gated[:, t, cols], ALU.mult, ALU.mult).then_inc(s["y_ready"], 1)

            def second_stream(b, between=()):
                tiles = range(QT * b, QT * b + QT)
                for t in tiles:
                    n_ = SIDE_AT["ro", t] + 1
                    dve.wait_ge(s["side_ready"], n_)
                    dve.tensor_tensor(x2[:, t, :], bank[:, SIDE, 0:D], x1[:, t, :], ALU.add).then_inc(s["side_taken"], 1)
                dve.wait_ge(s["side_taken"], n_)
                dve.wait_ge(s["y_ready"], RH * QT * (b + 1))
                layernorms("dve_post", x2, tiles, "n3_ready", between)

            def gate_logits(b):
                tiles = range(QT * b, QT * b + QT)
                both = slice(QT * b, QT * b + QT)
                for t in tiles:
                    n_ = SIDE_AT["logit", t] + 1
                    dve.wait_ge(s["side_ready"], n_)
                    dve.tensor_tensor(glog[:, t, :], bank[:, SIDE, 0:NE], gb_row[:, :], ALU.add).then_inc(s["side_taken"], 1)
                dve.wait_ge(s["side_taken"], n_)
                dve.tensor_reduce(gmax[:, both], glog[:, both, :], AXX, ALU.max, negate=True).then_inc(s["neg_max"], 1)

            def gate_weights(b):
                both = slice(QT * b, QT * b + QT)

                def wide(i):
                    return gw1[:, i, :].unsqueeze(2).to_broadcast([P, QT, NE])

                dve.wait_ge(s["exp_ready"], QT * (b + 1))
                post(dve.reciprocal(gw1[:, 0, :], gsum[:, both]))
                post(dve.tensor_tensor(glog[:, both, :], gexp[:, both, :], wide(0), ALU.mult))
                post(dve.scalar_tensor_tensor(gexp[:, both, :], glog[:, both, :], 0.1, glog[:, both, :], ALU.is_ge, ALU.mult))
                post(dve.tensor_reduce(gw1[:, 1, :], gexp[:, both, :], AXX, ALU.add))
                post(dve.scalar_tensor_tensor(gw1[:, 2, :], gw1[:, 1, :], 0.0, gw1[:, 1, :], ALU.is_equal, ALU.add))
                post(dve.reciprocal(gw1[:, 3, :], gw1[:, 2, :]))
                dve.tensor_tensor(nwts[:, both, :], gexp[:, both, :], wide(3), ALU.mult).then_inc(s["w_ready"], 1)
                dve.wait_ge(s["w_ready"], b + 1)

            def add_experts(t, experts):
                for e in experts:
                    m = t * (NE // 2) + e // 2
                    dve.wait_ge(s["pair_ready"], m + 1)
                    src = bank[:, PAIR_BANKS[m % 4], (e % 2) * D:(e % 2 + 1) * D]
                    dve.scalar_tensor_tensor(x_in[:, t, :], src, nwts[:, t, e:e + 1], x_in[:, t, :], ALU.mult, ALU.add).then_inc(s["pair_read"], 1)
                    dve.wait_ge(s["pair_read"], t * NE + e + 1)

            def add_biases(t):
                n_ = SIDE_AT["bias", t] + 1
                dve.wait_ge(s["side_ready"], n_)
                dve.tensor_tensor(x_in[:, t, :], x2[:, t, :], bank[:, SIDE, 0:D], ALU.add).then_inc(s["side_taken"], 1)
                dve.wait_ge(s["side_taken"], n_)

            for r in range(RH):
                decay_weights(r)
            rope_products(TT - 1)
            norm_and_gate(0, [lambda: rope_first(TT - 1), lambda: rope_second(TT - 1)])
            dve.wait_ge(s["rope_ready"], TT)
            gate_product(TT - 1)
            decay_weights(RH)
            decay_weights(RH + 1)
            second_stream(0, [lambda: None, lambda: decay_weights(RH + 2), lambda: decay_weights(RH + 3)])
            gate_logits(0)
            gate_weights(0)
            norm_and_gate(1)
            add_biases(0)
            add_experts(0, range(0, 4))
            second_stream(1, [lambda e=e: add_experts(0, [e]) for e in (4, 5, 6)])
            add_experts(0, [NE - 1])
            add_biases(1)
            add_experts(1, range(0, 4))
            gate_logits(1)
            add_experts(1, range(4, 6))
            gate_weights(1)
            add_experts(1, range(6, NE))
            for t in (2, 3):
                add_biases(t)
                add_experts(t, range(NE))
    

def _shape_constants():
    half = RDK // 2
    inv = 1.0 / 10000.0 ** (np.arange(0, RDK, 2, dtype=np.float32) / np.float32(RDK))
    ang = (np.arange(NQ, dtype=np.float32)[:, None] * inv[None, :].astype(np.float32)).astype(np.float32)
    rope = np.stack([np.cos(ang), np.sin(ang)]).astype(np.float32)
    rope = np.ascontiguousarray(rope.reshape(2, QT, P, half).transpose(2, 0, 1, 3))
    gamma = 1.0 - 2.0 ** (-5.0 - np.arange(RH))
    j = np.arange(P)[:, None, None]
    i = np.concatenate([np.arange(NQ), np.arange(P)])[None, None, :]
    diff = i - j
    decay = np.where(diff >= 0, gamma[None, :, None] ** np.maximum(diff, 0), 0.0) * RDK ** -0.5
    return {"ident": np.eye(P, dtype=np.float32), "index": np.arange(NCH, dtype=np.float32)[None, :],
            "rope": rope, "decay": decay.astype(np.float32)}


def by_head(w):
    return w.reshape(KIN, HF, DK, *w.shape[1:]).swapaxes(1, 2).reshape(w.shape)


def kernel(**inputs):
    import concourse.bacc as bacc
    from concourse.bass_utils import run_bass_kernel_spmd as run

    g = {k: np.asarray(v) for k, v in inputs.items()}
    mask = np.ascontiguousarray(g["mask_1x1xSxS2_bk1"].reshape(NQ, NKEY))
    arrays = {
        "x": g["x"].reshape(NB * NQ, D),
        "ctxT": np.ascontiguousarray(g["ctx_1024"].transpose(0, 2, 1)),
        "mask": mask, "maskT": np.ascontiguousarray(mask.T),
        "wq": by_head(g["L0_xattn_w_q"]).T, "bq": by_head(g["L0_xattn_b_q"]).reshape(KIN, P).T,
        "wk": by_head(g["L0_xattn_w_k"]).T, "bk": by_head(g["L0_xattn_b_k"]).reshape(KIN, P).T,
        "wv": g["L0_xattn_w_v"].T, "bv": g["L0_xattn_b_v"].reshape(KIN, P).T, "wo": g["L0_xattn_w_o"].T, "bo": g["L0_xattn_b_o"],
        "w_ret": np.concatenate([g["L0_attn_W" + n].T for n in "qkvg"], axis=1),
        "w_reto": g["L0_attn_Wo"].T, "gn": g["L0_attn_gnorm_w"],
        "w_gate": g["L0_ffn_gate_w"], "gb": g["L0_ffn_gate_b"],
        "w_exp": g["L0_ffn_expert_w"], "b_exp": g["L0_ffn_expert_b"],
        **_shape_constants(),
    }
    arrays = {k: np.ascontiguousarray(v) for k, v in arrays.items()}
    nc = bacc.Bacc("TRN2", target_bir_lowering=False, num_devices=1)
    args = {k: nc.dram_tensor(f"in_{k}", v.shape, mybir.dt.from_np(v.dtype), kind="ExternalInput").ap() for k, v in arrays.items()}
    args["kscr"] = nc.dram_tensor("kscr", (NB, KIN, 3, P, CH), BF16, kind="Internal").ap()
    args["qscr"] = nc.dram_tensor("qscr", (KIN, 3, P, TT * P), BF16, kind="Internal").ap()
    args["mscr"] = nc.dram_tensor("mscr", (STAGES, 3 * G, NQ), BF16, kind="Internal").ap()
    args["out"] = nc.dram_tensor("out_x", (NB * NQ, D), F32, kind="ExternalOutput").ap()
    build(nc, args)
    r = run(nc, [{f"in_{k}": v for k, v in arrays.items()}], core_ids=[0])
    return r.results[0]["out_x"].reshape(NB, NQ, D)
```
